# Optimizing a Trainium2 kernel written in Bass

```python
import numpy as np
import jax
import jax.numpy as jnp

def _softmax(x, axis=-1):
    return jax.nn.softmax(x, axis=axis)

def _gelu(x):
    return jax.nn.gelu(x, approximate=True)

def _silu(x):
    return jax.nn.silu(x)

def _sigmoid(x):
    return jax.nn.sigmoid(x)

def _layernorm(x, axis=-1, eps=1e-05):
    m = jnp.mean(x, axis=axis, keepdims=True)
    v = jnp.var(x, axis=axis, keepdims=True)
    return (x - m) / jnp.sqrt(v + eps)

def _scatter_add(tgt, idx, src, axis=0):
    return tgt.at[idx].add(src)

def _segment_sum(src, seg, n):
    return jax.ops.segment_sum(src, seg, n)
kernel_name = 'mk_hybrid_d2_jaxref_r8_3f9104'

def setup_inputs(seed: int=0):
    np.random.seed(seed)
    _w = jnp.asarray

    def _L0_attn_a_setup():
        import jax, jax.numpy as jnp
        import numpy as np
        D_MODEL = 128
        N_HEADS = 16
        D_HEAD = 64
        B, S = (8, 128)
        EPS = 1.1920929e-07
        key = jax.random.key(seed)
        k1, k2, k3 = jax.random.split(key, 3)
        x = jax.random.normal(k1, (B, S, D_MODEL), dtype=jnp.float32)
        W_qkv = jax.random.normal(k2, (3 * N_HEADS * D_HEAD, D_MODEL), dtype=jnp.float32) * 0.02
        b_qkv = jnp.zeros((3 * N_HEADS * D_HEAD,), dtype=jnp.float32)
        W_o = jax.random.normal(k3, (D_MODEL, N_HEADS * D_HEAD), dtype=jnp.float32) * 0.02
        b_o = jnp.zeros((D_MODEL,), dtype=jnp.float32)
        return {'x': x, 'W_qkv': W_qkv, 'b_qkv': b_qkv, 'W_o': W_o, 'b_o': b_o}
    _L0_attn_a_in = _L0_attn_a_setup()

    def _L0_attn_b_setup():
        import jax, jax.numpy as jnp
        import numpy as np
        HEAD = 8
        BLOCK = 64
        D_MODEL = 128
        key = jax.random.key(seed)
        ks = jax.random.split(key, 9)
        d = D_MODEL
        s = 0.02
        return {'src': jax.random.normal(ks[0], (4, 512, d), dtype=jnp.float32), 'Wq': jax.random.normal(ks[1], (d, d), dtype=jnp.float32) * s, 'bq': jax.random.normal(ks[2], (d,), dtype=jnp.float32) * s, 'Wk': jax.random.normal(ks[3], (d, d), dtype=jnp.float32) * s, 'bk': jax.random.normal(ks[4], (d,), dtype=jnp.float32) * s, 'Wv': jax.random.normal(ks[5], (d, d), dtype=jnp.float32) * s, 'bv': jax.random.normal(ks[6], (d,), dtype=jnp.float32) * s, 'Wo': jax.random.normal(ks[7], (d, d), dtype=jnp.float32) * s, 'bo': jax.random.normal(ks[8], (d,), dtype=jnp.float32) * s}
    _L0_attn_b_in = _L0_attn_b_setup()

    def _L0_ffn_setup():
        import jax, jax.numpy as jnp
        import numpy as np
        D_MODEL = 128
        N_HEAD = 16
        HEAD_DIM = D_MODEL // N_HEAD
        D_FF = 512
        N_EXPERTS = 4
        EPS = 1e-05

        def _layer_norm(x, gamma, beta):
            mu = jnp.mean(x, axis=-1, keepdims=True)
            var = jnp.mean((x - mu) ** 2, axis=-1, keepdims=True)
            return (x - mu) / jnp.sqrt(var + EPS) * gamma + beta
        key = jax.random.key(seed)
        ks = jax.random.split(key, 20)
        f32 = jnp.float32
        sc = 1.0 / np.sqrt(D_MODEL)
        scf = 1.0 / np.sqrt(D_FF)
        return {'src': jax.random.normal(ks[0], (4, 64, D_MODEL), f32), 'Wq': jax.random.normal(ks[1], (D_MODEL, D_MODEL), f32) * sc, 'bq': jnp.zeros((D_MODEL,), f32), 'Wk': jax.random.normal(ks[2], (D_MODEL, D_MODEL), f32) * sc, 'bk': jnp.zeros((D_MODEL,), f32), 'Wv': jax.random.normal(ks[3], (D_MODEL, D_MODEL), f32) * sc, 'bv': jnp.zeros((D_MODEL,), f32), 'Wo': jax.random.normal(ks[4], (D_MODEL, D_MODEL), f32) * sc, 'bo': jnp.zeros((D_MODEL,), f32), 'router_w': jax.random.normal(ks[5], (D_MODEL, 1), f32) * 0.05, 'router_b': jnp.zeros((1,), f32), 'W1': jax.random.normal(ks[6], (N_EXPERTS, D_MODEL, D_FF), f32) * sc, 'b1': jnp.zeros((N_EXPERTS, D_FF), f32), 'W2': jax.random.normal(ks[7], (N_EXPERTS, D_FF, D_MODEL), f32) * scf, 'b2': jnp.zeros((N_EXPERTS, D_MODEL), f32), 'ln1_g': jnp.ones((D_MODEL,), f32), 'ln1_b': jnp.zeros((D_MODEL,), f32), 'ln2_g': jnp.ones((D_MODEL,), f32), 'ln2_b': jnp.zeros((D_MODEL,), f32)}
    _L0_ffn_in = _L0_ffn_setup()

    def _L1_attn_a_setup():
        import jax, jax.numpy as jnp
        import numpy as np
        B, CTX, DIMS, HEAD = (8, 512, 128, 16)
        HD = DIMS // HEAD
        EPS = 1e-05
        THRESH = 0.01
        FACTOR = 0.1
        MAX_IT = 3

        def _ln(x, w):
            m = jnp.mean(x, axis=-1, keepdims=True)
            v = jnp.mean((x - m) ** 2, axis=-1, keepdims=True)
            return (x - m) * jax.lax.rsqrt(v + EPS) * w
        key = jax.random.key(seed)
        ks = jax.random.split(key, 9)
        w = lambda k, shp: jax.random.normal(k, shp, jnp.float32) * 0.02
        return {'x': jax.random.normal(ks[0], (B, CTX, DIMS), jnp.float32), 'qw': w(ks[1], (DIMS, DIMS)), 'qb': jnp.zeros((DIMS,), jnp.float32), 'kw': w(ks[2], (DIMS, DIMS)), 'vw': w(ks[3], (DIMS, DIMS)), 'vb': jnp.zeros((DIMS,), jnp.float32), 'ow': w(ks[4], (DIMS, DIMS)), 'ob': jnp.zeros((DIMS,), jnp.float32), 'lna_w': jnp.ones((DIMS,), jnp.float32), 'lnb_w': jnp.ones((DIMS,), jnp.float32), 'lnc_w': jnp.ones((HD,), jnp.float32), 'lnd_w': jnp.ones((HD,), jnp.float32), 'lqw': w(ks[5], (HD, HD)), 'lqb': jnp.zeros((HD,), jnp.float32), 'lkw': w(ks[6], (HD, HD)), 'lkb': jnp.zeros((HD,), jnp.float32), 'lvw': w(ks[7], (HD, HD)), 'lvb': jnp.zeros((HD,), jnp.float32)}
    _L1_attn_a_in = _L1_attn_a_setup()

    def _L1_attn_b_setup():
        import jax, jax.numpy as jnp
        import numpy as np
        THETA = 10000.0

        def _rope_tables(seq_len, dk, dtype):
            pos = jnp.arange(seq_len, dtype=jnp.float32)[:, None]
            k = jnp.arange(dk // 2, dtype=jnp.float32)[None, :]
            angle = pos / THETA ** (2.0 * k / dk)
            return (jnp.sin(angle).astype(dtype), jnp.cos(angle).astype(dtype))

        def _apply_rope(t, sin, cos):
            even = t[..., 0::2]
            odd = t[..., 1::2]
            even_out = even * cos - odd * sin
            odd_out = even * sin + odd * cos
            out = jnp.stack([even_out, odd_out], axis=-1)
            return out.reshape(t.shape)
        key = jax.random.key(seed)
        ks = jax.random.split(key, 5)
        b, s, d = (2, 256, 128)
        std = np.sqrt(2.0 / (d + d))
        return {'x': jax.random.normal(ks[0], (b, s, d), dtype=jnp.float32), 'wq': jax.random.normal(ks[1], (d, d), dtype=jnp.float32) * std, 'wk': jax.random.normal(ks[2], (d, d), dtype=jnp.float32) * std, 'wv': jax.random.normal(ks[3], (d, d), dtype=jnp.float32) * std, 'wo': jax.random.normal(ks[4], (d, d), dtype=jnp.float32) * std}
    _L1_attn_b_in = _L1_attn_b_setup()

    def _L1_ffn_setup():
        import jax, jax.numpy as jnp
        import numpy as np
        B, T, D, E, H = (4, 256, 128, 4, 8)
        EPS = 1e-05

        def _uniform(k, shape, bound):
            return jax.random.uniform(k, shape, jnp.float32, -bound, bound)

        def _layernorm(x, w, b):
            mu = jnp.mean(x, axis=-1, keepdims=True)
            var = jnp.mean(jnp.square(x - mu), axis=-1, keepdims=True)
            return (x - mu) * jax.lax.rsqrt(var + EPS) * w + b
        key = jax.random.key(seed)
        ks = jax.random.split(key, 12)
        wb = np.sqrt(6.0 / D) / np.sqrt(6.0)
        wb = 1.0 / np.sqrt(D)
        return {'x': jax.random.normal(ks[0], (B, T, D), jnp.float32), 'router_prob': jax.random.uniform(ks[1], (B, T, E), jnp.float32), 'norm_w': jnp.ones((D,), jnp.float32), 'norm_b': jnp.zeros((D,), jnp.float32), 'q_w': _uniform(ks[2], (D, D), wb), 'q_b': _uniform(ks[3], (D,), wb), 'k_w': _uniform(ks[4], (D, D), wb), 'k_b': _uniform(ks[5], (D,), wb), 'v_w': _uniform(ks[6], (D, D), wb), 'v_b': _uniform(ks[7], (D,), wb), 'o_w': _uniform(ks[8], (D, D), wb), 'o_b': _uniform(ks[9], (D,), wb)}
    _L1_ffn_in = _L1_ffn_setup()
    _d = {'L0_attn_a_x': _L0_attn_a_in['x'], 'L0_attn_a_W_qkv': _L0_attn_a_in['W_qkv'], 'L0_attn_a_b_qkv': _L0_attn_a_in['b_qkv'], 'L0_attn_a_W_o': _L0_attn_a_in['W_o'], 'L0_attn_a_b_o': _L0_attn_a_in['b_o'], 'L0_attn_b_Wq': _L0_attn_b_in['Wq'], 'L0_attn_b_bq': _L0_attn_b_in['bq'], 'L0_attn_b_Wk': _L0_attn_b_in['Wk'], 'L0_attn_b_bk': _L0_attn_b_in['bk'], 'L0_attn_b_Wv': _L0_attn_b_in['Wv'], 'L0_attn_b_bv': _L0_attn_b_in['bv'], 'L0_attn_b_Wo': _L0_attn_b_in['Wo'], 'L0_attn_b_bo': _L0_attn_b_in['bo'], 'L0_ffn_Wq': _L0_ffn_in['Wq'], 'L0_ffn_bq': _L0_ffn_in['bq'], 'L0_ffn_Wk': _L0_ffn_in['Wk'], 'L0_ffn_bk': _L0_ffn_in['bk'], 'L0_ffn_Wv': _L0_ffn_in['Wv'], 'L0_ffn_bv': _L0_ffn_in['bv'], 'L0_ffn_Wo': _L0_ffn_in['Wo'], 'L0_ffn_bo': _L0_ffn_in['bo'], 'L0_ffn_router_w': _L0_ffn_in['router_w'], 'L0_ffn_router_b': _L0_ffn_in['router_b'], 'L0_ffn_W1': _L0_ffn_in['W1'], 'L0_ffn_b1': _L0_ffn_in['b1'], 'L0_ffn_W2': _L0_ffn_in['W2'], 'L0_ffn_b2': _L0_ffn_in['b2'], 'L0_ffn_ln1_g': _L0_ffn_in['ln1_g'], 'L0_ffn_ln1_b': _L0_ffn_in['ln1_b'], 'L0_ffn_ln2_g': _L0_ffn_in['ln2_g'], 'L0_ffn_ln2_b': _L0_ffn_in['ln2_b'], 'L1_attn_a_qw': _L1_attn_a_in['qw'], 'L1_attn_a_qb': _L1_attn_a_in['qb'], 'L1_attn_a_kw': _L1_attn_a_in['kw'], 'L1_attn_a_vw': _L1_attn_a_in['vw'], 'L1_attn_a_vb': _L1_attn_a_in['vb'], 'L1_attn_a_ow': _L1_attn_a_in['ow'], 'L1_attn_a_ob': _L1_attn_a_in['ob'], 'L1_attn_a_lna_w': _L1_attn_a_in['lna_w'], 'L1_attn_a_lnb_w': _L1_attn_a_in['lnb_w'], 'L1_attn_a_lnc_w': _L1_attn_a_in['lnc_w'], 'L1_attn_a_lnd_w': _L1_attn_a_in['lnd_w'], 'L1_attn_a_lqw': _L1_attn_a_in['lqw'], 'L1_attn_a_lqb': _L1_attn_a_in['lqb'], 'L1_attn_a_lkw': _L1_attn_a_in['lkw'], 'L1_attn_a_lkb': _L1_attn_a_in['lkb'], 'L1_attn_a_lvw': _L1_attn_a_in['lvw'], 'L1_attn_a_lvb': _L1_attn_a_in['lvb'], 'L1_attn_b_wq': _L1_attn_b_in['wq'], 'L1_attn_b_wk': _L1_attn_b_in['wk'], 'L1_attn_b_wv': _L1_attn_b_in['wv'], 'L1_attn_b_wo': _L1_attn_b_in['wo'], 'L1_ffn_router_prob': _L1_ffn_in['router_prob'], 'L1_ffn_norm_w': _L1_ffn_in['norm_w'], 'L1_ffn_norm_b': _L1_ffn_in['norm_b'], 'L1_ffn_q_w': _L1_ffn_in['q_w'], 'L1_ffn_q_b': _L1_ffn_in['q_b'], 'L1_ffn_k_w': _L1_ffn_in['k_w'], 'L1_ffn_k_b': _L1_ffn_in['k_b'], 'L1_ffn_v_w': _L1_ffn_in['v_w'], 'L1_ffn_v_b': _L1_ffn_in['v_b'], 'L1_ffn_o_w': _L1_ffn_in['o_w'], 'L1_ffn_o_b': _L1_ffn_in['o_b']}
    _x0 = _d['L0_attn_a_x']
    _d['L0_attn_a_x'] = jax.random.normal(jax.random.fold_in(jax.random.key(seed), 1), (4, 1024, 128), dtype=_x0.dtype)
    del _x0
    return _d

def reference(L0_attn_a_x, L0_attn_a_W_qkv, L0_attn_a_b_qkv, L0_attn_a_W_o, L0_attn_a_b_o, L0_attn_b_Wq, L0_attn_b_bq, L0_attn_b_Wk, L0_attn_b_bk, L0_attn_b_Wv, L0_attn_b_bv, L0_attn_b_Wo, L0_attn_b_bo, L0_ffn_Wq, L0_ffn_bq, L0_ffn_Wk, L0_ffn_bk, L0_ffn_Wv, L0_ffn_bv, L0_ffn_Wo, L0_ffn_bo, L0_ffn_router_w, L0_ffn_router_b, L0_ffn_W1, L0_ffn_b1, L0_ffn_W2, L0_ffn_b2, L0_ffn_ln1_g, L0_ffn_ln1_b, L0_ffn_ln2_g, L0_ffn_ln2_b, L1_attn_a_qw, L1_attn_a_qb, L1_attn_a_kw, L1_attn_a_vw, L1_attn_a_vb, L1_attn_a_ow, L1_attn_a_ob, L1_attn_a_lna_w, L1_attn_a_lnb_w, L1_attn_a_lnc_w, L1_attn_a_lnd_w, L1_attn_a_lqw, L1_attn_a_lqb, L1_attn_a_lkw, L1_attn_a_lkb, L1_attn_a_lvw, L1_attn_a_lvb, L1_attn_b_wq, L1_attn_b_wk, L1_attn_b_wv, L1_attn_b_wo, L1_ffn_router_prob, L1_ffn_norm_w, L1_ffn_norm_b, L1_ffn_q_w, L1_ffn_q_b, L1_ffn_k_w, L1_ffn_k_b, L1_ffn_v_w, L1_ffn_v_b, L1_ffn_o_w, L1_ffn_o_b):

    def _L0_attn_a_ref(x, W_qkv, b_qkv, W_o, b_o):
        import jax, jax.numpy as jnp
        import numpy as np
        D_MODEL = 128
        N_HEADS = 16
        D_HEAD = 64
        B, S = (8, 128)
        EPS = 1.1920929e-07
        normed = x * jax.lax.rsqrt(jnp.mean(x * x, axis=-1, keepdims=True) + EPS)
        qkv = normed @ W_qkv.T + b_qkv
        qkv = qkv.reshape(*qkv.shape[:-1], N_HEADS, D_HEAD, 3)
        q, k, v = (qkv[..., 0], qkv[..., 1], qkv[..., 2])
        scores = jnp.einsum('bqhd,bkhd->bhqk', q, k)
        seq = x.shape[-2]
        causal_mask = jnp.triu(jnp.ones((seq, seq), dtype=bool), k=1)
        scores = jnp.where(causal_mask, -jnp.inf, scores)
        attn = jax.nn.softmax(scores, axis=-2)
        z = jnp.einsum('bhqk,bkhd->bqhd', attn, v)
        z = z.reshape(*z.shape[:-2], N_HEADS * D_HEAD)
        return z @ W_o.T + b_o

    def _L0_attn_b_ref(src, Wq, bq, Wk, bk, Wv, bv, Wo, bo):
        import jax, jax.numpy as jnp
        import numpy as np
        HEAD = 8
        BLOCK = 64
        D_MODEL = 128
        B, S, D = src.shape
        H, bs = (HEAD, BLOCK)
        dk = D // H
        nb = S // bs
        q = (src @ Wq + bq).reshape(B, nb, bs, H, dk)
        k = (src @ Wk + bk).reshape(B, nb, bs, H, dk)
        v = (src @ Wv + bv).reshape(B, nb, bs, H, dk)
        scores = jnp.einsum('bnqhd,bnkhd->bhnqk', q, k) * dk ** (-0.5)
        probs = jax.nn.softmax(scores, axis=-1)
        out = jnp.einsum('bhnqk,bnkhd->bnqhd', probs, v).reshape(B, S, D)
        return out @ Wo + bo

    def _L0_ffn_ref(src, Wq, bq, Wk, bk, Wv, bv, Wo, bo, router_w, router_b, W1, b1, W2, b2, ln1_g, ln1_b, ln2_g, ln2_b):
        import jax, jax.numpy as jnp
        import numpy as np
        D_MODEL = 128
        N_HEAD = 16
        HEAD_DIM = D_MODEL // N_HEAD
        D_FF = 512
        N_EXPERTS = 4
        EPS = 1e-05

        def _layer_norm(x, gamma, beta):
            mu = jnp.mean(x, axis=-1, keepdims=True)
            var = jnp.mean((x - mu) ** 2, axis=-1, keepdims=True)
            return (x - mu) / jnp.sqrt(var + EPS) * gamma + beta
        B, T, _ = src.shape
        q = (src @ Wq + bq).reshape(B, T, N_HEAD, HEAD_DIM)
        k = (src @ Wk + bk).reshape(B, T, N_HEAD, HEAD_DIM)
        v = (src @ Wv + bv).reshape(B, T, N_HEAD, HEAD_DIM)
        scale = HEAD_DIM ** (-0.5)
        scores = jnp.einsum('bqhd,bkhd->bhqk', q, k) * scale
        probs = jax.nn.softmax(scores, axis=-1)
        attn = jnp.einsum('bhqk,bkhd->bqhd', probs, v).reshape(B, T, D_MODEL)
        attn = attn @ Wo + bo
        x = _layer_norm(src + attn, ln1_g, ln1_b)
        keys = (x @ router_w + router_b)[..., 0]
        expert_idx = jnp.remainder(jnp.floor(keys).astype(jnp.int32), N_EXPERTS)
        ff_out = jnp.zeros_like(x)
        for e in range(N_EXPERTS):
            h = jax.nn.relu(x @ W1[e] + b1[e])
            y = h @ W2[e] + b2[e]
            ff_out = ff_out + jnp.where((expert_idx == e)[..., None], y, 0.0)
        return _layer_norm(x + ff_out, ln2_g, ln2_b)

    def _L1_attn_a_ref(x, qw, qb, kw, vw, vb, ow, ob, lna_w, lnb_w, lnc_w, lnd_w, lqw, lqb, lkw, lkb, lvw, lvb):
        import jax, jax.numpy as jnp
        import numpy as np
        B, CTX, DIMS, HEAD = (8, 512, 128, 16)
        HD = DIMS // HEAD
        EPS = 1e-05
        THRESH = 0.01
        FACTOR = 0.1
        MAX_IT = 3

        def _ln(x, w):
            m = jnp.mean(x, axis=-1, keepdims=True)
            v = jnp.mean((x - m) ** 2, axis=-1, keepdims=True)
            return (x - m) * jax.lax.rsqrt(v + EPS) * w
        b, ctx, dims = x.shape
        q = _ln(x, lna_w) @ qw.T + qb
        xb = _ln(x, lnb_w)
        k = xb @ kw.T
        v = xb @ vw.T + vb
        split = lambda t: t.reshape(b, ctx, HEAD, HD).transpose(0, 2, 1, 3)
        query, key_t, value = (split(q), split(k), split(v))
        eff = min(ctx, HEAD)
        kn = _ln(key_t[:, :, :eff, :] @ lkw.T + lkb, lnd_w)
        vi = value[:, :, :eff, :] @ lvw.T + lvb
        scale = 1.0 / np.sqrt(HD)

        def step(qcur):
            qn = _ln(qcur[:, :, :eff, :] @ lqw.T + lqb, lnc_w)
            logits = jnp.einsum('bhqd,bhkd->bhqk', qn, kn) * scale
            attn = jax.nn.softmax(logits, axis=-1) @ vi
            return jnp.zeros_like(qcur).at[:, :, :eff, :].set(attn)
        prev = jnp.zeros_like(query)
        attn_out = jnp.zeros_like(query)
        qcur = query
        done = jnp.asarray(False)
        for it in range(MAX_IT):
            iter_out = step(qcur)
            diff = jnp.mean(jnp.abs(iter_out - prev))
            brk = (diff < THRESH + FACTOR * diff) & jnp.asarray(it > 0) & ~done
            attn_out = jnp.where(done, attn_out, iter_out)
            prev = jnp.where(done, prev, iter_out)
            qcur = jnp.where(done | brk, qcur, qcur + iter_out)
            done = done | brk
        out = attn_out.transpose(0, 2, 1, 3).reshape(b, ctx, dims)
        return out @ ow.T + ob

    def _L1_attn_b_ref(x, wq, wk, wv, wo):
        import jax, jax.numpy as jnp
        import numpy as np
        THETA = 10000.0

        def _rope_tables(seq_len, dk, dtype):
            pos = jnp.arange(seq_len, dtype=jnp.float32)[:, None]
            k = jnp.arange(dk // 2, dtype=jnp.float32)[None, :]
            angle = pos / THETA ** (2.0 * k / dk)
            return (jnp.sin(angle).astype(dtype), jnp.cos(angle).astype(dtype))

        def _apply_rope(t, sin, cos):
            even = t[..., 0::2]
            odd = t[..., 1::2]
            even_out = even * cos - odd * sin
            odd_out = even * sin + odd * cos
            out = jnp.stack([even_out, odd_out], axis=-1)
            return out.reshape(t.shape)
        b, s, d = x.shape
        h = 16
        dk = d // h
        Q = jnp.einsum('bsd,ed->bse', x, wq).reshape(b, s, h, dk).transpose(0, 2, 1, 3)
        K = jnp.einsum('bsd,ed->bse', x, wk).reshape(b, s, h, dk).transpose(0, 2, 1, 3)
        V = jnp.einsum('bsd,ed->bse', x, wv).reshape(b, s, h, dk).transpose(0, 2, 1, 3)
        sin, cos = _rope_tables(s, dk, x.dtype)
        Q = _apply_rope(Q, sin, cos)
        K = _apply_rope(K, sin, cos)
        scale = 1.0 / np.sqrt(dk)
        scores = jnp.einsum('bhqd,bhkd->bhqk', Q, K) * scale
        causal = jnp.tril(jnp.ones((s, s), dtype=bool))
        scores = jnp.where(causal, scores, -jnp.inf)
        probs = jax.nn.softmax(scores, axis=-1)
        attn = jnp.einsum('bhqk,bhkd->bhqd', probs, V)
        attn = attn.transpose(0, 2, 1, 3).reshape(b, s, d)
        return jnp.einsum('bse,de->bsd', attn, wo)

    def _L1_ffn_ref(x, router_prob, norm_w, norm_b, q_w, q_b, k_w, k_b, v_w, v_b, o_w, o_b):
        import jax, jax.numpy as jnp
        import numpy as np
        B, T, D, E, H = (4, 256, 128, 4, 8)
        EPS = 1e-05

        def _uniform(k, shape, bound):
            return jax.random.uniform(k, shape, jnp.float32, -bound, bound)

        def _layernorm(x, w, b):
            mu = jnp.mean(x, axis=-1, keepdims=True)
            var = jnp.mean(jnp.square(x - mu), axis=-1, keepdims=True)
            return (x - mu) * jax.lax.rsqrt(var + EPS) * w + b
        e_cnt = router_prob.shape[2]
        b, t, d = x.shape
        n = t // e_cnt
        h = H
        scale = d ** (-0.5)
        qs, ks_, vs = ([], [], [])
        for e in range(e_cnt):
            xe = x[:, e * n:(e + 1) * n, :]
            xn = _layernorm(xe, norm_w, norm_b)
            m = d // 2 ** e
            xm = xn[..., :m]
            qs.append(jnp.einsum('bnm,dm->bnd', xm, q_w[:, :m]) + q_b)
            ks_.append(jnp.einsum('bnm,dm->bnd', xm, k_w[:, :m]) + k_b)
            vs.append(jnp.einsum('bnm,dm->bnd', xm, v_w[:, :m]) + v_b)
        q = jnp.concatenate(qs, axis=1)
        k = jnp.concatenate(ks_, axis=1)
        v = jnp.concatenate(vs, axis=1)
        dh = d // h
        q = q.reshape(b, t, h, dh).transpose(0, 2, 1, 3)
        k = k.reshape(b, t, h, dh).transpose(0, 2, 1, 3)
        v = v.reshape(b, t, h, dh).transpose(0, 2, 1, 3)
        attn = jnp.einsum('bhqd,bhkd->bhqk', q, k) * scale
        attn = jax.nn.softmax(attn, axis=-1)
        attn_out = jnp.einsum('bhqk,bhkd->bhqd', attn, v)
        attn_out = attn_out.transpose(0, 2, 1, 3).reshape(b, t, d)
        outs = []
        for e in range(e_cnt):
            sl = slice(e * n, (e + 1) * n)
            m = d // 2 ** e
            xm = attn_out[:, sl, :m]
            out = jnp.einsum('bnm,om->bno', xm, o_w[:m, :m]) + o_b[:m]
            pad = d - m
            if pad:
                out = jnp.pad(out, ((0, 0), (0, 0), (0, pad)))
            outs.append(out + x[:, sl, :])
        return jnp.concatenate(outs, axis=1)
    x = L0_attn_a_x
    x = x + _L0_attn_a_ref(_layernorm(x, axis=-1), L0_attn_a_W_qkv, L0_attn_a_b_qkv, L0_attn_a_W_o, L0_attn_a_b_o)
    x = x + _L0_ffn_ref(_layernorm(x, axis=-1), L0_ffn_Wq, L0_ffn_bq, L0_ffn_Wk, L0_ffn_bk, L0_ffn_Wv, L0_ffn_bv, L0_ffn_Wo, L0_ffn_bo, L0_ffn_router_w, L0_ffn_router_b, L0_ffn_W1, L0_ffn_b1, L0_ffn_W2, L0_ffn_b2, L0_ffn_ln1_g, L0_ffn_ln1_b, L0_ffn_ln2_g, L0_ffn_ln2_b)
    x = x + _L0_attn_b_ref(_layernorm(x, axis=-1), L0_attn_b_Wq, L0_attn_b_bq, L0_attn_b_Wk, L0_attn_b_bk, L0_attn_b_Wv, L0_attn_b_bv, L0_attn_b_Wo, L0_attn_b_bo)
    x = x + _L0_ffn_ref(_layernorm(x, axis=-1), L0_ffn_Wq, L0_ffn_bq, L0_ffn_Wk, L0_ffn_bk, L0_ffn_Wv, L0_ffn_bv, L0_ffn_Wo, L0_ffn_bo, L0_ffn_router_w, L0_ffn_router_b, L0_ffn_W1, L0_ffn_b1, L0_ffn_W2, L0_ffn_b2, L0_ffn_ln1_g, L0_ffn_ln1_b, L0_ffn_ln2_g, L0_ffn_ln2_b)
    x = x + _L1_attn_a_ref(_layernorm(x, axis=-1), L1_attn_a_qw, L1_attn_a_qb, L1_attn_a_kw, L1_attn_a_vw, L1_attn_a_vb, L1_attn_a_ow, L1_attn_a_ob, L1_attn_a_lna_w, L1_attn_a_lnb_w, L1_attn_a_lnc_w, L1_attn_a_lnd_w, L1_attn_a_lqw, L1_attn_a_lqb, L1_attn_a_lkw, L1_attn_a_lkb, L1_attn_a_lvw, L1_attn_a_lvb)
    x = x + _L1_ffn_ref(_layernorm(x, axis=-1), L1_ffn_router_prob, L1_ffn_norm_w, L1_ffn_norm_b, L1_ffn_q_w, L1_ffn_q_b, L1_ffn_k_w, L1_ffn_k_b, L1_ffn_v_w, L1_ffn_v_b, L1_ffn_o_w, L1_ffn_o_b)
    x = x + _L1_attn_b_ref(_layernorm(x, axis=-1), L1_attn_b_wq, L1_attn_b_wk, L1_attn_b_wv, L1_attn_b_wo)
    x = x + _L1_ffn_ref(_layernorm(x, axis=-1), L1_ffn_router_prob, L1_ffn_norm_w, L1_ffn_norm_b, L1_ffn_q_w, L1_ffn_q_b, L1_ffn_k_w, L1_ffn_k_b, L1_ffn_v_w, L1_ffn_v_b, L1_ffn_o_w, L1_ffn_o_b)
    return x

_drawn_inputs = setup_inputs


def setup_inputs(seed=0):
    import zlib

    import numpy as np

    out = dict(_drawn_inputs(seed))
    spreads = {'L0_attn_a_b_qkv': (0.0, 0.1),
     'L0_attn_a_b_o': (0.0, 0.1),
     'L0_ffn_bq': (0.0, 0.1),
     'L0_ffn_bk': (0.0, 0.8),
     'L0_ffn_bv': (0.0, 0.1),
     'L0_ffn_bo': (0.0, 0.1),
     'L0_ffn_b1': (0.0, 0.1),
     'L0_ffn_b2': (0.0, 0.1),
     'L0_ffn_ln1_g': (1.0, 0.2),
     'L0_ffn_ln1_b': (0.0, 0.1),
     'L0_ffn_ln2_g': (1.0, 0.2),
     'L0_ffn_ln2_b': (0.0, 0.1),
     'L1_attn_a_qb': (0.0, 0.8),
     'L1_attn_a_vb': (0.0, 0.8),
     'L1_attn_a_ob': (0.0, 0.1),
     'L1_attn_a_lna_w': (1.0, 0.6),
     'L1_attn_a_lnb_w': (1.0, 0.6),
     'L1_attn_a_lnc_w': (1.0, 0.6),
     'L1_attn_a_lnd_w': (1.0, 0.6),
     'L1_attn_a_lqb': (0.0, 0.8),
     'L1_attn_a_lkb': (0.0, 0.8),
     'L1_attn_a_lvb': (0.0, 0.8),
     'L1_ffn_norm_w': (1.0, 0.6),
     'L1_ffn_norm_b': (0.0, 0.8)}
    factors = {'L0_attn_b_Wq': 8.0,
     'L0_attn_b_bq': 8.0,
     'L0_attn_b_Wk': 8.0,
     'L0_attn_b_bk': 8.0,
     'L0_attn_b_Wv': 5.292,
     'L0_attn_b_bv': 4.394,
     'L0_attn_b_Wo': 3.034,
     'L0_attn_b_bo': 3.439,
     'L1_attn_a_qw': 8.0,
     'L1_attn_a_kw': 8.0,
     'L1_attn_a_vw': 8.0,
     'L1_attn_a_ow': 8.0,
     'L1_attn_a_lqw': 8.0,
     'L1_attn_a_lkw': 8.0,
     'L1_attn_a_lvw': 8.0,
     'L1_ffn_q_w': 8.0,
     'L1_ffn_q_b': 8.0,
     'L1_ffn_k_w': 8.0,
     'L1_ffn_k_b': 8.0,
     'L1_ffn_v_w': 4.599,
     'L1_ffn_v_b': 7.258,
     'L1_ffn_o_w': 3.928,
     'L1_ffn_o_b': 3.232}
    for name, (base, spread) in spreads.items():
        noise = np.random.default_rng([zlib.crc32(name.encode()), seed]).standard_normal(out[name].shape)
        drawn = base * np.exp(spread * noise) if base else spread * noise
        out[name] = jnp.asarray(drawn.astype(out[name].dtype))
    for name, factor in factors.items():
        out[name] = (out[name] * factor).astype(out[name].dtype)
    return out
```

```python
from contextlib import ExitStack, contextmanager

import concourse.bass as bass
import numpy as np
from concourse import mybir

ACT = mybir.ActivationFunctionType
ALU = mybir.AluOpType
F32 = mybir.dt.float32
BF16 = mybir.dt.bfloat16
I32 = mybir.dt.int32
AX_X = mybir.AxisListType.X

P = 128
BATCH, SEQ, D = 4, 1024, 128
TILES = BATCH * SEQ // P
TPB = SEQ // P
CHUNK = 512
TPC = CHUNK // P
CHUNKS = BATCH * SEQ // CHUNK
HG = 4
EPS = 1e-5
MASKED = -1.0e30


class Tally:

    def __init__(self, sem):
        self.sem, self.n, self.loop = sem, 0, 0

    def add(self, k=1):
        self.n += k
        return self.value()

    def one(self, k=1):
        self.n += k
        return k

    def past(self, back=0):
        v = self.value(back)
        return not isinstance(v, int) or v > 0

    def value(self, back=0):
        v = self.n - back
        return v if isinstance(self.loop, int) else self.loop + v


def hold(eng, tick):
    eng.sem_inc(tick, 1)


def run_steps(eng, tallies, emit, total, full_from, unroll=2):
    for s in range(full_from + 1):
        before = [t.n for t in tallies]
        emit(s, s // unroll, s % unroll)
    first = full_from + 1
    trips = max(0, total - 1 - first) // unroll
    if trips:
        per = [unroll * (t.n - b) for t, b in zip(tallies, before)]
        with eng.Fori(0, trips) as i:
            start = [t.n for t in tallies]
            for t, k in zip(tallies, per):
                t.loop = i * k if k else 0
            for s in range(first, first + unroll):
                emit(i * unroll + s, i + s // unroll, s % unroll)
            for t, k, a in zip(tallies, per, start):
                assert t.n - a == k, (t.sem, t.n - a, k)
                t.n, t.loop = a, 0
        for t, k in zip(tallies, per):
            t.n += k * trips
    for s in range(first + unroll * trips, total):
        emit(s, s // unroll, s % unroll)


@contextmanager
def semaphores(nc, name):
    taken = []

    def take(n):
        taken.append(nc.alloc_semaphore(f"{name}_{n}"))
        return taken[-1]

    yield take
    nc.clear_and_free_semaphores(taken)
    nc.all_engine_barrier()


class Core:
    pass



def plan_full():
    maxes = [dict(mms=[(h, qb, kc * 512, 512, 0)], mask=[], n=1, w=512, h0=h, qb=qb, kc=kc)
             for qb in range(TPB) for h in range(HG) for kc in range(2)]
    subs = []
    for qc in range(2):
        for kb in range(TPB):
            tiles = [dict(mms=[(2 * t + k, kb, qc * 512, 512, 512 * k) for k in range(2)], mask=[],
                          w=512, halves=True) for t in range(2)]
            evs = [(h, kb, 0, 512, h // 2, 512 * (h % 2), kb == 0, kb == TPB - 1) for h in range(HG)]
            subs.append(dict(tiles=tiles, evs=evs, qc=qc, last=kb == TPB - 1))
    return dict(maxes=maxes, subs=subs, kc=2)


def plan_causal():
    maxes = []
    for qb in range(TPB):
        for kc in range(1 + qb // 4):
            w = min(512, (qb + 1) * P - kc * 512)
            n = {128: 4, 256: 2}.get(w, 1)
            for h0 in range(0, HG, n):
                diag = kc * 512 + w == (qb + 1) * P
                maxes.append(dict(mms=[(h0 + i, qb, kc * 512, w, i * w) for i in range(n)],
                                  mask=[i * w + w - P for i in range(n)] if diag else [],
                                  n=n, w=w, h0=h0, qb=qb, kc=kc))
    subs = []
    for qc in range(2):
        for kb in range(4 * qc + 4):
            q0 = max(qc * 512, kb * P)
            w = (qc + 1) * 512 - q0
            tiles = [dict(mms=[(2 * t + k, kb, q0, w, 512 * k) for k in range(2)],
                          mask=[0, 512] if q0 == kb * P else [], w=w, halves=True) for t in range(2)]
            evs = [(h, kb, q0 - qc * 512, w, h // 2, 512 * (h % 2), kb == 0, kb == 4 * qc + 3)
                   for h in range(HG)]
            subs.append(dict(tiles=tiles, evs=evs, qc=qc, last=kb == 4 * qc + 3))
    return dict(maxes=maxes, subs=subs, kc=2)


def plan_local():
    maxes = [dict(mms=[(h, qb, qb * P, P, h * P) for h in range(HG)], mask=[h * P for h in range(HG)],
                  n=HG, w=P, h0=0, qb=qb, kc=0) for qb in range(TPB)]
    subs = []
    for x in range(TPB // 2):
        js = (2 * x, 2 * x + 1)
        mms = [(h, j, j * P, P, 512 * (j % 2) + h * P) for j in js for h in range(HG)]
        tiles = [dict(mms=mms, mask=[m[4] for m in mms], w=512, halves=True)]
        evs = [(h, j, (j % 4) * P, P, 0, 512 * (j % 2) + h * P, True, True) for j in js for h in range(HG)]
        subs.append(dict(tiles=tiles, evs=evs, qc=x // 2, last=x % 2 == 1))
    return dict(maxes=maxes, subs=subs, kc=1)


def allot(n_items, n_slots, lead):
    slots = max(1, n_slots - lead)
    return [(n_items * (s + 1)) // slots - (n_items * s) // slots if s < slots else 0
            for s in range(n_slots)]



def project(nc, c, L):
    name, G, dk = L["name"], L["heads"] // HG, L["dk"]
    rope, double, keep = L.get("rope"), L.get("double"), L.get("keep")
    n_qk = 4 if rope else 2
    with ExitStack() as ctx:
        sb = lambda n, s, d=F32: ctx.enter_context(nc.sbuf_tensor(f"{name}_{n}", s, d))
        ps = lambda n, s: ctx.enter_context(nc.psum_tensor(f"{name}_{n}", s, F32))
        sem = ctx.enter_context(semaphores(nc, name))
        stats, mv = sb("stats", [P, 2, TPC, 6]), sb("mv", [P, 2, TPC, 2])
        rs, tmp = sb("rs", [P, 2, 2, TPC]), sb("tmp", [P, 2, TPC])
        xn, xnT = sb("xn", [P, 2, TPC, D]), sb("xnT", [P, 2, CHUNK])
        full = sb("full", [P, 2, CHUNK])
        rest = sb("rest", [P, 2, CHUNK])
        part = sb("part", [P, 2, 2, 3, CHUNK], BF16)
        rot = sb("rot", [P, 2, CHUNK]) if rope else None
        psT, psQK, psV = ps("psT", [P, 2, CHUNK]), ps("psQK", [P, n_qk, CHUNK]), ps("psV", [P, CHUNK])
        s_var, s_rstd, s_xn, s_T, s_xnT = (sem(n) for n in ("var", "rstd", "xn", "T", "xnT"))
        s_qk, s_high, s_rest, s_mid, s_cut = (sem(n) for n in ("qk", "high", "rest", "mid", "cut"))
        s_v, s_vout, s_dve, s_pool, tick, s_tickp, s_ticks, s_rot = (
            sem(n) for n in ("v", "vout", "dve", "pool", "tick", "tickp", "ticks", "rot"))
        s_taken = s_rot if rope else s_high
        s_st, STORE = [sem("stored0"), sem("stored1")], 6 * 16
        scratch = c.scratch.rearrange("(a g t r n) -> a g t r n", a=2, g=BATCH * G, t=3, r=HG * dk)

        with nc.Block() as block:
            @block.vector
            def _(eng):
                chain, rstd, T, high, rest_, mid, rotd = (
                    Tally(s) for s in (s_dve, s_rstd, s_T, s_high, s_rest, s_mid, s_rot))
                v, qk, var, xnr, vout, cut = (Tally(s) for s in (s_v, s_qk, s_var, s_xn, s_vout, s_cut))

                def norm(s, half, p):
                    for j in range(TPC):
                        eng.bn_stats(stats[:, p, j, :], c.X[:, s * TPC + j, :]).then_inc(s_dve, chain.one())
                    eng.wait_ge(s_dve, chain.value())
                    hold(eng, tick)
                    for j in range(TPC):
                        ins = eng.bn_aggr(mv[:, p, j, :], stats[:, p, j, :])
                    ins.then_inc(s_var, var.one())
                    eng.wait_ge(s_rstd, rstd.add())
                    if T.past():
                        eng.wait_ge(s_T, T.value())
                    if not isinstance(s, int) or s >= 1:
                        T.add()
                    for j in range(TPC):
                        ins = eng.tensor_scalar(xn[:, p, j, :], c.X[:, s * TPC + j, :], mv[:, p, j, 0:1],
                                                rs[:, p, 1 if double else 0, j:j + 1], ALU.subtract, ALU.mult)
                    ins.then_inc(s_xn, xnr.one())
                    if keep:
                        for j in range(TPC):
                            ins = eng.tensor_scalar(c.Y[:, s * TPC + j, :], c.X[:, s * TPC + j, :],
                                                    mv[:, p, j, 0:1], rs[:, p, 0, j:j + 1],
                                                    ALU.subtract, ALU.mult)
                        ins.then_inc(s_dve, chain.one())

                def after(b, p):
                    if rope:
                        eng.wait_ge(s_qk, qk.add(2))
                        for a in range(2):
                            eng.tensor_tensor(full[:, a, :], psQK[:, 2 * a, :], c.rope[:, 0, p * CHUNK:(p + 1) * CHUNK], ALU.mult).then_inc(s_dve, chain.one())
                            eng.tensor_tensor(rot[:, a, :], psQK[:, 2 * a + 1, :], c.rope[:, 1, p * CHUNK:(p + 1) * CHUNK], ALU.mult).then_inc(s_dve, chain.one())
                            eng.wait_ge(s_dve, chain.value())
                            eng.tensor_tensor(full[:, a, :], full[:, a, :], rot[:, a, :], ALU.add).then_inc(s_rot, rotd.one())
                    if cut.past():
                        eng.wait_ge(s_cut, cut.value())
                    for a in range(2):
                        eng.wait_ge(s_high, high.add())
                        eng.tensor_tensor(rest[:, a, :], full[:, a, :], part[:, p, a, 0, :], ALU.subtract).then_inc(s_rest, rest_.one())
                    eng.wait_ge(s_v, v.add())
                    eng.tensor_tensor(
                        c.V[:].rearrange("p (g j r) -> p g j r", g=BATCH * G, j=TPB)[:, bass.ds(b * G, G), p * TPC:(p + 1) * TPC, :],
                        psV[:].rearrange("p (j g r) -> p g j r", j=TPC, g=G),
                        L["bv"].rearrange("p (g r) -> p g r", g=G)[:, :, None, :].to_broadcast([P, G, TPC, HG * dk]),
                        ALU.add).then_inc(s_vout, vout.one())
                    for a in range(2):
                        eng.wait_ge(s_mid, mid.add())
                        if rest_.past():
                            eng.wait_ge(s_rest, rest_.value())
                        eng.tensor_tensor(part[:, p, a, 2, :], rest[:, a, :], part[:, p, a, 1, :], ALU.subtract).then_inc(s_cut, cut.one())

                def emit(s, half, p):
                    if not isinstance(s, int) or s < CHUNKS:
                        norm(s, half, p)
                    if not isinstance(s, int) or s >= 1:
                        after(half - 1 + p, 1 - p)

                run_steps(eng, [chain, rstd, T, high, rest_, mid, v, qk, var, xnr, vout, cut, rotd],
                          emit, CHUNKS + 1, 2)

            @block.gpsimd
            def _(eng):
                var, chain, rstd = Tally(s_var), Tally(s_pool), Tally(s_rstd)

                def emit(s, half, p):
                    eng.wait_ge(s_var, var.add())
                    hold(eng, s_tickp)

                    def power(j, source):
                        eng.tensor_scalar(tmp[:, p, :], source, EPS, None, ALU.add).then_inc(s_pool, chain.one())
                        eng.wait_ge(s_pool, chain.value())
                        return eng.tensor_tensor(rs[:, p, j, :], tmp[:, p, :], c.minus_half[:, 0:TPC], ALU.pow)

                    if not double:
                        power(0, mv[:, p, :, 1]).then_inc(s_rstd, rstd.one())
                        return
                    power(0, mv[:, p, :, 1]).then_inc(s_pool, chain.one())
                    eng.wait_ge(s_pool, chain.value())
                    eng.tensor_tensor(tmp[:, p, :], mv[:, p, :, 1], rs[:, p, 0, :], ALU.mult).then_inc(s_pool, chain.one())
                    eng.wait_ge(s_pool, chain.value())
                    eng.tensor_tensor(tmp[:, p, :], tmp[:, p, :], rs[:, p, 0, :], ALU.mult).then_inc(s_pool, chain.one())
                    eng.wait_ge(s_pool, chain.value())
                    hold(eng, s_tickp)
                    power(1, tmp[:, p, :]).then_inc(s_pool, chain.one())
                    eng.wait_ge(s_pool, chain.value())
                    eng.tensor_tensor(rs[:, p, 1, :], rs[:, p, 1, :], rs[:, p, 0, :], ALU.mult).then_inc(s_rstd, rstd.one())

                run_steps(eng, [var, chain, rstd], emit, CHUNKS, 1)

            @block.tensor
            def _(eng):
                xnr, T, xnTr, qk, taken, v, vout = (
                    Tally(s) for s in (s_xn, s_T, s_xnT, s_qk, s_taken, s_v, s_vout))

                def emit(s, half, p):
                    eng.wait_ge(s_xn, xnr.add())
                    if xnTr.past(1):
                        eng.wait_ge(s_xnT, xnTr.value(1))
                    for j in range(TPC):
                        ins = eng.transpose(psT[:, p, j * P:(j + 1) * P], xn[:, p, j, :], c.ident[:])
                    ins.then_inc(s_T, T.one())
                    eng.wait_ge(s_xnT, xnTr.add())
                    if taken.past():
                        eng.wait_ge(s_taken, taken.value())
                    taken.add(2)
                    for a in range(n_qk):
                        ins = eng.matmul(psQK[:, a, :], L["wqk"][a], xnT[:, p, :], start=True, stop=True)
                        if not rope or a % 2:
                            ins.then_inc(s_qk, qk.one())
                    if vout.past():
                        eng.wait_ge(s_vout, vout.value())
                    vout.add()
                    for j in range(TPC):
                        ins = eng.matmul(psV[:, j * P:(j + 1) * P], xnT[:, p, j * P:(j + 1) * P], L["wv"],
                                         start=True, stop=True)
                    ins.then_inc(s_v, v.one())

                run_steps(eng, [xnr, T, xnTr, qk, taken, v, vout], emit, CHUNKS, 1)

            @block.scalar
            def _(eng):
                T, xnTr, qk, high, rest_, mid, v, rotd = (
                    Tally(s) for s in (s_T, s_xnT, s_qk, s_high, s_rest, s_mid, s_v, s_rot))

                def emit(s, half, p):
                    eng.wait_ge(s_T, T.add())
                    if v.past(1):
                        eng.wait_ge(s_v, v.value(1))
                    v.add()
                    if double:
                        for k in range(2):
                            ins = eng.activation(xnT[:, p, k * 256:(k + 1) * 256], psT[:, p, k * 256:(k + 1) * 256],
                                                 ACT.Identity, scale=c.norm_w[:, 2 * p + k:2 * p + k + 1],
                                                 bias=c.norm_b[:, 2 * p + k:2 * p + k + 1])
                    else:
                        ins = eng.copy(xnT[:, p, :], psT[:, p, :])
                    ins.then_inc(s_xnT, xnTr.one())
                    if not isinstance(s, int) or s >= 2:
                        eng.wait_ge(s_st[p], half * STORE)
                    for a in range(2):
                        if rope:
                            eng.wait_ge(s_rot, rotd.add())
                            eng.copy(part[:, p, a, 0, :], full[:, a, :]).then_inc(s_high, high.one())
                        else:
                            eng.wait_ge(s_qk, qk.add())
                            if rest_.past():
                                eng.wait_ge(s_rest, rest_.value())
                            eng.activation(full[:, a, :], psQK[:, a, :], ACT.Identity, bias=L["bqk"][a])
                            eng.activation(part[:, p, a, 0, :], psQK[:, a, :], ACT.Identity, bias=L["bqk"][a]).then_inc(s_high, high.one())
                    for a in range(2):
                        eng.wait_ge(s_rest, rest_.add())
                        eng.copy(part[:, p, a, 1, :], rest[:, a, :]).then_inc(s_mid, mid.one())

                run_steps(eng, [T, xnTr, qk, high, rest_, mid, v, rotd], emit, CHUNKS, 1)

            @block.sync
            def _(eng):
                cut = Tally(s_cut)

                def emit(s, half, p):
                    eng.wait_ge(s_cut, cut.add(2))
                    hold(eng, s_ticks)
                    for a in range(2):
                        for t in range(3):
                            dst = scratch[a, bass.ds(half * G, G), t, :, p * CHUNK:(p + 1) * CHUNK]
                            eng.dma_start(dst, part[:, p, a, t, :]).then_inc(s_st[p], 16)

                run_steps(eng, [cut], emit, CHUNKS, 1)
                for p in range(2):
                    eng.wait_ge(s_st[p], CHUNKS // 2 * STORE)



def attend(nc, c, L):
    name, G, dk, plan = L["name"] + "a", L["heads"] // HG, L["dk"], L["plan"]
    NG = BATCH * G
    pairs = L["pairs"]
    R = len(pairs) * dk
    maxes, subs, KC = plan["maxes"], plan["subs"], plan["kc"]
    NM, NX = len(maxes), len(subs)
    lots = allot(NM, NX, L.get("lead", 2))
    starts = [sum(lots[:x]) for x in range(NX)]
    ct_at = next(x for x in range(NX) if starts[x] + lots[x] == NM) + (1 if NX > 4 else 0)
    ct_at = min(ct_at, NX - 1)
    qc0_end = max(x for x in range(NX) if subs[x]["qc"] == 0)
    with ExitStack() as ctx:
        sb = lambda n, s, d=F32: ctx.enter_context(nc.sbuf_tensor(f"{name}_{n}", s, d))
        ps = lambda n, s: ctx.enter_context(nc.psum_tensor(f"{name}_{n}", s, F32))
        sem = ctx.enter_context(semaphores(nc, name))
        Q, K = sb("Q", [P, 2, HG, SEQ], BF16), sb("K", [P, 2, HG, SEQ], BF16)
        Vs = sb("Vs", [P, 2, TPB, HG, 32])
        E = sb("E", [P, 4, 2 * 512])
        OT = sb("OT", [P, 2, 512])
        rowmax, rowmax1 = sb("rowmax", [P, HG, TPB, KC]), sb("rowmax1", [P, HG * TPB])
        negf, rem, shift = sb("negf", [HG * TPB, P]), sb("rem", [HG * TPB, P]), sb("shift", [HG * TPB, 3, P], BF16)
        rz = sb("rz", [P, TPC, HG])
        psM, psE = ps("psM", [P, 2, 512]), ps("psE", [P, 2, 2 * 512])
        psO, psX = ps("psO", [P, 512]), ps("psX", [P, 512])
        s_load, s_shift = [sem("load0"), sem("load1")], [sem("shift0"), sem("shift1")]
        s_vs, s_mm, s_red, s_cm, s_ct, s_cs = (sem(n) for n in ("vs", "mm", "red", "cm", "ct", "cs"))
        s_smm, s_exp, s_ev, s_oev, s_tom, s_xfree = (
            sem(n) for n in ("smm", "exp", "ev", "oev", "tom", "xfree"))
        s_dve, s_set, s_att, tick, tickp = (sem(n) for n in ("dve", "set", "att", "tick", "tickp"))
        scratch = c.scratch.rearrange("(a g t r n) -> a g t (r n)", a=2, g=NG, t=3, r=HG * dk)
        rows_of = lambda a, s, t0, t1: scratch[a, bass.ds(s, 1), t0:t1, :].rearrange(
            "g t (r n) -> (g t r) n", n=HG * SEQ)
        V = c.V[:].rearrange("p (g j h d) -> p g j h d", g=NG, j=TPB, h=HG)
        ATT = c.ATT[:].rearrange("p (g j h d) -> p g j h d", g=NG, j=TPB, h=HG)
        fills = [(0, i * dk, q, q + 1) for i, (q, _) in enumerate(pairs)]
        i = 0
        while i < len(pairs):
            n = 1
            while i + n < len(pairs) and pairs[i + n][1] == pairs[i][1] + n:
                n += 1
            fills.append((1, i * dk, pairs[i][1], pairs[i][1] + n))
            i += n
        LOAD = 16 * len(fills)
        is_first = lambda s: isinstance(s, int) and s == 0
        has_max = lambda s: not isinstance(s, int) or s < NG
        has_exp = lambda s: not isinstance(s, int) or s >= 1
        late = lambda s: not isinstance(s, int) or s >= 2

        with nc.Block() as block:
            @block.sync
            def _(eng):
                cs, smm = Tally(s_cs), Tally(s_smm)

                def load(s, p):
                    for a, row, t0, t1 in fills:
                        dst = (Q, K)[a][row:row + (t1 - t0) * dk, p, :, :].rearrange("r h n -> r (h n)")
                        eng.dma_start(dst, rows_of(a, s, t0, t1)).then_inc(s_load[p], 16)

                eng.wait_ge(s_set, 4)
                load(0, 0)

                def emit(s, half, p):
                    if not isinstance(s, int) or s < NG:
                        if is_first(s):
                            load(1, 1)
                        eng.wait_ge(s_cs, cs.add())
                        hold(eng, tick)
                        for t in range(3):
                            dst = Q[R + t:R + t + 1, p, :, :].rearrange("r h (b n) -> r (h b) n", n=P)
                            eng.dma_start(dst, shift[:, t, :]).then_inc(s_shift[p], 16)
                    if (not isinstance(s, int) or s >= 1):
                        eng.wait_ge(s_smm, smm.add(sum(len(x["tiles"]) for x in subs)))
                        if not isinstance(s, int) or s + 1 < NG:
                            hold(eng, tick)
                            load(s + 1, 1 - p)

                run_steps(eng, [cs, smm], emit, NG + 1, 2)

            @block.gpsimd
            def _(eng):
                eng.memset(K[:].rearrange("p u h n -> p (u h n)"), 1.0).then_inc(s_set, 1)
                eng.memset(Vs[:].rearrange("p u j h d -> p (u j h d)"), 0.0).then_inc(s_set, 1)
                eng.wait_ge(s_set, 4)
                eng.memset(Vs[:, 0, :, :, dk:dk + 1], 1.0).then_inc(s_set, 1)
                eng.memset(Vs[:, 1, :, :, dk:dk + 1], 1.0).then_inc(s_set, 1)
                ev, vs = Tally(s_ev), Tally(s_vs)
                eng.wait_ge(s_set, 6)

                def emit(s, half, p):
                    if not isinstance(s, int) or s >= 2:
                        eng.wait_ge(s_ev, ev.add(NX))
                        hold(eng, tickp)
                    eng.tensor_copy(Vs[:, p, :, :, 0:dk], V[:, bass.ds(s, 1)].rearrange("p g j h d -> p (g j) h d")).then_inc(s_vs, vs.one())

                run_steps(eng, [ev, vs], emit, NG, 2)

            @block.tensor
            def _(eng):
                mm, red, cm, ct, smm, ex, ev, oev, tom, xfree, vs = (
                    Tally(s) for s in (s_mm, s_red, s_cm, s_ct, s_smm, s_exp, s_ev, s_oev, s_tom, s_xfree, s_vs))

                turned = Tally(s_oev)

                def max_tile(m, p):
                    t = maxes[m]
                    if red.past(1):
                        eng.wait_ge(s_red, red.value(1))
                    red.add()
                    bank = psM[:, m % 2, :]
                    for i, (h, qb, k0, w, off) in enumerate(t["mms"]):
                        masked = i < len(t["mask"])
                        ins = eng.matmul(bank[:, off:off + w], Q[0:R, p, h, qb * P:(qb + 1) * P],
                                         K[0:R, p, h, k0:k0 + w], start=True, stop=not masked)
                        if masked:
                            o = t["mask"][i]
                            ins = eng.matmul(bank[:, o:o + P], c.ident_bf[:], L["mask_qk"], start=False, stop=True)
                    ins.then_inc(s_mm, mm.one())

                def score_tile(t, k, p):
                    if ex.past(1):
                        eng.wait_ge(s_exp, ex.value(1))
                    ex.add()
                    bank = psE[:, k % 2, :]
                    for i, (h, kb, q0, w, off) in enumerate(t["mms"]):
                        masked = i < len(t["mask"])
                        ins = eng.matmul(bank[:, off:off + w], K[0:R + 3, p, h, kb * P:(kb + 1) * P],
                                         Q[0:R + 3, p, h, q0:q0 + w], start=True, stop=not masked)
                        if masked:
                            o = t["mask"][i]
                            ins = eng.matmul(bank[:, o:o + P], c.ident_bf[:], L["mask_kq"], start=False, stop=True)
                    ins.then_inc(s_smm, smm.one())

                def value_products(x, p, done):
                    s = subs[x]
                    eng.wait_ge(s_exp, done)
                    if s["evs"][0][6] and (x == 0 or subs[x - 1]["qc"] != s["qc"]):
                        if oev.past():
                            eng.wait_ge(s_oev, oev.value())
                        oev.add()
                    for h, kb, col, w, tile, off, first, last in s["evs"]:
                        ins = eng.matmul(psO[32 * h:32 * h + 32, col:col + w], Vs[:, p, kb, h, :],
                                         E[:, (x % 2) * 2 + tile, off:off + w], start=first, stop=last)
                    ins.then_inc(s_ev, ev.one())

                def turn_out(qc):
                    eng.wait_ge(s_oev, turned.add())
                    if xfree.past():
                        eng.wait_ge(s_xfree, xfree.value())
                    xfree.add()
                    for j in range(TPC):
                        ins = eng.transpose(psX[:, j * P:(j + 1) * P], OT[:, qc, j * P:(j + 1) * P], c.ident[:])
                    ins.then_inc(s_tom, tom.one())

                def emit(s, half, p):
                    k = 0
                    if has_max(s):
                        eng.wait_ge(s_load[p], (half + 1) * LOAD)
                    if has_exp(s):
                        eng.wait_ge(s_shift[1 - p], (half + p) * 48)
                        eng.wait_ge(s_vs, vs.add())
                    for x in range(NX):
                        if has_exp(s):
                            for t in subs[x]["tiles"]:
                                score_tile(t, k, 1 - p)
                                k += 1
                        if has_max(s):
                            for m in range(starts[x], starts[x] + lots[x]):
                                max_tile(m, p)
                        if has_exp(s) and x >= 1:
                            value_products(x - 1, 1 - p, ex.value(len(subs[x]["tiles"])))
                        if late(s) and x == min(1, NX - 1):
                            turn_out(1)
                        if has_exp(s) and x == min(qc0_end + 2, NX - 1):
                            turn_out(0)
                        if has_max(s) and x == ct_at:
                            eng.wait_ge(s_cm, cm.add())
                            if xfree.past():
                                eng.wait_ge(s_xfree, xfree.value())
                            xfree.add()
                            eng.transpose(psX[0:HG * TPB, 0:P], rowmax1[:], c.ident[:]).then_inc(s_ct, ct.one())
                    if has_exp(s):
                        value_products(NX - 1, 1 - p, ex.value())

                eng.wait_ge(s_set, 6)
                run_steps(eng, [mm, red, cm, ct, smm, ex, ev, oev, tom, xfree, vs, turned], emit, NG + 1, 2)
                turn_out(1)

            @block.scalar
            def _(eng):
                smm, ev, ex, oev, tom = (Tally(s) for s in (s_smm, s_ev, s_exp, s_oev, s_tom))

                def take_out(qc):
                    if ev.past(1 - qc):
                        eng.wait_ge(s_ev, ev.value(1 - qc))
                    if tom.past(1):
                        eng.wait_ge(s_tom, tom.value(1))
                    tom.add()
                    eng.copy(OT[:, qc, :], psO[:]).then_inc(s_oev, oev.one())

                def emit(s, half, p):
                    if not has_exp(s):
                        return
                    k = 0
                    for x in range(NX):
                        if ev.past(1):
                            eng.wait_ge(s_ev, ev.value(1))
                        ev.add()
                        for i, t in enumerate(subs[x]["tiles"]):
                            eng.wait_ge(s_smm, smm.add())
                            o = E[:, (x % 2) * 2 + i, :].rearrange("p (k n) -> p k n", k=2)[:, :, 0:t["w"]]
                            v = psE[:, k % 2, :].rearrange("p (k n) -> p k n", k=2)[:, :, 0:t["w"]]
                            eng.activation(o, v, ACT.Exp, scale=L["scale"]).then_inc(s_exp, ex.one())
                            k += 1
                        if x == qc0_end + 1:
                            take_out(0)
                    take_out(1)

                run_steps(eng, [smm, ev, ex, oev, tom], emit, NG + 1, 2)

            @block.vector
            def _(eng):
                eng.memset(rowmax[:].rearrange("p h b k -> p (h b k)"), -3.0e38).then_inc(s_set, 1)
                eng.memset(Q[:].rearrange("p u h n -> p (u h n)"), 0.0).then_inc(s_set, 1)
                mm, red, chain, cm, ct, cs, tom, xfree = (
                    Tally(s) for s in (s_mm, s_red, s_dve, s_cm, s_ct, s_cs, s_tom, s_xfree))
                eng.wait_ge(s_set, 4)

                def reduce(m):
                    t = maxes[m]
                    eng.wait_ge(s_mm, mm.add())
                    v = psM[:, m % 2, 0:t["n"] * t["w"]].rearrange("p (n w) -> p n w", n=t["n"])
                    eng.tensor_reduce(rowmax[:, t["h0"]:t["h0"] + t["n"], t["qb"], t["kc"]:t["kc"] + 1].rearrange("p h k -> p (h k)"),
                                             v, AX_X, ALU.max).then_inc(s_red, red.one())

                def normalise(s, qc):
                    eng.wait_ge(s_tom, tom.add())
                    x = psX[:].rearrange("p (j h d) -> p j h d", j=TPC, h=HG)
                    eng.reciprocal(rz[:], x[:, :, :, dk]).then_inc(s_dve, chain.one())
                    eng.wait_ge(s_dve, chain.value())
                    eng.tensor_tensor(
                        ATT[:, bass.ds(s, 1), qc * TPC:(qc + 1) * TPC].rearrange("p g j h d -> p (g j) h d"),
                        x[:, :, :, 0:dk], rz[:][:, :, :, None].to_broadcast([P, TPC, HG, dk]), ALU.mult).then_inc(s_xfree, xfree.one())

                def cut_shift(s, half, p):
                    eng.wait_ge(s_ct, ct.add())
                    eng.tensor_scalar(negf[:], psX[0:HG * TPB, 0:P], -1.0, None, ALU.mult).then_inc(s_xfree, xfree.one())
                    if not isinstance(s, int) or s >= 1:
                        eng.wait_ge(s_shift[1 - p], (half + p) * 48)
                    if xfree.past():
                        eng.wait_ge(s_xfree, xfree.value())
                    eng.tensor_copy(shift[:, 0, :], negf[:]).then_inc(s_dve, chain.one())
                    eng.wait_ge(s_dve, chain.value())
                    eng.tensor_tensor(rem[:], negf[:], shift[:, 0, :], ALU.subtract).then_inc(s_dve, chain.one())
                    eng.wait_ge(s_dve, chain.value())
                    eng.tensor_copy(shift[:, 1, :], rem[:]).then_inc(s_dve, chain.one())
                    eng.wait_ge(s_dve, chain.value())
                    eng.tensor_tensor(shift[:, 2, :], rem[:], shift[:, 1, :], ALU.subtract).then_inc(s_cs, cs.one())

                def emit(s, half, p):
                    for x in range(NX):
                        if has_max(s):
                            for m in range(starts[x], starts[x] + lots[x]):
                                reduce(m)
                            if starts[x] + lots[x] == NM and (x == 0 or starts[x - 1] + lots[x - 1] < NM):
                                if red.past():
                                    eng.wait_ge(s_red, red.value())
                                if KC == 2:
                                    eng.tensor_tensor(rowmax1[:].rearrange("p (h b) -> p h b", h=HG),
                                                             rowmax[:, :, :, 0], rowmax[:, :, :, 1], ALU.max).then_inc(s_cm, cm.one())
                                else:
                                    eng.tensor_copy(rowmax1[:].rearrange("p (h b) -> p h b", h=HG), rowmax[:, :, :, 0]).then_inc(s_cm, cm.one())
                        if late(s) and x == min(1, NX - 1):
                            normalise(s - 2, 1)
                        if has_exp(s) and x == min(qc0_end + 2, NX - 1):
                            normalise(s - 1, 0)
                        if has_max(s) and x == ct_at:
                            cut_shift(s, half, p)

                run_steps(eng, [mm, red, chain, cm, ct, cs, tom, xfree], emit, NG + 1, 2)
                normalise(NG - 1, 1)



def gather_heads(eng, c, G, dk, out, half, p):
    src = c.ATT[:].rearrange("p (g j r) -> p g j r", g=BATCH * G, j=TPB)
    return eng.activation(out.rearrange("p j (g r) -> p g j r", g=G),
                          src[:, bass.ds(half * G, G), p * TPC:(p + 1) * TPC, :], ACT.Identity)


def output(nc, c, L, store=None):
    name, G, dk, nested = L["name"] + "o", L["heads"] // HG, L["dk"], L.get("double")
    with ExitStack() as ctx:
        sb = lambda n, s, d=F32: ctx.enter_context(nc.sbuf_tensor(f"{name}_{n}", s, d))
        ps = lambda n, s: ctx.enter_context(nc.psum_tensor(f"{name}_{n}", s, F32))
        sem = ctx.enter_context(semaphores(nc, name))
        heads, headsT, add = sb("heads", [P, 2, TPC, D]), sb("headsT", [P, 2, CHUNK]), sb("add", [P, 2, TPC, D])
        psT, psO = ps("psT", [P, 2, CHUNK]), ps("psO", [P, 2, CHUNK])
        s_h, s_T, s_hT, s_o, s_add, s_dve, s_out, s_tick = (
            sem(n) for n in ("h", "T", "hT", "o", "add", "dve", "out", "tick"))
        with nc.Block() as block:
            @block.scalar
            def _(eng):
                h, T, hT, o = (Tally(s) for s in (s_h, s_T, s_hT, s_o))

                def emit(s, half, p):
                    if not isinstance(s, int) or s < CHUNKS:
                        if T.past():
                            eng.wait_ge(s_T, T.value())
                        gather_heads(eng, c, G, dk, heads[:, p], half, p).then_inc(s_h, h.one())
                    if not isinstance(s, int) or s >= 1:
                        eng.wait_ge(s_T, T.add())
                        if o.past(1):
                            eng.wait_ge(s_o, o.value(1))
                        o.add()
                        if nested:
                            for k in range(2):
                                ins = eng.activation(headsT[:, 1 - p, k * 256:(k + 1) * 256], psT[:, 1 - p, k * 256:(k + 1) * 256],
                                                     ACT.Identity, scale=c.width[:, 2 * (1 - p) + k:2 * (1 - p) + k + 1])
                        else:
                            ins = eng.copy(headsT[:, 1 - p, :], psT[:, 1 - p, :])
                        ins.then_inc(s_hT, hT.one())

                run_steps(eng, [h, T, hT, o], emit, CHUNKS + 1, 2)

            @block.tensor
            def _(eng):
                h, T, hT, o, added = (Tally(s) for s in (s_h, s_T, s_hT, s_o, s_add))

                def emit(s, half, p):
                    eng.wait_ge(s_h, h.add())
                    if hT.past(1):
                        eng.wait_ge(s_hT, hT.value(1))
                    for j in range(TPC):
                        ins = eng.transpose(psT[:, p, j * P:(j + 1) * P], heads[:, p, j, :], c.ident[:])
                    ins.then_inc(s_T, T.one())
                    eng.wait_ge(s_hT, hT.add())
                    if added.past(1):
                        eng.wait_ge(s_add, added.value(1))
                    added.add()
                    for j in range(TPC):
                        ins = eng.matmul(psO[:, p, j * P:(j + 1) * P], headsT[:, p, j * P:(j + 1) * P], L["wo"],
                                         start=True, stop=True)
                    ins.then_inc(s_o, o.one())

                run_steps(eng, [h, T, hT, o, added], emit, CHUNKS, 1)

            @block.vector
            def _(eng):
                o, added, chain = Tally(s_o), Tally(s_add), Tally(s_dve)

                def emit(s, half, p):
                    eng.wait_ge(s_o, o.add())
                    x = c.X[:, bass.ds(s * TPC, TPC), :]
                    t, v = add[:, p], psO[:, p, :].rearrange("p (j d) -> p j d", j=TPC)
                    if "bo" in L:
                        eng.tensor_tensor(t, v, L["bo"][:, None, :].to_broadcast([P, TPC, D]), ALU.add).then_inc(s_add, added.one())
                        eng.wait_ge(s_add, added.value())
                        if nested:
                            cols = c.columns[:, p * TPC:(p + 1) * TPC, :]
                            eng.tensor_tensor(t, t, cols, ALU.mult).then_inc(s_dve, chain.one())
                            eng.wait_ge(s_dve, chain.value())
                            eng.tensor_tensor(t, t, c.Y[:, bass.ds(s * TPC, TPC), :], ALU.add).then_inc(s_dve, chain.one())
                            eng.wait_ge(s_dve, chain.value())
                        eng.tensor_tensor(x, x, t, ALU.add).then_inc(s_dve, chain.one())
                    else:
                        eng.tensor_tensor(x, x, v, ALU.add).then_inc(s_add, added.one())

                run_steps(eng, [o, added, chain], emit, CHUNKS, 1)


def experts_output(nc, c, L):
    name, G, dk = L["name"] + "o", L["heads"] // HG, L["dk"]
    NE, NF = 4, 4
    with ExitStack() as ctx:
        sb = lambda n, s, d=F32: ctx.enter_context(nc.sbuf_tensor(f"{name}_{n}", s, d))
        ps = lambda n, s: ctx.enter_context(nc.psum_tensor(f"{name}_{n}", s, F32))
        sem = ctx.enter_context(semaphores(nc, name))
        heads, headsT = sb("heads", [P, 2, TPC, D]), sb("headsT", [P, CHUNK])
        x1, x1T, hid = sb("x1", [P, 2, TPC, D]), sb("x1T", [P, 2, CHUNK]), sb("hid", [P, 2, NF, CHUNK])
        stats, mv, rs, tmp = sb("stats", [P, TPC, 6]), sb("mv", [P, TPC, 2]), sb("rs", [P, TPC]), sb("tmp", [P, TPC])
        acc, bias_y = sb("acc", [P, TPC, D]), sb("bias_y", [P, NE, D])
        chosen = sb("chosen", [P, 2, TPC, NE])
        key, whole, over = sb("key", [P, TPC]), sb("whole", [P, TPC]), sb("over", [P, TPC])
        whole_i, index = sb("whole_i", [P, TPC], I32), sb("index", [P, TPC])
        psT, psO, psH, psY = ps("psT", [P, CHUNK]), ps("psO", [P, CHUNK]), ps("psH", [P, 2, CHUNK]), ps("psY", [P, TPC, NE * D])
        s_h, s_T, s_hT, s_o, s_var, s_rstd, s_x1, s_x1t, s_x1T, s_key, s_chosen = (
            sem(n) for n in ("h", "T", "hT", "o", "var", "rstd", "x1", "x1t", "x1T", "key", "chosen"))
        s_up, s_relu, s_down, s_y, s_comb, s_dve, s_pool, tick, tickp = (
            sem(n) for n in ("up", "relu", "down", "y", "comb", "dve", "pool", "tick", "tickp"))
        has_pre = lambda s: not isinstance(s, int) or s < CHUNKS
        has_post = lambda s: not isinstance(s, int) or s >= 1

        with nc.Block() as block:
            @block.scalar
            def _(eng):
                h, T, hT, up, relu, down, x1t, x1T_ = (
                    Tally(s) for s in (s_h, s_T, s_hT, s_up, s_relu, s_down, s_x1t, s_x1T))
                gather_heads(eng, c, G, dk, heads[:, 0], 0, 0).then_inc(s_h, h.one())

                def emit(s, half, p):
                    if has_pre(s):
                        eng.wait_ge(s_T, T.add())
                        eng.copy(headsT[:], psT[:]).then_inc(s_hT, hT.one())
                    if has_post(s):
                        for e in range(NE):
                            if down.past(1):
                                eng.wait_ge(s_down, down.value(1))
                            down.add()
                            for f in range(NF):
                                eng.wait_ge(s_up, up.add())
                                eng.activation(hid[:, e % 2, f, :], psH[:, f % 2, :], ACT.Relu,
                                                      bias=c.b1[:, e * NF + f:e * NF + f + 1]).then_inc(s_relu, relu.one())
                    if not isinstance(s, int) or s + 1 < CHUNKS:
                        gather_heads(eng, c, G, dk, heads[:, 1 - p], half + p, 1 - p).then_inc(s_h, h.one())
                    if has_pre(s):
                        eng.wait_ge(s_x1t, x1t.add())
                        eng.copy(x1T[:, p, :], psT[:]).then_inc(s_x1T, x1T_.one())

                run_steps(eng, [h, T, hT, up, relu, down, x1t, x1T_], emit, CHUNKS + 1, 2)

            @block.gpsimd
            def _(eng):
                var, chain, rstd = Tally(s_var), Tally(s_pool), Tally(s_rstd)

                def emit(s, half, p):
                    for _ in range(has_pre(s) + has_post(s)):
                        eng.wait_ge(s_var, var.add())
                        hold(eng, tickp)
                        eng.tensor_scalar(tmp[:], mv[:, :, 1], EPS, None, ALU.add).then_inc(s_pool, chain.one())
                        eng.wait_ge(s_pool, chain.value())
                        eng.tensor_tensor(rs[:], tmp[:], c.minus_half[:, 0:TPC], ALU.pow).then_inc(s_rstd, rstd.one())

                run_steps(eng, [var, chain, rstd], emit, CHUNKS + 1, 2)

            @block.tensor
            def _(eng):
                h, T, hT, o, x1_, x1t, x1T_, key_, chosen_ = (
                    Tally(s) for s in (s_h, s_T, s_hT, s_o, s_x1, s_x1t, s_x1T, s_key, s_chosen))
                up, relu, down, y, comb = (Tally(s) for s in (s_up, s_relu, s_down, s_y, s_comb))

                def hidden(e, p):
                    for f in range(NF):
                        if relu.past(1):
                            eng.wait_ge(s_relu, relu.value(1))
                        relu.add()
                        eng.matmul(psH[:, f % 2, :], c.W1[:, e, f * P:(f + 1) * P], x1T[:, p, :],
                                          start=True, stop=True).then_inc(s_up, up.one())

                def out_of(e, done):
                    eng.wait_ge(s_relu, done)
                    if e == 0:
                        if comb.past():
                            eng.wait_ge(s_comb, comb.value())
                        comb.add()
                    for j in range(TPC):
                        for f in range(NF):
                            ins = eng.matmul(psY[:, j, e * D:(e + 1) * D], hid[:, e % 2, f, j * P:(j + 1) * P],
                                             c.W2[:, e, f, :], start=f == 0, stop=f == NF - 1)
                        if e == NE - 1 and j < TPC - 1:
                            ins.then_inc(s_y, y.one())
                    ins.then_inc(s_down, down.one())

                def emit(s, half, p):
                    if has_pre(s):
                        eng.wait_ge(s_h, h.add())
                        if x1T_.past():
                            eng.wait_ge(s_x1T, x1T_.value())
                        for j in range(TPC):
                            ins = eng.transpose(psT[:, j * P:(j + 1) * P], heads[:, p, j, :], c.ident[:])
                        ins.then_inc(s_T, T.one())
                        eng.wait_ge(s_hT, hT.add())
                        if chosen_.past():
                            eng.wait_ge(s_chosen, chosen_.value())
                        chosen_.add()
                        for j in range(TPC):
                            ins = eng.matmul(psO[:, j * P:(j + 1) * P], headsT[:, j * P:(j + 1) * P], L["wo"],
                                             start=True, stop=True)
                        ins.then_inc(s_o, o.one())
                    if has_post(s):
                        for e in range(NE):
                            hidden(e, 1 - p)
                            if e:
                                out_of(e - 1, relu.value(NF))
                        out_of(NE - 1, relu.value())
                    if has_pre(s):
                        eng.wait_ge(s_x1, x1_.add())
                        for j in range(TPC):
                            ins = eng.transpose(psT[:, j * P:(j + 1) * P], x1[:, p, j, :], c.ident[:])
                        ins.then_inc(s_x1t, x1t.one())
                        eng.wait_ge(s_x1T, x1T_.add())
                        for j in range(TPC):
                            ins = eng.matmul(psO[:, j:j + 1], x1T[:, p, j * P:(j + 1) * P], c.router_w[:, 0:1],
                                             start=True, stop=True)
                        ins.then_inc(s_key, key_.one())

                run_steps(eng, [h, T, hT, o, x1_, x1t, x1T_, key_, chosen_, up, relu, down, y, comb],
                          emit, CHUNKS + 1, 2)

            @block.vector
            def _(eng):
                o, var, rstd, x1_, key_, chosen_, y, down, comb, chain = (
                    Tally(s) for s in (s_o, s_var, s_rstd, s_x1, s_key, s_chosen, s_y, s_down, s_comb, s_dve))
                tiles = lambda r: r[:, None, :].to_broadcast([P, TPC, D])

                def norm(x, out, gain, shift):
                    for j in range(TPC):
                        eng.bn_stats(stats[:, j, :], x[:, j, :]).then_inc(s_dve, chain.one())
                    eng.wait_ge(s_dve, chain.value())
                    hold(eng, tick)
                    for j in range(TPC):
                        ins = eng.bn_aggr(mv[:, j, :], stats[:, j, :])
                    ins.then_inc(s_var, var.one())
                    eng.wait_ge(s_rstd, rstd.add())
                    for j in range(TPC):
                        ins = eng.tensor_scalar(out[:, j, :], x[:, j, :], mv[:, j, 0:1], rs[:, j:j + 1],
                                                ALU.subtract, ALU.mult)
                    ins.then_inc(s_dve, chain.one())
                    eng.wait_ge(s_dve, chain.value())
                    eng.tensor_tensor(out, out, tiles(gain), ALU.mult).then_inc(s_dve, chain.one())
                    eng.wait_ge(s_dve, chain.value())
                    return eng.tensor_tensor(out, out, tiles(shift), ALU.add)

                def emit(s, half, p):
                    if has_pre(s):
                        eng.wait_ge(s_o, o.add())
                        a = acc[:]
                        eng.tensor_tensor(a, psO[:].rearrange("p (j d) -> p j d", j=TPC), tiles(L["bo"]), ALU.add).then_inc(s_dve, chain.one())
                        eng.wait_ge(s_dve, chain.value())
                        eng.tensor_tensor(a, a, c.Y[:, bass.ds(s * TPC, TPC), :], ALU.add).then_inc(s_dve, chain.one())
                        eng.wait_ge(s_dve, chain.value())
                        norm(a, x1[:, p], c.ln1_g, c.ln1_b).then_inc(s_x1, x1_.one())
                    if has_post(s):
                        down.add(NE - 1)
                        for j in range(TPC):
                            if j < TPC - 1:
                                eng.wait_ge(s_y, y.add())
                            else:
                                eng.wait_ge(s_down, down.add())
                            ins = eng.tensor_tensor(bias_y[:], psY[:, j, :].rearrange("p (e d) -> p e d", e=NE), c.b2, ALU.add)
                            if j == TPC - 1:
                                ins.then_inc(s_comb, comb.one())
                                eng.wait_ge(s_comb, comb.value())
                            else:
                                ins.then_inc(s_dve, chain.one())
                                eng.wait_ge(s_dve, chain.value())
                            eng.tensor_scalar(acc[:, j, :], bias_y[:, 0, :], chosen[:, 1 - p, j, 0:1], None, ALU.mult).then_inc(s_dve, chain.one())
                            eng.wait_ge(s_dve, chain.value())
                            for e in range(1, NE):
                                eng.scalar_tensor_tensor(out=acc[:, j, :], in0=bias_y[:, e, :],
                                                              scalar=chosen[:, 1 - p, j, e:e + 1],
                                                              in1=acc[:, j, :], op0=ALU.mult, op1=ALU.add).then_inc(s_dve, chain.one())
                                eng.wait_ge(s_dve, chain.value())
                        a = acc[:]
                        eng.tensor_tensor(a, a, x1[:, 1 - p], ALU.add).then_inc(s_dve, chain.one())
                        eng.wait_ge(s_dve, chain.value())
                        norm(a, a, c.ln2_g, c.ln2_b).then_inc(s_dve, chain.one())
                        eng.wait_ge(s_dve, chain.value())
                        x = c.X[:, bass.ds((s - 1) * TPC, TPC), :]
                        eng.tensor_tensor(x, x, a, ALU.add).then_inc(s_dve, chain.one())
                        eng.wait_ge(s_dve, chain.value())
                    if has_pre(s):
                        eng.wait_ge(s_key, key_.add())
                        eng.tensor_scalar(key[:], psO[:, 0:TPC], c.router_b[:, 0:1], None, ALU.add).then_inc(s_dve, chain.one())
                        eng.wait_ge(s_dve, chain.value())
                        eng.tensor_copy(whole_i[:], key[:]).then_inc(s_dve, chain.one())
                        eng.wait_ge(s_dve, chain.value())
                        eng.tensor_copy(whole[:], whole_i[:]).then_inc(s_dve, chain.one())
                        eng.wait_ge(s_dve, chain.value())
                        eng.tensor_tensor(over[:], whole[:], key[:], ALU.is_gt).then_inc(s_dve, chain.one())
                        eng.wait_ge(s_dve, chain.value())
                        eng.tensor_tensor(whole[:], whole[:], over[:], ALU.subtract).then_inc(s_dve, chain.one())
                        eng.wait_ge(s_dve, chain.value())
                        eng.tensor_copy(whole_i[:], whole[:]).then_inc(s_dve, chain.one())
                        eng.wait_ge(s_dve, chain.value())
                        eng.tensor_scalar(whole_i[:], whole_i[:], NE - 1, None, ALU.bitwise_and).then_inc(s_dve, chain.one())
                        eng.wait_ge(s_dve, chain.value())
                        eng.tensor_copy(index[:], whole_i[:]).then_inc(s_dve, chain.one())
                        eng.wait_ge(s_dve, chain.value())
                        eng.tensor_tensor(chosen[:, p], index[:][:, :, None].to_broadcast([P, TPC, NE]),
                                                 c.iota[:, None, 0:NE].to_broadcast([P, TPC, NE]), ALU.is_equal).then_inc(s_chosen, chosen_.one())

                run_steps(eng, [o, var, rstd, x1_, key_, chosen_, y, down, comb, chain], emit, CHUNKS + 1, 2)



RMS_EPS = 1.1920929e-07


def causal_columns(nc, c, a):
    NPAIR, KB, QC = 8, TPB, 2
    STEPS = NPAIR * BATCH
    with ExitStack() as ctx:
        sb = lambda n, s, d=F32: ctx.enter_context(nc.sbuf_tensor("aa_" + n, s, d))
        ps = lambda n, s: ctx.enter_context(nc.psum_tensor("aa_" + n, s, F32))
        sem = ctx.enter_context(semaphores(nc, "aa"))
        xT = c.Y[:].rearrange("p t d -> p (t d)")
        Wqkv = c.ATT[:, 0:3 * NPAIR * P].rearrange("p (h m e) -> p h m e", h=NPAIR, m=3)
        Wo = c.V[:, 0:NPAIR * D].rearrange("p (h e) -> p h e", h=NPAIR)
        bv = c.V[:, NPAIR * D:2 * NPAIR * D].rearrange("p (h e) -> p h e", h=NPAIR)
        bqk, nbq, bo = sb("bqk", [P, 2, NPAIR]), sb("nbq", [P, NPAIR]), sb("bo", [P, D])
        stats, mv = sb("stats", [P, TPC, 6]), sb("mv", [P, TPC, 2])
        tmp, rs = sb("tmp", [P, TPC]), sb("rs", [P, 2, TPC])
        xn = sb("xn", [P, 2, TPC, D])
        s_w, s_const, ticka = sem("weights"), sem("const"), sem("ticka")

        with ExitStack() as c2:
            psT = c2.enter_context(nc.psum_tensor("aa_psT", [P, 2, CHUNK], F32))
            s_var, s_rstd, s_xn, s_T, s_xT, s_dve, s_pool, tick, tickp = (
                sem(n) for n in ("var", "rstd", "xn", "T", "xT", "dve", "pool", "tick", "tickp"))
            with nc.Block() as block:
                @block.sync
                def _(eng):
                    eng.dma_start(bo[:], a["aa_bo"]).then_inc(s_w, 16)
                    eng.dma_start(bqk[:], a["aa_bqk"]).then_inc(s_w, 16)
                    eng.dma_start(Wqkv, a["aa_Wqkv"]).then_inc(s_w, 16)
                    eng.dma_start(Wo, a["aa_Wo"]).then_inc(s_w, 16)
                    eng.dma_start(bv, a["aa_bv"]).then_inc(s_w, 16)

                @block.vector
                def _(eng):
                    chain, var, rstd, xn_, T = (Tally(s) for s in (s_dve, s_var, s_rstd, s_xn, s_T))
                    eng.wait_ge(s_w, 5 * 16)
                    eng.tensor_scalar(nbq[:], bqk[:, 0, :], -1.0, None, ALU.mult).then_inc(s_const, 1)

                    def emit(s, half, p):
                        for j in range(TPC):
                            eng.bn_stats(stats[:, j, :], c.X[:, s * TPC + j, :]).then_inc(s_dve, chain.one())
                        eng.wait_ge(s_dve, chain.value())
                        hold(eng, tick)
                        for j in range(TPC):
                            ins = eng.bn_aggr(mv[:, j, :], stats[:, j, :])
                        ins.then_inc(s_var, var.one())
                        eng.wait_ge(s_rstd, rstd.add())
                        if T.past():
                            eng.wait_ge(s_T, T.value())
                        if not isinstance(s, int) or s >= 1:
                            T.add()
                        for j in range(TPC):
                            ins = eng.tensor_scalar(xn[:, p, j, :], c.X[:, s * TPC + j, :], mv[:, j, 0:1],
                                                    rs[:, 1, j:j + 1], ALU.subtract, ALU.mult)
                        ins.then_inc(s_xn, xn_.one())
                        eng.wait_ge(s_xn, xn_.value())
                        x = c.X[:, bass.ds(s * TPC, TPC), :]
                        eng.tensor_tensor(x, x, bo[:, None, :].to_broadcast([P, TPC, D]), ALU.add).then_inc(s_dve, chain.one())

                    run_steps(eng, [chain, var, rstd, xn_, T], emit, CHUNKS, 1)
                    if chain.past():
                        eng.wait_ge(s_dve, chain.value())

                @block.gpsimd
                def _(eng):
                    var, chain, rstd = Tally(s_var), Tally(s_pool), Tally(s_rstd)

                    def emit(s, half, p):
                        eng.wait_ge(s_var, var.add())
                        hold(eng, tickp)
                        eng.tensor_scalar(tmp[:], mv[:, :, 1], EPS, None, ALU.add).then_inc(s_pool, chain.one())
                        eng.wait_ge(s_pool, chain.value())
                        eng.tensor_tensor(rs[:, 0, :], tmp[:], c.minus_half[:, 0:TPC], ALU.pow).then_inc(s_pool, chain.one())
                        eng.wait_ge(s_pool, chain.value())
                        eng.tensor_tensor(tmp[:], mv[:, :, 1], rs[:, 0, :], ALU.mult).then_inc(s_pool, chain.one())
                        eng.wait_ge(s_pool, chain.value())
                        eng.tensor_tensor(tmp[:], tmp[:], rs[:, 0, :], ALU.mult).then_inc(s_pool, chain.one())
                        eng.wait_ge(s_pool, chain.value())
                        hold(eng, tickp)
                        eng.tensor_scalar(tmp[:], tmp[:], RMS_EPS, None, ALU.add).then_inc(s_pool, chain.one())
                        eng.wait_ge(s_pool, chain.value())
                        eng.tensor_tensor(rs[:, 1, :], tmp[:], c.minus_half[:, 0:TPC], ALU.pow).then_inc(s_pool, chain.one())
                        eng.wait_ge(s_pool, chain.value())
                        eng.tensor_tensor(rs[:, 1, :], rs[:, 1, :], rs[:, 0, :], ALU.mult).then_inc(s_rstd, rstd.one())

                    run_steps(eng, [var, chain, rstd], emit, CHUNKS, 1)

                @block.tensor
                def _(eng):
                    xn_, T, xT_ = (Tally(s) for s in (s_xn, s_T, s_xT))

                    def emit(s, half, p):
                        eng.wait_ge(s_xn, xn_.add())
                        if xT_.past(1):
                            eng.wait_ge(s_xT, xT_.value(1))
                        xT_.add()
                        for j in range(TPC):
                            ins = eng.transpose(psT[:, p, j * P:(j + 1) * P], xn[:, p, j, :], c.ident[:])
                        ins.then_inc(s_T, T.one())

                    run_steps(eng, [xn_, T, xT_], emit, CHUNKS, 1)

                @block.scalar
                def _(eng):
                    T, xT_ = Tally(s_T), Tally(s_xT)

                    def emit(s, half, p):
                        eng.wait_ge(s_T, T.add())
                        hold(eng, ticka)
                        eng.activation(xT[:, bass.ds(s * CHUNK, CHUNK)], psT[:, p, :], ACT.Identity).then_inc(s_xT, xT_.one())

                    run_steps(eng, [T, xT_], emit, CHUNKS, 1)

        q, k = sb("q", [P, 2, SEQ]), sb("k", [P, 2, 2, SEQ])
        v, vz = sb("v", [P, 2, KB, P]), sb("vz", [P, 2, P])
        E, zT = sb("E", [P, 2, 2, SEQ]), sb("zT", [P, 2, SEQ])
        w = sb("w", [P, 3, P])
        least, total, rz = sb("least", [P, 2 * KB]), sb("total", [P, 2 * KB]), sb("rz", [P, 2 * KB])
        psS, psZ, psW = ps("psS", [P, 2, SEQ]), ps("psZ", [P, SEQ]), ps("psW", [P, 2, CHUNK])
        s_set, s_wst, s_S, s_min, s_exp, s_rz, s_vz, s_ev, s_zT = (
            sem(n) for n in ("set", "wst", "S", "min", "exp", "rz", "vz", "ev", "zT"))
        s_qk, s_qkout, s_v, s_vout, s_o, s_oout, tickq = (
            sem(n) for n in ("qk", "qkout", "v", "vout", "o", "oout", "tickq"))
        SLOTS = [["o0"], ["o1", "q0"], ["q1"], ["k0"], ["k1"], ["v0"], ["v1"], []]
        chunks = lambda kb: [(max(kb * P, qc * CHUNK), (qc + 1) * CHUNK, qc) for qc in range(QC) if kb * P < (qc + 1) * CHUNK]
        more = lambda s: not isinstance(s, int) or s + 1 < STEPS
        later = lambda s: not isinstance(s, int) or s >= 1
        nxt = lambda pair, b: (pair + 1, 0) if b == BATCH - 1 else (pair, b + 1)
        prv = lambda pair, b: (pair - 1, BATCH - 1) if b == 0 else (pair, b - 1)

        with nc.Block() as block:
            @block.gpsimd
            def _(eng):
                eng.memset(k[:].rearrange("p u h n -> p (u h n)"), 0.0).then_inc(s_set, 1)
                eng.tensor_copy(w[:], Wqkv[:, 0]).then_inc(s_wst, 1)
                with eng.Fori(0, NPAIR - 1) as i:
                    eng.wait_ge(s_v, i * (2 * BATCH) + 2 * BATCH)
                    hold(eng, tickq)
                    eng.tensor_copy(w[:], Wqkv[:, bass.ds(i + 1, 1)].rearrange("p h m e -> p (h m) e")).then_inc(s_wst, 1)

            @block.tensor
            def _(eng):
                S, ex, vz_, ev, zT_ = (Tally(s) for s in (s_S, s_exp, s_vz, s_ev, s_zT))
                qk, qkout, v_, vout, o, oout = (Tally(s) for s in (s_qk, s_qkout, s_v, s_vout, s_o, s_oout))

                def fill(what, pair, b, p, outs_before=False):
                    kind, n = what[0], int(what[1])
                    bank = psW[:, n, :]
                    if kind == "q" and outs_before:
                        eng.wait_ge(s_oout, oout.add())
                    if kind in "kv":
                        eng.wait_ge(s_qkout, qkout.add())
                    if kind in "qk":
                        x = xT[:, b * SEQ + n * CHUNK:b * SEQ + (n + 1) * CHUNK]
                        eng.matmul(bank, w[:, "qk".index(kind), :], x, start=True, stop=True).then_inc(s_qk, qk.one())
                    elif kind == "v":
                        for j in range(TPC):
                            t = b * SEQ + n * CHUNK + j * P
                            ins = eng.matmul(bank[:, j * P:(j + 1) * P], xT[:, t:t + P], w[:, 2, :], start=True, stop=True)
                        ins.then_inc(s_v, v_.one())
                    else:
                        for j in range(TPC):
                            t = n * CHUNK + j * P
                            ins = eng.matmul(bank[:, j * P:(j + 1) * P], zT[:, p, t:t + P], Wo[:, pair, :], start=True, stop=True)
                        ins.then_inc(s_o, o.one())

                def out_product(what, pair, b, p):
                    if what == "o0":
                        eng.wait_ge(s_zT, zT_.add())
                    fill(what, pair, b, p)

                def score(kb, h, p, t):
                    if ex.past(1):
                        eng.wait_ge(s_exp, ex.value(1))
                    ex.add()
                    for a0, a1, qc in chunks(kb):
                        diag = a0 == kb * P
                        ins = eng.matmul(psS[:, t % 2, a0:a1], k[:, p, h, kb * P:(kb + 1) * P], q[:, p, a0:a1],
                                         start=True, stop=not diag)
                        if diag:
                            ins = eng.matmul(psS[:, t % 2, a0:a0 + P], c.ident_bf[:], c.mask_columns, start=False, stop=True)
                    ins.then_inc(s_S, S.one())

                def value(kb):
                    eng.wait_ge(s_vz, vz_.add(2))
                    if kb == 0:
                        if zT_.past():
                            eng.wait_ge(s_zT, zT_.value())
                    for a0, a1, qc in chunks(kb):
                        for h in range(2):
                            ins = eng.matmul(psZ[64 * h:64 * h + 64, a0:a1], vz[:, kb % 2, 64 * h:64 * h + 64],
                                             E[:, kb % 2, h, a0:a1], start=kb == 0, stop=kb == 4 * qc + 3)
                    ins.then_inc(s_ev, ev.one())

                def emit(s, pair, b):
                    p = b % 2
                    for kb in range(KB):
                        if kb == 0:
                            eng.wait_ge(s_vout, v_.value())
                        for h in range(2):
                            score(kb, h, p, h)
                        for what in SLOTS[kb]:
                            if what[0] == "o":
                                if later(s):
                                    out_product(what, *prv(pair, b), 1 - p)
                                continue
                            if more(s):
                                n_pair, n_b = nxt(pair, b)
                                if what == "q0" and n_b == 0:
                                    eng.wait_ge(s_wst, n_pair + 1)
                                fill(what, n_pair, n_b, 1 - p, later(s))
                        if kb:
                            value(kb - 1)
                    value(KB - 1)

                eng.wait_ge(s_wst, 1)
                for what in ("q0", "q1", "k0", "k1", "v0", "v1"):
                    fill(what, 0, 0, 0)
                run_steps(eng, [S, ex, vz_, ev, zT_, qk, qkout, v_, vout, o, oout], emit, STEPS, 1, unroll=BATCH)
                eng.wait_ge(s_oout, 2 * (STEPS - 1))
                for what in ("o0", "o1"):
                    out_product(what, *prv(NPAIR, 0), (STEPS - 1) % 2)

            @block.scalar
            def _(eng):
                mn, ex, ev, zT_, o, qk, qkout = (Tally(s) for s in (s_min, s_exp, s_ev, s_zT, s_o, s_qk, s_qkout))

                def take(what, pair, p):
                    kind, n = what[0], int(what[1])
                    eng.wait_ge(s_qk, qk.add())
                    hold(eng, ticka)
                    cols = slice(n * CHUNK, (n + 1) * CHUNK)
                    if kind == "q":
                        eng.activation(q[:, p, cols], psW[:, n, :], ACT.Identity, scale=-1.0,
                                              bias=nbq[:, bass.ds(pair, 1)]).then_inc(s_qkout, qkout.one())
                    else:
                        for h in range(2):
                            r = slice(64 * h, 64 * h + 64)
                            ins = eng.activation(k[r, p, h, cols], psW[r, n, :], ACT.Identity,
                                                 bias=bqk[r, 1, bass.ds(pair, 1)])
                        ins.then_inc(s_qkout, qkout.one())

                def emit(s, pair, b):
                    p = b % 2
                    for kb in range(KB):
                        if ev.past(1):
                            eng.wait_ge(s_ev, ev.value(1))
                        ev.add()
                        for h in range(2):
                            t = 2 * kb + h
                            eng.wait_ge(s_min, mn.add())
                            eng.activation(E[:, kb % 2, h, kb * P:SEQ], psS[:, h, kb * P:SEQ], ACT.Exp,
                                                  bias=least[:, t:t + 1], scale=-1.0, accum_out=total[:, t:t + 1]).then_inc(s_exp, ex.one())
                        for what in SLOTS[kb]:
                            if what[0] in "qk" and more(s):
                                n_pair, n_b = nxt(pair, b)
                                take(what, n_pair, 1 - p)
                    if ev.past():
                        eng.wait_ge(s_ev, ev.value())
                    if o.past(2):
                        eng.wait_ge(s_o, o.value(2))
                    if later(s):
                        o.add(2)
                    eng.copy(zT[:, p, :], psZ[:]).then_inc(s_zT, zT_.one())

                eng.wait_ge(s_set, 1)
                for what in ("q0", "q1", "k0", "k1"):
                    take(what, 0, 0)
                run_steps(eng, [mn, ex, ev, zT_, o, qk, qkout], emit, STEPS, 1, unroll=BATCH)

            @block.vector
            def _(eng):
                S, mn, ex, rz_, vz_, ev = (Tally(s) for s in (s_S, s_min, s_exp, s_rz, s_vz, s_ev))
                v_, vout, o, oout = (Tally(s) for s in (s_v, s_vout, s_o, s_oout))

                def minimum(kb, h):
                    eng.wait_ge(s_S, S.add())
                    t = 2 * kb + h
                    eng.tensor_reduce(least[:, t:t + 1], psS[:, h, kb * P:SEQ], AX_X, ALU.min).then_inc(s_min, mn.one())

                def scale_v(kb, h, p):
                    t = 2 * kb + h
                    eng.wait_ge(s_exp, ex.add())
                    eng.reciprocal(rz[:, t:t + 1], total[:, t:t + 1]).then_inc(s_rz, rz_.one())
                    eng.wait_ge(s_rz, rz_.value())
                    if h == 0:
                        if ev.past(1):
                            eng.wait_ge(s_ev, ev.value(1))
                        ev.add()
                    r = slice(64 * h, 64 * h + 64)
                    eng.tensor_scalar(vz[:, kb % 2, r], v[:, p, kb, r], rz[:, t:t + 1], None, ALU.mult).then_inc(s_vz, vz_.one())

                def take_v(n, pair, p):
                    eng.wait_ge(s_v, v_.add())
                    eng.tensor_tensor(v[:, p, n * TPC:(n + 1) * TPC, :], psW[:, n, :].rearrange("p (j e) -> p j e", j=TPC),
                                             bv[:, bass.ds(pair, 1), :].to_broadcast([P, TPC, P]), ALU.add).then_inc(s_vout, vout.one())

                def add_out(n, b):
                    eng.wait_ge(s_o, o.add())
                    x = c.X[:, b * TPB + n * TPC:b * TPB + (n + 1) * TPC, :]
                    eng.tensor_tensor(x, x, psW[:, n, :].rearrange("p (j d) -> p j d", j=TPC), ALU.add).then_inc(s_oout, oout.one())

                def emit(s, pair, b):
                    p = b % 2
                    for kb in range(KB):
                        minimum(kb, 0)
                        if kb:
                            scale_v(kb - 1, 1, p)
                        minimum(kb, 1)
                        scale_v(kb, 0, p)
                        for what in SLOTS[kb]:
                            if what[0] == "o" and later(s):
                                add_out(int(what[1]), prv(pair, b)[1])
                            if what[0] == "v" and more(s):
                                take_v(int(what[1]), nxt(pair, b)[0], 1 - p)
                    scale_v(KB - 1, 1, p)

                for n in range(2):
                    take_v(n, 0, 0)
                run_steps(eng, [S, mn, ex, rz_, vz_, ev, v_, vout, o, oout], emit, STEPS, 1, unroll=BATCH)
                for n in range(2):
                    add_out(n, BATCH - 1)



def iterated(nc, c, a):
    NT, H, HD, IT = 16, 16, 8, 3
    R = BATCH * NT
    COUNT = float(BATCH * H * SEQ * HD)
    THRESH, FACTOR = 0.01, 0.1
    with ExitStack() as ctx:
        sb = lambda n, s, d=F32: ctx.enter_context(nc.sbuf_tensor("la_" + n, s, d))
        ps = lambda n, s: ctx.enter_context(nc.psum_tensor("la_" + n, s, F32))
        sem = ctx.enter_context(semaphores(nc, "la"))
        xs, xn, va, vb_ = sb("xs", [R, D]), sb("xn", [R, D]), sb("va", [R, D]), sb("vb_", [R, D])
        stats, mv, rs, tmp = sb("stats", [R, 6]), sb("mv", [R, 2]), sb("rs", [R, 2]), sb("tmp", [R, H])
        turn_in, turnedT = sb("turn_in", [R, 3, D]), sb("turnedT", [P, 3, R])
        qcur, lin, cen, sq, inv = sb("qcur", [R, D]), sb("lin", [R, D]), sb("cen", [R, D]), sb("sq", [R, D]), sb("inv", [R, H])
        mean, kn, vi, qn = sb("mean", [R, H]), sb("kn", [R, D]), sb("vi", [R, D]), sb("qn", [R, D])
        knB, viB, prod = sb("knB", [R, NT, D]), sb("viB", [R, NT, D]), sb("prod", [R, NT, D])
        logit, top, expo, den = sb("logit", [R, NT, H]), sb("top", [R, H]), sb("expo", [R, NT, H]), sb("den", [R, H])
        outs = sb("outs", [R, IT, D])
        spread, ones, dif = sb("spread", [R, NT, R]), sb("ones", [R, R]), sb("dif", [R, 4])
        psA, psB = ps("psA", [P, CHUNK]), ps("psB", [R, NT, D])
        s_load, s_dve, s_act, s_pool, s_pe, s_back, tick, tickp = (
            sem(n) for n in ("load", "dve", "act", "pool", "pe", "back", "tick", "tickp"))
        s_turn, s_root, s_expo = sem("turn"), sem("root"), sem("expo")
        m = c.mat
        heads = lambda t: t.rearrange("p (h d) -> p h d", h=H)
        over_d = lambda t: t[:, :, None].to_broadcast([R, H, HD])

        with nc.Block() as block:
            @block.sync
            def _(eng):
                for b in range(BATCH):
                    eng.dma_start(xs[b * NT:(b + 1) * NT, :], c.X[0:NT, b * TPB, :]).then_inc(s_load, 16)
                eng.dma_start(spread[:], a["spread"]).then_inc(s_load, 16)
                eng.wait_ge(s_back, 1)
                for b in range(BATCH):
                    eng.dma_start(c.X[0:NT, b * TPB, :], xs[b * NT:(b + 1) * NT, :]).then_inc(s_load, 16)
                eng.wait_ge(s_load, 9 * 16)

            @block.gpsimd
            def _(eng):
                asked, chain = Tally(s_root), Tally(s_pool)

                def root(out, source, width):
                    eng.tensor_scalar(tmp[:, 0:width], source, EPS, None, ALU.add).then_inc(s_pool, chain.one())
                    eng.wait_ge(s_pool, chain.value())
                    return eng.tensor_tensor(out, tmp[:, 0:width], c.minus_half[0:R, 0:width], ALU.pow)

                eng.wait_ge(s_root, asked.add())
                root(rs[:, 0:1], mv[:, 1:2], 1).then_inc(s_pool, chain.one())
                eng.wait_ge(s_pool, chain.value())
                eng.tensor_tensor(mv[:, 1:2], mv[:, 1:2], rs[:, 0:1], ALU.mult).then_inc(s_pool, chain.one())
                eng.wait_ge(s_pool, chain.value())
                eng.tensor_tensor(mv[:, 1:2], mv[:, 1:2], rs[:, 0:1], ALU.mult).then_inc(s_pool, chain.one())
                eng.wait_ge(s_pool, chain.value())
                root(rs[:, 1:2], mv[:, 1:2], 1).then_inc(s_pool, chain.one())
                eng.wait_ge(s_pool, chain.value())
                eng.tensor_tensor(rs[:, 1:2], rs[:, 1:2], rs[:, 0:1], ALU.mult).then_inc(s_pool, chain.one())
                eng.wait_ge(s_pool, chain.value())
                for _ in range(1 + IT):
                    eng.wait_ge(s_root, asked.add())
                    root(inv[:], mean[:], H).then_inc(s_pool, chain.one())
                    eng.wait_ge(s_pool, chain.value())

            @block.scalar
            def _(eng):
                asked, done = Tally(s_expo), Tally(s_act)
                for _ in range(IT):
                    eng.wait_ge(s_expo, asked.add())
                    eng.activation(expo[:], logit[:], ACT.Exp, scale=HD ** -0.5).then_inc(s_act, done.one())

            @block.tensor
            def _(eng):
                asked, done = Tally(s_turn), Tally(s_pe)

                def turn(n):
                    eng.wait_ge(s_turn, asked.add())
                    for i in range(n):
                        ins = eng.transpose(psA[:, i * R:(i + 1) * R], turn_in[:, i, :], c.ident[0:R, 0:R])
                    ins.then_inc(s_pe, done.one())

                def product(weights):
                    eng.wait_ge(s_turn, asked.add())
                    for i, wt in enumerate(weights):
                        ins = eng.matmul(psA[0:R, i * D:(i + 1) * D], turnedT[:, i, :], wt, start=True, stop=True)
                    ins.then_inc(s_pe, done.one())

                def spread_rows(x):
                    eng.wait_ge(s_turn, asked.add())
                    for t in range(NT):
                        ins = eng.matmul(psB[:, t, :], spread[:, t, :], x[:], start=True, stop=True)
                    ins.then_inc(s_pe, done.one())

                turn(2)
                product([m["la_wq"]])
                eng.wait_ge(s_turn, asked.add())
                for i, n in enumerate(("la_wk", "la_wv")):
                    ins = eng.matmul(psA[0:R, i * D:(i + 1) * D], turnedT[:, 1, :], m[n], start=True, stop=True)
                ins.then_inc(s_pe, done.one())
                turn(3)
                product([m["la_lq"], m["la_lk"], m["la_lv"]])
                spread_rows(kn)
                spread_rows(vi)
                for it in range(IT):
                    if it:
                        turn(1)
                        product([m["la_lq"]])
                eng.wait_ge(s_turn, asked.add())
                eng.matmul(psA[0:R, 0:1], ones[:], dif[:, 0:1], start=True, stop=True).then_inc(s_pe, done.one())
                turn(1)
                product([m["la_wo"]])

            @block.vector
            def _(eng):
                chain, pe, pool, act = Tally(s_dve), Tally(s_pe), Tally(s_pool), Tally(s_act)
                ask_pe, ask_root, ask_exp = Tally(s_turn), Tally(s_root), Tally(s_expo)

                def nudge(tally):
                    eng.tensor_copy(dif[:, 3:4], dif[:, 2:3]).then_inc(tally.sem, tally.one())
                    if tally.past():
                        eng.wait_ge(tally.sem, tally.value())

                def product():
                    nudge(ask_pe)
                    eng.wait_ge(s_pe, pe.add())

                def turn(tiles):
                    for i, t in enumerate(tiles):
                        eng.tensor_copy(turn_in[:, i, :], t).then_inc(s_dve, chain.one())
                        eng.wait_ge(s_dve, chain.value())
                    product()
                    eng.tensor_copy(turnedT[:, 0:len(tiles), :], psA[:, 0:len(tiles) * R].rearrange("p (i r) -> p i r", r=R)).then_inc(s_dve, chain.one())
                    eng.wait_ge(s_dve, chain.value())

                def head_norm(out, x, gain):
                    eng.tensor_reduce(mean[:], heads(x), AX_X, ALU.add).then_inc(s_dve, chain.one())
                    eng.wait_ge(s_dve, chain.value())
                    eng.tensor_scalar(mean[:], mean[:], 1.0 / HD, None, ALU.mult).then_inc(s_dve, chain.one())
                    eng.wait_ge(s_dve, chain.value())
                    eng.tensor_tensor(heads(cen[:]), heads(x), over_d(mean[:]), ALU.subtract).then_inc(s_dve, chain.one())
                    eng.wait_ge(s_dve, chain.value())
                    eng.tensor_tensor(sq[:], cen[:], cen[:], ALU.mult).then_inc(s_dve, chain.one())
                    eng.wait_ge(s_dve, chain.value())
                    eng.tensor_reduce(mean[:], heads(sq[:]), AX_X, ALU.add).then_inc(s_dve, chain.one())
                    eng.wait_ge(s_dve, chain.value())
                    eng.tensor_scalar(mean[:], mean[:], 1.0 / HD, None, ALU.mult).then_inc(s_dve, chain.one())
                    eng.wait_ge(s_dve, chain.value())
                    nudge(ask_root)
                    eng.wait_ge(s_pool, pool.add(2))
                    eng.tensor_tensor(heads(cen[:]), heads(cen[:]), over_d(inv[:]), ALU.mult).then_inc(s_dve, chain.one())
                    eng.wait_ge(s_dve, chain.value())
                    eng.tensor_tensor(out, cen[:], gain, ALU.mult).then_inc(s_dve, chain.one())
                    eng.wait_ge(s_dve, chain.value())

                row = lambda n: c.row[n][0:R, :]
                eng.memset(dif[:], 0.0).then_inc(s_dve, chain.one())
                eng.wait_ge(s_dve, chain.value())
                eng.memset(ones[:], 1.0).then_inc(s_dve, chain.one())
                eng.wait_ge(s_dve, chain.value())
                eng.wait_ge(s_load, 5 * 16)
                eng.tensor_tensor(c.X[:], c.X[:], c.row["la_bo"][:, None, :].to_broadcast([P, TILES, D]), ALU.add).then_inc(s_dve, chain.one())
                eng.wait_ge(s_dve, chain.value())
                eng.bn_stats(stats[:], xs[:]).then_inc(s_dve, chain.one())
                eng.wait_ge(s_dve, chain.value())
                eng.bn_aggr(mv[:], stats[:]).then_inc(s_dve, chain.one())
                eng.wait_ge(s_dve, chain.value())
                nudge(ask_root)
                eng.wait_ge(s_pool, pool.add(7))
                eng.tensor_scalar(xn[:], xs[:], mv[:, 0:1], rs[:, 1:2], ALU.subtract, ALU.mult).then_inc(s_dve, chain.one())
                eng.wait_ge(s_dve, chain.value())
                eng.tensor_tensor(va[:], xn[:], row("la_lna"), ALU.mult).then_inc(s_dve, chain.one())
                eng.wait_ge(s_dve, chain.value())
                eng.tensor_tensor(vb_[:], xn[:], row("la_lnb"), ALU.mult).then_inc(s_dve, chain.one())
                eng.wait_ge(s_dve, chain.value())
                turn([va[:], vb_[:]])
                product()
                eng.tensor_tensor(qcur[:], psA[0:R, 0:D], row("la_bq"), ALU.add).then_inc(s_dve, chain.one())
                eng.wait_ge(s_dve, chain.value())
                product()
                eng.tensor_copy(va[:], psA[0:R, 0:D]).then_inc(s_dve, chain.one())
                eng.wait_ge(s_dve, chain.value())
                eng.tensor_tensor(vb_[:], psA[0:R, D:2 * D], row("la_bv"), ALU.add).then_inc(s_dve, chain.one())
                eng.wait_ge(s_dve, chain.value())
                turn([qcur[:], va[:], vb_[:]])
                product()
                eng.tensor_tensor(lin[:], psA[0:R, 0:D], row("la_lqb"), ALU.add).then_inc(s_dve, chain.one())
                eng.wait_ge(s_dve, chain.value())
                eng.tensor_tensor(kn[:], psA[0:R, D:2 * D], row("la_lkb"), ALU.add).then_inc(s_dve, chain.one())
                eng.wait_ge(s_dve, chain.value())
                eng.tensor_tensor(vi[:], psA[0:R, 2 * D:3 * D], row("la_lvb"), ALU.add).then_inc(s_dve, chain.one())
                eng.wait_ge(s_dve, chain.value())
                head_norm(kn[:], kn[:], row("la_lnd"))
                product()
                eng.tensor_copy(knB[:], psB[:]).then_inc(s_dve, chain.one())
                eng.wait_ge(s_dve, chain.value())
                product()
                eng.tensor_copy(viB[:], psB[:]).then_inc(s_dve, chain.one())
                eng.wait_ge(s_dve, chain.value())
                for it in range(IT):
                    if it:
                        eng.tensor_tensor(qcur[:], qcur[:], outs[:, it - 1, :], ALU.add).then_inc(s_dve, chain.one())
                        eng.wait_ge(s_dve, chain.value())
                        turn([qcur[:]])
                        product()
                        eng.tensor_tensor(lin[:], psA[0:R, 0:D], row("la_lqb"), ALU.add).then_inc(s_dve, chain.one())
                        eng.wait_ge(s_dve, chain.value())
                    head_norm(qn[:], lin[:], row("la_lnc"))
                    eng.tensor_tensor(prod[:], knB[:], qn[:, None, :].to_broadcast([R, NT, D]), ALU.mult).then_inc(s_dve, chain.one())
                    eng.wait_ge(s_dve, chain.value())
                    eng.tensor_reduce(logit[:].rearrange("p t h -> p (t h)"),
                                           prod[:].rearrange("p t (h d) -> p (t h) d", h=H), AX_X, ALU.add).then_inc(s_dve, chain.one())
                    eng.wait_ge(s_dve, chain.value())
                    eng.tensor_reduce(top[:], logit[:].rearrange("p t h -> p h t"), AX_X, ALU.max).then_inc(s_dve, chain.one())
                    eng.wait_ge(s_dve, chain.value())
                    eng.tensor_tensor(logit[:], logit[:], top[:, None, :].to_broadcast([R, NT, H]), ALU.subtract).then_inc(s_dve, chain.one())
                    eng.wait_ge(s_dve, chain.value())
                    nudge(ask_exp)
                    eng.wait_ge(s_act, act.add())
                    eng.tensor_reduce(den[:], expo[:].rearrange("p t h -> p h t"), AX_X, ALU.add).then_inc(s_dve, chain.one())
                    eng.wait_ge(s_dve, chain.value())
                    eng.reciprocal(den[:], den[:]).then_inc(s_dve, chain.one())
                    eng.wait_ge(s_dve, chain.value())
                    eng.tensor_tensor(expo[:], expo[:], den[:, None, :].to_broadcast([R, NT, H]), ALU.mult).then_inc(s_dve, chain.one())
                    eng.wait_ge(s_dve, chain.value())
                    eng.tensor_tensor(prod[:].rearrange("p t (h d) -> p (t h) d", h=H),
                                           viB[:].rearrange("p t (h d) -> p (t h) d", h=H),
                                           expo[:].rearrange("p t h -> p (t h)")[:, :, None].to_broadcast([R, NT * H, HD]), ALU.mult).then_inc(s_dve, chain.one())
                    eng.wait_ge(s_dve, chain.value())
                    eng.tensor_reduce(outs[:, it, :], prod[:].rearrange("p t e -> p e t"), AX_X, ALU.add).then_inc(s_dve, chain.one())
                    eng.wait_ge(s_dve, chain.value())
                eng.tensor_tensor(sq[:], outs[:, 1, :], outs[:, 0, :], ALU.subtract).then_inc(s_dve, chain.one())
                eng.wait_ge(s_dve, chain.value())
                eng.scalar_tensor_tensor(out=cen[:], in0=sq[:], scalar=-1.0, in1=sq[:], op0=ALU.mult, op1=ALU.max).then_inc(s_dve, chain.one())
                eng.wait_ge(s_dve, chain.value())
                eng.tensor_reduce(dif[:, 0:1], cen[:], AX_X, ALU.add).then_inc(s_dve, chain.one())
                eng.wait_ge(s_dve, chain.value())
                product()
                eng.tensor_scalar(dif[:, 0:1], psA[0:R, 0:1], 1.0 / COUNT, None, ALU.mult).then_inc(s_dve, chain.one())
                eng.wait_ge(s_dve, chain.value())
                eng.tensor_scalar(dif[:, 1:2], dif[:, 0:1], FACTOR, THRESH, ALU.mult, ALU.add).then_inc(s_dve, chain.one())
                eng.wait_ge(s_dve, chain.value())
                eng.tensor_tensor(dif[:, 0:1], dif[:, 0:1], dif[:, 1:2], ALU.is_lt).then_inc(s_dve, chain.one())
                eng.wait_ge(s_dve, chain.value())
                eng.tensor_scalar(dif[:, 1:2], dif[:, 0:1], -1.0, 1.0, ALU.mult, ALU.add).then_inc(s_dve, chain.one())
                eng.wait_ge(s_dve, chain.value())
                eng.tensor_scalar(sq[:], outs[:, 1, :], dif[:, 0:1], None, ALU.mult).then_inc(s_dve, chain.one())
                eng.wait_ge(s_dve, chain.value())
                eng.scalar_tensor_tensor(out=cen[:], in0=outs[:, 2, :], scalar=dif[:, 1:2], in1=sq[:], op0=ALU.mult, op1=ALU.add).then_inc(s_dve, chain.one())
                eng.wait_ge(s_dve, chain.value())
                turn([cen[:]])
                product()
                eng.tensor_tensor(xs[:], xs[:], row("la_bo"), ALU.add).then_inc(s_dve, chain.one())
                eng.wait_ge(s_dve, chain.value())
                eng.tensor_tensor(xs[:], xs[:], psA[0:R, 0:D], ALU.add).then_inc(s_back, 1)



MATRICES = ("f0_wq f0_wk f0_wv f0_wo ab_wq ab_wk ab_wv ab_wo f1_wq f1_wk f1_wv f1_wo "
            "rb_wq rb_wqs rb_wk rb_wks rb_wv rb_wo la_wq la_wk la_wv la_wo la_lq la_lk la_lv").split()
COLUMNS = "f0_bq f0_bk ab_bq ab_bk f1_bq f1_bk norm_w norm_b router_w router_b".split()
ROWS = ("f0_bv f0_bo ab_bv ab_bo f1_bv f1_bo rb_bv ln1_g ln1_b ln2_g ln2_b b2_0 b2_1 b2_2 b2_3 "
        "la_bq la_bv la_bo la_lna la_lnb la_lnc la_lnd la_lqb la_lkb la_lvb").split()
SIX = [(0, 0), (0, 1), (0, 2), (1, 0), (1, 1), (2, 0)]
NINE = [(i, j) for i in range(3) for j in range(3)]


def build(nc, a, out, stages=None):
    c = Core()
    with ExitStack() as ctx:
        sb = lambda n, s, d=F32: ctx.enter_context(nc.sbuf_tensor(n, s, d))
        c.X, c.Y = sb("X", [P, TILES, D]), sb("Y", [P, TILES, D])
        c.ATT, c.V = sb("ATT", [P, TILES * D]), sb("V", [P, TILES * D])
        mats, cols = sb("mats", [P, len(MATRICES), D]), sb("cols", [P, len(COLUMNS)])
        rows = sb("rows", [P, len(ROWS), D])
        c.b1, c.W1, c.W2 = sb("b1", [P, 16]), sb("W1", [P, 4, 512]), sb("W2", [P, 4, 4, D])
        c.ident, c.ident_bf = sb("ident", [P, P]), sb("ident_bf", [P, P], BF16)
        masks_f, masks = sb("masks_f", [P, 4, P]), sb("masks", [P, 4, P], BF16)
        c.mask_columns = masks[:, 3, :]
        c.rope = sb("rope", [P, 2, SEQ])
        c.width, c.minus_half, c.iota = sb("width", [P, 4]), sb("minus_half", [P, 16]), sb("iota", [P, 4])
        c.columns = sb("columns", [P, TPB, D])
        nw, nb = sb("nw", [P, 4]), sb("nb", [P, 4])
        c.scratch = nc.dram_tensor("qk_parts", [2 * 3 * D * BATCH * SEQ], BF16).ap()
        s_in, s_const, s_done = (ctx.enter_context(nc.semaphore(n)) for n in ("in", "const", "done"))
        mat = {n: mats[:, i, :] for i, n in enumerate(MATRICES)}
        col = {n: cols[:, i:i + 1] for i, n in enumerate(COLUMNS)}
        row = {n: rows[:, i, :] for i, n in enumerate(ROWS)}
        c.ln1_g, c.ln1_b, c.ln2_g, c.ln2_b = (row[n] for n in ("ln1_g", "ln1_b", "ln2_g", "ln2_b"))
        i = ROWS.index("b2_0")
        c.b2 = rows[:, i:i + 4, :]
        c.router_w, c.router_b = col["router_w"], col["router_b"]
        c.norm_w, c.norm_b = nw[:], nb[:]
        c.mat, c.col, c.row = mat, col, row

        loads = [(c.X[:], a["x"].rearrange("b (j p) d -> p (b j) d", p=P)), (mats[:], a["mats"]), (cols[:], a["cols"]),
                 (rows[:], a["rows"]), (c.b1[:], a["b1"]), (c.W1[:], a["W1"]), (c.W2[:], a["W2"]),
                 (c.ident[:], a["ident"]), (masks_f[:], a["masks"]), (c.rope[:], a["rope"]), (c.width[:], a["width"]),
                 (c.iota[:], a["iota"]), (c.columns[:], a["columns"])]
        with nc.Block() as block:
            @block.sync
            def _(eng):
                for dst, src in loads:
                    eng.dma_start(dst, src).then_inc(s_in, 16)

            @block.vector
            def _(eng):
                eng.memset(c.minus_half[:], -0.5).then_inc(s_const, 1)
                eng.wait_ge(s_in, 16 * len(loads))
                eng.tensor_copy(c.ident_bf[:], c.ident[:]).then_inc(s_const, 1)
                eng.tensor_copy(masks[:], masks_f[:]).then_inc(s_const, 1)
                eng.tensor_scalar(nw[:], c.width[:], col["norm_w"], None, ALU.mult).then_inc(s_const, 1)
                eng.tensor_scalar(nb[:], c.width[:], col["norm_b"], None, ALU.mult).then_inc(s_const, 1)
                eng.wait_ge(s_const, 5)

        f0 = dict(heads=16, dk=8, pairs=NINE, plan=plan_full(), scale=8 ** -0.5, keep=True,
                  wqk=[mat["f0_wq"], mat["f0_wk"]], bqk=[col["f0_bq"], col["f0_bk"]], wv=mat["f0_wv"],
                  bv=row["f0_bv"], wo=mat["f0_wo"], bo=row["f0_bo"])
        ab = dict(heads=8, dk=16, pairs=SIX, plan=plan_local(), scale=16 ** -0.5, lead=1,
                  mask_qk=masks[:, 2, :], mask_kq=masks[:, 2, :],
                  wqk=[mat["ab_wq"], mat["ab_wk"]], bqk=[col["ab_bq"], col["ab_bk"]], wv=mat["ab_wv"],
                  bv=row["ab_bv"], wo=mat["ab_wo"], bo=row["ab_bo"])
        f1 = dict(heads=8, dk=16, pairs=SIX, plan=plan_full(), scale=128 ** -0.5, keep=True, double=True,
                  wqk=[mat["f1_wq"], mat["f1_wk"]], bqk=[col["f1_bq"], col["f1_bk"]], wv=mat["f1_wv"],
                  bv=row["f1_bv"], wo=mat["f1_wo"], bo=row["f1_bo"])
        rb = dict(heads=16, dk=8, pairs=NINE, plan=plan_causal(), scale=8 ** -0.5, rope=True,
                  mask_qk=masks[:, 0, :], mask_kq=masks[:, 1, :],
                  wqk=[mat["rb_wq"], mat["rb_wqs"], mat["rb_wk"], mat["rb_wks"]], wv=mat["rb_wv"],
                  bv=row["rb_bv"], wo=mat["rb_wo"])

        def attention(L, name, finish):
            L = dict(L, name=name)
            project(nc, c, L)
            attend(nc, c, L)
            finish(nc, c, L)

        order = [("aa", lambda: causal_columns(nc, c, a)),
                 ("f0a", lambda: attention(f0, "f0a", experts_output)),
                 ("ab", lambda: attention(ab, "ab", output)),
                 ("f0b", lambda: attention(f0, "f0b", experts_output)),
                 ("la", lambda: iterated(nc, c, a)),
                 ("f1a", lambda: attention(f1, "f1a", output)),
                 ("rb", lambda: attention(rb, "rb", output)),
                 ("f1b", lambda: attention(f1, "f1b", output))]
        for name, go in order:
            if stages is None or name in stages:
                go()

        with nc.Block() as block:
            @block.sync
            def _(eng):
                eng.dma_start(out.rearrange("b (j p) d -> p (b j) d", p=P), c.X[:]).then_inc(s_done, 16)
                eng.wait_ge(s_done, 16)


def lay_out(inputs):
    w = {k: np.asarray(v) for k, v in inputs.items()}
    f = np.float32

    def group_order(heads):
        dk = D // heads
        return np.arange(D).reshape(heads // HG, HG, dk).transpose(0, 2, 1).reshape(-1)

    g16, g8 = group_order(16), group_order(8)
    swap = np.arange(D) ^ 1

    def diagonal(m):
        o = np.zeros((D, D), f)
        for h in range(16):
            o[8 * h:8 * h + 8, 8 * h:8 * h + 8] = m
        return o

    A, B, F0, F1, R, LA = "L0_attn_a_", "L0_attn_b_", "L0_ffn_", "L1_ffn_", "L1_attn_b_", "L1_attn_a_"
    mats = dict(
        f0_wq=w[F0 + "Wq"][:, g16], f0_wk=w[F0 + "Wk"][:, g16], f0_wv=w[F0 + "Wv"], f0_wo=w[F0 + "Wo"],
        ab_wq=w[B + "Wq"][:, g8], ab_wk=w[B + "Wk"][:, g8], ab_wv=w[B + "Wv"], ab_wo=w[B + "Wo"],
        f1_wq=w[F1 + "q_w"].T[:, g8], f1_wk=w[F1 + "k_w"].T[:, g8], f1_wv=w[F1 + "v_w"].T, f1_wo=w[F1 + "o_w"].T,
        rb_wq=w[R + "wq"].T[:, g16], rb_wqs=w[R + "wq"].T[:, swap][:, g16],
        rb_wk=w[R + "wk"].T[:, g16], rb_wks=w[R + "wk"].T[:, swap][:, g16],
        rb_wv=w[R + "wv"].T, rb_wo=w[R + "wo"].T,
        la_wq=w[LA + "qw"].T, la_wk=w[LA + "kw"].T, la_wv=w[LA + "vw"].T, la_wo=w[LA + "ow"].T,
        la_lq=diagonal(w[LA + "lqw"].T), la_lk=diagonal(w[LA + "lkw"].T), la_lv=diagonal(w[LA + "lvw"].T))
    cols = dict(f0_bq=w[F0 + "bq"][g16], f0_bk=w[F0 + "bk"][g16], ab_bq=w[B + "bq"][g8], ab_bk=w[B + "bk"][g8],
                f1_bq=w[F1 + "q_b"][g8], f1_bk=w[F1 + "k_b"][g8], norm_w=w[F1 + "norm_w"], norm_b=w[F1 + "norm_b"],
                router_w=w[F0 + "router_w"][:, 0], router_b=np.broadcast_to(w[F0 + "router_b"], (D,)))
    tile8 = lambda v: np.tile(v, 16)
    rows = dict(f0_bv=w[F0 + "bv"], f0_bo=w[F0 + "bo"], ab_bv=w[B + "bv"], ab_bo=w[B + "bo"],
                f1_bv=w[F1 + "v_b"], f1_bo=w[F1 + "o_b"], rb_bv=np.zeros(D, f),
                ln1_g=w[F0 + "ln1_g"], ln1_b=w[F0 + "ln1_b"], ln2_g=w[F0 + "ln2_g"], ln2_b=w[F0 + "ln2_b"],
                **{f"b2_{e}": w[F0 + "b2"][e] for e in range(4)},
                la_bq=w[LA + "qb"], la_bv=w[LA + "vb"], la_bo=w[LA + "ob"], la_lna=w[LA + "lna_w"],
                la_lnb=w[LA + "lnb_w"], la_lnc=tile8(w[LA + "lnc_w"]), la_lnd=tile8(w[LA + "lnd_w"]),
                la_lqb=tile8(w[LA + "lqb"]), la_lkb=tile8(w[LA + "lkb"]), la_lvb=tile8(w[LA + "lvb"]))

    wqkv = w[A + "W_qkv"].reshape(8, 2, 64, 3, D)
    bqkv = w[A + "b_qkv"].reshape(8, 2, 64, 3)
    spread = np.zeros((64, 16, 64), f)
    for b in range(BATCH):
        for t in range(16):
            spread[16 * b + t, t, 16 * b:16 * b + 16] = 1
    n = np.arange(P)
    above = np.where(n[None, :] > n[:, None], f(MASKED), f(0))
    blocks = np.where(n[None, :] // 64 != n[:, None] // 64, f(MASKED), f(0))
    dk = 8
    pos = np.arange(SEQ, dtype=f)[:, None]
    angle = (pos / f(10000.0) ** (f(2.0) * np.arange(dk // 2, dtype=f)[None, :] / f(dk))).astype(f)
    sin, cos = np.sin(angle).astype(f), np.cos(angle).astype(f)
    d = g16 % dk
    sign = np.where(d % 2 == 0, f(-1), f(1))
    rope = np.stack([cos[:, d // 2].T, (sin[:, d // 2] * sign[None, :]).T], 1)
    width = (n[:, None] < (D >> np.arange(4))[None, :]).astype(f)
    per_tile = np.stack([width[:, j // 2] for j in range(TPB)], 0)
    return {
        "x": w[A + "x"],
        "mats": np.stack([mats[k] for k in MATRICES], 1),
        "cols": np.stack([cols[k] for k in COLUMNS], 1),
        "rows": np.broadcast_to(np.stack([rows[k] for k in ROWS], 0)[None], (P, len(ROWS), D)),
        "b1": w[F0 + "b1"].reshape(16, P).T,
        "W1": w[F0 + "W1"].transpose(1, 0, 2),
        "W2": w[F0 + "W2"].reshape(4, 4, P, D).transpose(2, 0, 1, 3),
        "ident": np.eye(P, dtype=f), "masks": np.stack([above, above.T, blocks, -above.T], 1), "rope": rope, "width": width,
        "iota": np.broadcast_to(np.arange(4, dtype=f), (P, 4)),
        "columns": np.broadcast_to(per_tile[None], (P, TPB, D)),
        "spread": spread, "aa_Wqkv": np.ascontiguousarray(wqkv.transpose(4, 0, 3, 1, 2)).reshape(P, 8, 3, P),
        "aa_bqk": bqkv[:, :, :, 0:2].transpose(1, 2, 3, 0).reshape(P, 2, 8),
        "aa_bv": np.broadcast_to(bqkv[:, :, :, 2].reshape(1, 8, P), (P, 8, P)),
        "aa_Wo": w[A + "W_o"].T.reshape(8, P, D).transpose(1, 0, 2), "aa_bo": np.broadcast_to(w[A + "b_o"], (P, D)),
    }


def kernel(**inputs):
    import concourse.bacc as bacc
    from concourse.bass_utils import run_bass_kernel_spmd

    nc = bacc.Bacc("TRN2", target_bir_lowering=False, num_devices=1)
    arrays = {k: np.ascontiguousarray(v) for k, v in lay_out(inputs).items()}
    aps = {k: nc.dram_tensor("in_" + k, v.shape, mybir.dt.from_np(v.dtype), kind="ExternalInput").ap()
           for k, v in arrays.items()}
    out = nc.dram_tensor("out", arrays["x"].shape, F32, kind="ExternalOutput").ap()
    build(nc, aps, out)
    r = run_bass_kernel_spmd(nc, [{"in_" + k: v for k, v in arrays.items()}], core_ids=[0])
    return r.results[0]["out"]
```

```python
from contextlib import ExitStack, contextmanager

import concourse.bass as bass
import numpy as np
from concourse import mybir

ACT = mybir.ActivationFunctionType
ALU = mybir.AluOpType
F32 = mybir.dt.float32
BF16 = mybir.dt.bfloat16
I32 = mybir.dt.int32
AX_X = mybir.AxisListType.X

P = 128
BATCH, SEQ, D = 4, 1024, 128
TILES = BATCH * SEQ // P
TPB = SEQ // P
CHUNK = 512
TPC = CHUNK // P
CHUNKS = BATCH * SEQ // CHUNK
HG = 4
EPS = 1e-5
MASKED = -1.0e30


class Tally:

    def __init__(self, sem):
        self.sem, self.n, self.loop = sem, 0, 0

    def add(self, k=1):
        self.n += k
        return self.value()

    def one(self, k=1):
        self.n += k
        return k

    def past(self, back=0):
        v = self.value(back)
        return not isinstance(v, int) or v > 0

    def value(self, back=0):
        v = self.n - back
        return v if isinstance(self.loop, int) else self.loop + v


def hold(eng, tick):
    eng.sem_inc(tick, 1)


def run_steps(eng, tallies, emit, total, full_from, unroll=2, full_to=None):
    for s in range(full_from + 1):
        before = [t.n for t in tallies]
        emit(s, s // unroll, s % unroll)
    first = full_from + 1
    full_to = total - 2 if full_to is None else full_to
    trips = max(0, full_to + 1 - first) // unroll
    if trips:
        per = [unroll * (t.n - b) for t, b in zip(tallies, before)]
        with eng.Fori(0, trips) as i:
            start = [t.n for t in tallies]
            for t, k in zip(tallies, per):
                t.loop = i * k if k else 0
            for s in range(first, first + unroll):
                emit(i * unroll + s, i + s // unroll, s % unroll)
            for t, k, a in zip(tallies, per, start):
                assert t.n - a == k, (t.sem, t.n - a, k)
                t.n, t.loop = a, 0
        for t, k in zip(tallies, per):
            t.n += k * trips
    for s in range(first + unroll * trips, total):
        emit(s, s // unroll, s % unroll)


@contextmanager
def semaphores(nc, name):
    taken = []

    def take(n):
        taken.append(nc.alloc_semaphore(f"{name}_{n}"))
        return taken[-1]

    yield take
    nc.clear_and_free_semaphores(taken)
    nc.all_engine_barrier()


class Core:
    pass



def max_item(h0, heads, qb, blocks, stride, width, masked):
    mms, mask = [], []
    for h in range(heads):
        for b in range(blocks):
            off = (h * blocks + b) * stride
            k0 = (qb + b) * P if blocks > 1 else 0
            for k in range(0, width, 512):
                mms.append((h0 + h, qb + b, k0 + k, min(512, width - k), off + k))
            mask.append(off + width - P if masked else None)
    return dict(mms=mms, mask=mask, h0=h0, heads=heads, qb=qb, blocks=blocks, stride=stride, width=width)


def plan_full():
    maxes = [max_item(h, 1, qb, 1, SEQ, SEQ, False) for qb in range(TPB) for h in range(HG)]
    subs = []
    for qc in range(2):
        for kb in range(TPB):
            tiles = [dict(mms=[(h, kb, qc * 512, 512, 0)], mask=[], w=512) for h in range(HG)]
            evs = [(h, kb, 0, 512, h, 0, kb == 0, kb == TPB - 1) for h in range(HG)]
            subs.append(dict(tiles=tiles, evs=evs, qc=qc))
    return dict(maxes=maxes, subs=subs)


def plan_causal():
    maxes = []
    for qb in range(TPB):
        w = (qb + 1) * P
        stride = 128 if w <= 128 else 256 if w <= 256 else 512 if w <= 512 else 1024
        heads = min(HG, SEQ // stride)
        maxes += [max_item(h0, heads, qb, 1, stride, w, True) for h0 in range(0, HG, heads)]
    subs = []
    for qc in range(2):
        for kb in range(4 * qc + 4):
            q0 = max(qc * 512, kb * P)
            w = (qc + 1) * 512 - q0
            tiles = [dict(mms=[(h, kb, q0, w, 0)], mask=[0] if q0 == kb * P else [], w=w) for h in range(HG)]
            evs = [(h, kb, q0 - qc * 512, w, h, 0, kb == 0, kb == 4 * qc + 3) for h in range(HG)]
            subs.append(dict(tiles=tiles, evs=evs, qc=qc))
    return dict(maxes=maxes, subs=subs)


def plan_local():
    maxes = [max_item(0, HG, qb, 2, P, P, True) for qb in range(0, TPB, 2)]
    subs = []
    for x in range(TPB // 2):
        js = (2 * x, 2 * x + 1)
        tiles = [dict(mms=[(h, j, j * P, P, h * P) for h in range(HG)], mask=[h * P for h in range(HG)], w=512)
                 for j in js]
        evs = [(h, j, (j % 4) * P, P, j % 2, h * P, True, True) for j in js for h in range(HG)]
        subs.append(dict(tiles=tiles, evs=evs, qc=x // 2))
    return dict(maxes=maxes, subs=subs)


def allot(n_items, n_slots):
    return [(n_items * (s + 1)) // n_slots - (n_items * s) // n_slots for s in range(n_slots)]



STACKS = 3
PRELOADED = 2


def stack_fills(L):
    pairs, dk = L["pairs"], L["dk"]
    fills = [(0, i * dk, q, q + 1) for i, (q, _) in enumerate(pairs)]
    i = 0
    while i < len(pairs):
        n = 1
        while i + n < len(pairs) and pairs[i + n][1] == pairs[i][1] + n:
            n += 1
        fills.append((1, i * dk, pairs[i][1], pairs[i][1] + n))
        i += n
    return fills


def load_stacks(eng, c, L, s, p, signal):
    dk, NG = L["dk"], BATCH * L["heads"] // HG
    scratch = c.scratch.rearrange("(a g t r n) -> a g t (r n)", a=2, g=NG, t=3, r=HG * dk)
    for a, row, t0, t1 in stack_fills(L):
        dst = (c.Q, c.K)[a][row:row + (t1 - t0) * dk, p, :, :].rearrange("r h n -> r (h n)")
        src = scratch[a, bass.ds(s, 1), t0:t1, :].rearrange("g t (r n) -> (g t r) n", n=HG * SEQ)
        eng.dma_start(dst, src).then_inc(signal, 16)


def project(nc, c, L):
    name, G, dk = L["name"], L["heads"] // HG, L["dk"]
    rope, double, keep = L.get("rope"), L.get("double"), L.get("keep")
    n_qk, slots = (4, 1) if rope else (2, 2)
    with ExitStack() as ctx:
        sb = lambda n, s, d=F32: ctx.enter_context(nc.sbuf_tensor(f"{name}_{n}", s, d))
        ps = lambda n, s: ctx.enter_context(nc.psum_tensor(f"{name}_{n}", s, F32))
        sem = ctx.enter_context(semaphores(nc, name))
        stats, mv = sb("stats", [P, 2, TPC, 6]), sb("mv", [P, 2, TPC, 2])
        rs, tmp = sb("rs", [P, 2, 2, TPC]), sb("tmp", [P, 2, TPC])
        xn, xnT = sb("xn", [P, 2, TPC, D]), sb("xnT", [P, 2, CHUNK])
        full = sb("full", [P, 2, CHUNK])
        rest = sb("rest", [P, 2, CHUNK])
        part = sb("part", [P, 2, 2, 3, CHUNK], BF16)
        rot = sb("rot", [P, 2, CHUNK]) if rope else None
        psT, psQK, psV = ps("psT", [P, 2, CHUNK]), ps("psQK", [P, slots, n_qk, CHUNK]), ps("psV", [P, CHUNK])
        s_var, s_rstd, s_xn, s_T, s_xnT = (sem(n) for n in ("var", "rstd", "xn", "T", "xnT"))
        s_qk, s_high, s_rest, s_mid, s_cut = (sem(n) for n in ("qk", "high", "rest", "mid", "cut"))
        s_v, s_vout, s_dve, s_pool, tick, s_tickp, s_ticks, s_rot = (
            sem(n) for n in ("v", "vout", "dve", "pool", "tick", "tickp", "ticks", "rot"))
        s_taken = s_rot if rope else s_high
        s_ones, s_pre = sem("ones"), sem("preloaded")
        s_st, STORE = [sem("stored0"), sem("stored1")], 6 * 16
        scratch = c.scratch.rearrange("(a g t r n) -> a g t r n", a=2, g=BATCH * G, t=3, r=HG * dk)

        with nc.Block() as block:
            @block.vector
            def _(eng):
                chain, rstd, T, high, rest_, rotd = (
                    Tally(s) for s in (s_dve, s_rstd, s_T, s_high, s_rest, s_rot))
                v, qk, var, xnr, vout, cut = (Tally(s) for s in (s_v, s_qk, s_var, s_xn, s_vout, s_cut))

                def moments(s, p):
                    for j in range(TPC):
                        eng.bn_stats(stats[:, p, j, :], c.X[:, s * TPC + j, :]).then_inc(s_dve, chain.one())
                    eng.wait_ge(s_dve, chain.value())
                    hold(eng, tick)
                    for j in range(TPC):
                        ins = eng.bn_aggr(mv[:, p, j, :], stats[:, p, j, :])
                    ins.then_inc(s_var, var.one())

                def norm(s, p):
                    eng.wait_ge(s_rstd, rstd.add())
                    if T.past():
                        eng.wait_ge(s_T, T.value())
                    if not isinstance(s, int) or s >= 1:
                        T.add()
                    for j in range(TPC):
                        ins = eng.tensor_scalar(xn[:, p, j, :], c.X[:, s * TPC + j, :], mv[:, p, j, 0:1],
                                                rs[:, p, 1 if double else 0, j:j + 1], ALU.subtract, ALU.mult)
                    ins.then_inc(s_xn, xnr.one())
                    if keep:
                        for j in range(TPC):
                            ins = eng.tensor_scalar(c.Y[:, s * TPC + j, :], c.X[:, s * TPC + j, :],
                                                    mv[:, p, j, 0:1], rs[:, p, 0, j:j + 1],
                                                    ALU.subtract, ALU.mult)
                        ins.then_inc(s_dve, chain.one())

                def after(b, p):
                    if rope:
                        eng.wait_ge(s_qk, qk.add(2))
                        if rest_.past():
                            eng.wait_ge(s_rest, rest_.value())
                        for a in range(2):
                            eng.tensor_tensor(full[:, a, :], psQK[:, 0, 2 * a, :], c.rope[:, 0, p * CHUNK:(p + 1) * CHUNK], ALU.mult).then_inc(s_dve, chain.one())
                            eng.tensor_tensor(rot[:, a, :], psQK[:, 0, 2 * a + 1, :], c.rope[:, 1, p * CHUNK:(p + 1) * CHUNK], ALU.mult).then_inc(s_dve, chain.one())
                            eng.wait_ge(s_dve, chain.value())
                            eng.tensor_tensor(full[:, a, :], full[:, a, :], rot[:, a, :], ALU.add).then_inc(s_rot, rotd.one())
                    if cut.past():
                        eng.wait_ge(s_cut, cut.value())
                    cut.add(2)
                    for a in range(2):
                        eng.wait_ge(s_high, high.add())
                        eng.tensor_tensor(rest[:, a, :], full[:, a, :], part[:, p, a, 0, :], ALU.subtract).then_inc(s_rest, rest_.one())
                    eng.wait_ge(s_v, v.add())
                    eng.tensor_tensor(
                        c.V[:].rearrange("p (g j r) -> p g j r", g=BATCH * G, j=TPB)[:, bass.ds(b * G, G), p * TPC:(p + 1) * TPC, :],
                        psV[:].rearrange("p (j g r) -> p g j r", j=TPC, g=G),
                        L["bv"].rearrange("p (g r) -> p g r", g=G)[:, :, None, :].to_broadcast([P, G, TPC, HG * dk]),
                        ALU.add).then_inc(s_vout, vout.one())

                def emit(s, half, p):
                    if not isinstance(s, int) or s < CHUNKS:
                        moments(s, p)
                    if not isinstance(s, int) or 1 <= s <= CHUNKS:
                        norm(s - 1, 1 - p)
                    if not isinstance(s, int) or s >= 2:
                        after(half - 1, p)

                run_steps(eng, [chain, rstd, T, high, rest_, v, qk, var, xnr, vout, cut, rotd],
                          emit, CHUNKS + 2, 2, 2, CHUNKS - 1)

            @block.gpsimd
            def _(eng):
                var, chain, rstd, mid, cut = (Tally(s) for s in (s_var, s_pool, s_rstd, s_mid, s_cut))
                ones_row = len(L["pairs"]) * dk // 32 * 32

                def low_parts(p):
                    for a in range(2):
                        eng.wait_ge(s_mid, mid.add())
                        eng.tensor_tensor(part[:, p, a, 2, :], rest[:, a, :], part[:, p, a, 1, :], ALU.subtract).then_inc(s_cut, cut.one())

                def root(p):
                    eng.wait_ge(s_var, var.add())
                    hold(eng, s_tickp)

                    def power(j, source):
                        eng.tensor_scalar(tmp[:, p, :], source, EPS, None, ALU.add).then_inc(s_pool, chain.one())
                        eng.wait_ge(s_pool, chain.value())
                        return eng.tensor_tensor(rs[:, p, j, :], tmp[:, p, :], c.minus_half[:, 0:TPC], ALU.pow)

                    if not double:
                        power(0, mv[:, p, :, 1]).then_inc(s_rstd, rstd.one())
                        return
                    power(0, mv[:, p, :, 1]).then_inc(s_pool, chain.one())
                    eng.wait_ge(s_pool, chain.value())
                    eng.tensor_tensor(tmp[:, p, :], mv[:, p, :, 1], rs[:, p, 0, :], ALU.mult).then_inc(s_pool, chain.one())
                    eng.wait_ge(s_pool, chain.value())
                    eng.tensor_tensor(tmp[:, p, :], tmp[:, p, :], rs[:, p, 0, :], ALU.mult).then_inc(s_pool, chain.one())
                    eng.wait_ge(s_pool, chain.value())
                    hold(eng, s_tickp)
                    power(1, tmp[:, p, :]).then_inc(s_pool, chain.one())
                    eng.wait_ge(s_pool, chain.value())
                    eng.tensor_tensor(rs[:, p, 1, :], rs[:, p, 1, :], rs[:, p, 0, :], ALU.mult).then_inc(s_rstd, rstd.one())

                def emit(s, half, p):
                    if not isinstance(s, int) or s < CHUNKS:
                        root(p)
                    if isinstance(s, int) and s < STACKS:
                        eng.wait_ge(s_rstd, rstd.value())
                        eng.memset(c.K[ones_row:ones_row + 32, s, :, :].rearrange("r h n -> r (h n)"), 1.0).then_inc(s_ones, 1)
                        eng.wait_ge(s_ones, s + 1)
                    if not isinstance(s, int) or s >= 2:
                        low_parts(p)

                run_steps(eng, [var, chain, rstd, mid, cut], emit, CHUNKS + 2, 2, 2, CHUNKS - 1)

            @block.tensor
            def _(eng):
                xnr, T, xnTr, qk, taken, v, vout = (
                    Tally(s) for s in (s_xn, s_T, s_xnT, s_qk, s_taken, s_v, s_vout))

                def emit(s, half, p):
                    eng.wait_ge(s_xn, xnr.add())
                    if xnTr.past(1):
                        eng.wait_ge(s_xnT, xnTr.value(1))
                    for j in range(TPC):
                        ins = eng.transpose(psT[:, p, j * P:(j + 1) * P], xn[:, p, j, :], c.ident[:])
                    ins.then_inc(s_T, T.one())
                    eng.wait_ge(s_xnT, xnTr.add())
                    if taken.past(2 * slots - 2):
                        eng.wait_ge(s_taken, taken.value(2 * slots - 2))
                    taken.add(2)
                    for a in range(n_qk):
                        ins = eng.matmul(psQK[:, p % slots, a, :], L["wqk"][a], xnT[:, p, :], start=True, stop=True)
                        if not rope or a % 2:
                            ins.then_inc(s_qk, qk.one())
                    if vout.past():
                        eng.wait_ge(s_vout, vout.value())
                    vout.add()
                    for j in range(TPC):
                        ins = eng.matmul(psV[:, j * P:(j + 1) * P], xnT[:, p, j * P:(j + 1) * P], L["wv"],
                                         start=True, stop=True)
                    ins.then_inc(s_v, v.one())

                run_steps(eng, [xnr, T, xnTr, qk, taken, v, vout], emit, CHUNKS, 1)

            @block.scalar
            def _(eng):
                T, xnTr, qk, high, rest_, mid, v, rotd = (
                    Tally(s) for s in (s_T, s_xnT, s_qk, s_high, s_rest, s_mid, s_v, s_rot))

                def middle_parts(p):
                    for a in range(2):
                        eng.wait_ge(s_rest, rest_.add())
                        eng.copy(part[:, p, a, 1, :], rest[:, a, :]).then_inc(s_mid, mid.one())

                def take(s, half, p):
                    eng.wait_ge(s_T, T.add())
                    if v.past(1):
                        eng.wait_ge(s_v, v.value(1))
                    v.add()
                    if double:
                        for k in range(2):
                            ins = eng.activation(xnT[:, p, k * 256:(k + 1) * 256], psT[:, p, k * 256:(k + 1) * 256],
                                                 ACT.Identity, scale=c.norm_w[:, 2 * p + k:2 * p + k + 1],
                                                 bias=c.norm_b[:, 2 * p + k:2 * p + k + 1])
                    else:
                        ins = eng.copy(xnT[:, p, :], psT[:, p, :])
                    ins.then_inc(s_xnT, xnTr.one())

                def high_parts(s, half, p):
                    if not isinstance(s, int) or s >= 2:
                        eng.wait_ge(s_st[p], half * STORE)
                    for a in range(2):
                        if rope:
                            eng.wait_ge(s_rot, rotd.add())
                            eng.copy(part[:, p, a, 0, :], full[:, a, :]).then_inc(s_high, high.one())
                        else:
                            eng.wait_ge(s_qk, qk.add())
                            if rest_.past():
                                eng.wait_ge(s_rest, rest_.value())
                            eng.activation(full[:, a, :], psQK[:, p % slots, a, :], ACT.Identity, bias=L["bqk"][a])
                            eng.activation(part[:, p, a, 0, :], psQK[:, p % slots, a, :], ACT.Identity, bias=L["bqk"][a]).then_inc(s_high, high.one())

                def emit(s, half, p):
                    if not isinstance(s, int) or s < CHUNKS:
                        take(s, half, p)
                    if not isinstance(s, int) or s >= 1:
                        middle_parts(1 - p)
                    if not isinstance(s, int) or s < CHUNKS:
                        high_parts(s, half, p)

                run_steps(eng, [T, xnTr, qk, high, rest_, mid, v, rotd], emit, CHUNKS + 1, 1)

            @block.sync
            def _(eng):
                for s in range(CHUNKS):
                    half, p = s // 2, s % 2
                    for t in range(3):
                        if t == 0:
                            eng.wait_ge(s_mid, 2 * (s + 1))
                        if t == 2:
                            eng.wait_ge(s_cut, 2 * (s + 1))
                        for a in range(2):
                            dst = scratch[a, half * G:(half + 1) * G, t, :, p * CHUNK:(p + 1) * CHUNK]
                            eng.dma_start(dst, part[:, p, a, t, :]).then_inc(s_st[p], 16)
                    if p and half >= 1 and half <= PRELOADED:
                        g = half - 1
                        eng.wait_ge(s_ones, g + 1)
                        for q in range(2):
                            eng.wait_ge(s_st[q], STORE)
                        load_stacks(eng, c, L, g, g, s_pre)
                for p in range(2):
                    eng.wait_ge(s_st[p], CHUNKS // 2 * STORE)
                eng.wait_ge(s_pre, PRELOADED * 16 * len(stack_fills(L)))
                eng.wait_ge(s_ones, STACKS)



def attend(nc, c, L):
    name, G, dk, plan = L["name"] + "a", L["heads"] // HG, L["dk"], L["plan"]
    NG = BATCH * G
    pairs = L["pairs"]
    R = len(pairs) * dk
    maxes, subs = plan["maxes"], plan["subs"]
    NM, NX, LAG = len(maxes), len(subs), L.get("lag", 4)
    lots = allot(NM, NX)
    starts = [sum(lots[:x]) for x in range(NX)]
    half_end = max(x for x in range(NX) if subs[x]["qc"] == 0)
    SCORES = sum(len(x["tiles"]) for x in subs)
    with ExitStack() as ctx:
        sb = lambda n, s, d=F32: ctx.enter_context(nc.sbuf_tensor(f"{name}_{n}", s, d))
        ps = lambda n, s: ctx.enter_context(nc.psum_tensor(f"{name}_{n}", s, F32))
        sem = ctx.enter_context(semaphores(nc, name))
        Q, K = c.Q, c.K
        Vs = sb("Vs", [P, STACKS, TPB, HG, 32])
        E = sb("E", [P, 2, HG, 512])
        OT = sb("OT", [P, 2, 512])
        rowmax = sb("rowmax", [P, STACKS, HG, TPB])
        negf, rem, shift = sb("negf", [HG * TPB, P]), sb("rem", [HG * TPB, P]), sb("shift", [HG * TPB, 3, P], BF16)
        rz = sb("rz", [P, TPC, HG])
        psM, psE = ps("psM", [P, 2, SEQ]), ps("psE", [P, 2, 512])
        psO, psX = ps("psO", [P, 512]), ps("psX", [P, 512])
        s_load, s_shift = [sem(f"load{i}") for i in range(STACKS)], [sem(f"shift{i}") for i in range(STACKS)]
        s_vs, s_mm, s_red, s_ct, s_cs = (sem(n) for n in ("vs", "mm", "red", "ct", "cs"))
        s_smm, s_exp, s_ev, s_oev, s_tom, s_xfree = (
            sem(n) for n in ("smm", "exp", "ev", "oev", "tom", "xfree"))
        s_dve, s_set, tick, tickp = (sem(n) for n in ("dve", "set", "tick", "tickp"))
        V = c.V[:].rearrange("p (g j h d) -> p g j h d", g=NG, j=TPB, h=HG)
        ATT = c.ATT[:].rearrange("p (g j h d) -> p g j h d", g=NG, j=TPB, h=HG)
        LOAD, SHIFT = 16 * len(stack_fills(L)), 16 * 3
        is_group = lambda s, back: not isinstance(s, int) or 0 <= s - back < NG

        def exp_slot(x):
            return (1, x - LAG) if x >= LAG else (2, x - LAG + NX)

        def value_slot(x):
            back, v = exp_slot(x)
            return (back, v - 1) if v else (back + 1, NX - 1)

        half0_slot, half1_slot = (half_end + 2 + LAG) % NX, (1 + LAG) % NX
        half0_back, half1_back = exp_slot(half0_slot)[0], exp_slot(half1_slot)[0] + 1

        with nc.Block() as block:
            @block.sync
            def _(eng):
                cs, smm = Tally(s_cs), Tally(s_smm)

                load_stacks(eng, c, L, PRELOADED, PRELOADED, s_load[PRELOADED])

                def emit(s, trip, i):
                    if is_group(s, 1):
                        eng.wait_ge(s_cs, cs.add())
                        hold(eng, tick)
                        p = (i - 1) % STACKS
                        for t in range(3):
                            dst = Q[R + t:R + t + 1, p, :, :].rearrange("r h (b n) -> r (h b) n", n=P)
                            eng.dma_start(dst, shift[:, t, :]).then_inc(s_shift[p], 16)
                    if is_group(s, 2) and is_group(s, -1):
                        eng.wait_ge(s_smm, smm.add(SCORES))
                        hold(eng, tick)
                        load_stacks(eng, c, L, s + 1, (i + 1) % STACKS, s_load[(i + 1) % STACKS])

                run_steps(eng, [cs, smm], emit, NG + 1, 2, STACKS, NG - 2)

            @block.gpsimd
            def _(eng):
                eng.memset(Vs[:].rearrange("p u j h d -> p (u j h d)"), 0.0).then_inc(s_set, 1)
                eng.wait_ge(s_set, 1)
                for p in range(STACKS):
                    eng.memset(Vs[:, p, :, :, dk:dk + 1], 1.0).then_inc(s_set, 1)
                ev, vs = Tally(s_ev), Tally(s_vs)
                eng.wait_ge(s_set, 1 + STACKS)

                def emit(s, trip, i):
                    if is_group(s, STACKS):
                        eng.wait_ge(s_ev, ev.add(NX))
                        hold(eng, tickp)
                    eng.tensor_copy(Vs[:, i, :, :, 0:dk], V[:, bass.ds(s, 1)].rearrange("p g j h d -> p (g j) h d")).then_inc(s_vs, vs.one())

                run_steps(eng, [ev, vs], emit, NG, STACKS, STACKS)

            @block.tensor
            def _(eng):
                mm, red, ct, smm, ex, ev, oev, tom, xfree, vs = (
                    Tally(s) for s in (s_mm, s_red, s_ct, s_smm, s_exp, s_ev, s_oev, s_tom, s_xfree, s_vs))
                turned = Tally(s_oev)

                def max_item_scores(m, p):
                    t = maxes[m]
                    if red.past(1):
                        eng.wait_ge(s_red, red.value(1))
                    red.add()
                    bank = psM[:, m % 2, :]
                    for h, qb, k0, w, off in t["mms"]:
                        mask = [o for o in t["mask"] if o is not None and off <= o < off + w]
                        ins = eng.matmul(bank[:, off:off + w], Q[0:R, p, h, qb * P:(qb + 1) * P],
                                         K[0:R, p, h, k0:k0 + w], start=True, stop=not mask)
                        for o in mask:
                            ins = eng.matmul(bank[:, o:o + P], c.ident_bf[:], L["mask_qk"], start=False, stop=True)
                    ins.then_inc(s_mm, mm.one())

                def score_tile(t, k, p):
                    if ex.past(1):
                        eng.wait_ge(s_exp, ex.value(1))
                    ex.add()
                    bank = psE[:, k % 2, :]
                    for i, (h, kb, q0, w, off) in enumerate(t["mms"]):
                        masked = i < len(t["mask"])
                        ins = eng.matmul(bank[:, off:off + w], K[0:R + 3, p, h, kb * P:(kb + 1) * P],
                                         Q[0:R + 3, p, h, q0:q0 + w], start=True, stop=not masked)
                        if masked:
                            o = t["mask"][i]
                            ins = eng.matmul(bank[:, o:o + P], c.ident_bf[:], L["mask_kq"], start=False, stop=True)
                    ins.then_inc(s_smm, smm.one())

                def value_products(v, p, after):
                    eng.wait_ge(s_exp, ex.value(after))
                    if v == 0 or subs[v - 1]["qc"] != subs[v]["qc"]:
                        if oev.past():
                            eng.wait_ge(s_oev, oev.value())
                        oev.add()
                    for h, kb, col, w, tile, off, first, last in subs[v]["evs"]:
                        ins = eng.matmul(psO[32 * h:32 * h + 32, col:col + w], Vs[:, p, kb, h, :],
                                         E[:, v % 2, tile, off:off + w], start=first, stop=last)
                    ins.then_inc(s_ev, ev.one())

                def turn_out(qc):
                    eng.wait_ge(s_oev, turned.add())
                    if xfree.past():
                        eng.wait_ge(s_xfree, xfree.value())
                    xfree.add()
                    for j in range(TPC):
                        ins = eng.transpose(psX[:, j * P:(j + 1) * P], OT[:, qc, j * P:(j + 1) * P], c.ident[:])
                    ins.then_inc(s_tom, tom.one())

                def emit(s, trip, i):
                    if is_group(s, 0):
                        loads = trip + (i >= PRELOADED)
                        if not isinstance(loads, int) or loads > 0:
                            eng.wait_ge(s_load[i], loads * LOAD)
                    for x in range(NX):
                        (back, v), (vback, vv) = exp_slot(x), value_slot(x)
                        tiles = subs[v]["tiles"] if is_group(s, back) else []
                        items = list(range(starts[x], starts[x] + lots[x])) if is_group(s, 0) else []
                        if tiles and v == 0:
                            p, turn = (i - 1) % STACKS, trip + (i - 1) // STACKS
                            eng.wait_ge(s_shift[p], (turn + 1) * SHIFT)
                            eng.wait_ge(s_vs, vs.add())
                        values = is_group(s, vback)
                        for k, t in enumerate(tiles):
                            score_tile(t, k, (i - back) % STACKS)
                            if items:
                                max_item_scores(items.pop(0), i)
                            if values and k == max(0, len(tiles) - 2):
                                value_products(vv, (i - vback) % STACKS, k + 1)
                                values = False
                        if values:
                            value_products(vv, (i - vback) % STACKS, 0)
                        for m in items:
                            max_item_scores(m, i)
                        if x == 0 and is_group(s, 1):
                            eng.wait_ge(s_red, red.value(lots[0] if is_group(s, 0) else 0))
                            if xfree.past():
                                eng.wait_ge(s_xfree, xfree.value())
                            xfree.add()
                            eng.transpose(psX[0:HG * TPB, 0:P], rowmax[:, (i - 1) % STACKS].rearrange("p h b -> p (h b)"),
                                          c.ident[:]).then_inc(s_ct, ct.one())
                        if x == half0_slot and is_group(s, half0_back):
                            turn_out(0)
                        if x == half1_slot and is_group(s, half1_back):
                            turn_out(1)

                run_steps(eng, [mm, red, ct, smm, ex, ev, oev, tom, xfree, vs, turned], emit,
                          NG + 2, 3, STACKS, NG - 1)

            @block.scalar
            def _(eng):
                smm, ev, ex, oev, tom = (Tally(s) for s in (s_smm, s_ev, s_exp, s_oev, s_tom))

                def take_out(qc):
                    eng.wait_ge(s_ev, ev.value())
                    if tom.past(1):
                        eng.wait_ge(s_tom, tom.value(1))
                    tom.add()
                    eng.copy(OT[:, qc, :], psO[:]).then_inc(s_oev, oev.one())

                def emit(s, trip, i):
                    for x in range(NX):
                        (back, v), (vback, vv) = exp_slot(x), value_slot(x)
                        if is_group(s, back):
                            if ev.past():
                                eng.wait_ge(s_ev, ev.value())
                            for k, t in enumerate(subs[v]["tiles"]):
                                eng.wait_ge(s_smm, smm.add())
                                eng.activation(E[:, v % 2, k, 0:t["w"]], psE[:, k % 2, 0:t["w"]], ACT.Exp,
                                               scale=L["scale"]).then_inc(s_exp, ex.one())
                        if is_group(s, vback):
                            ev.add()
                            if vv == half_end:
                                take_out(0)
                            if vv == NX - 1:
                                take_out(1)

                run_steps(eng, [smm, ev, ex, oev, tom], emit, NG + 2, 3, STACKS, NG - 1)

            @block.vector
            def _(eng):
                mm, red, chain, ct, cs, tom, xfree = (
                    Tally(s) for s in (s_mm, s_red, s_dve, s_ct, s_cs, s_tom, s_xfree))

                def reduce(m, p):
                    t = maxes[m]
                    h, b, w = t["heads"], t["blocks"], t["width"]
                    scores = psM[:, m % 2, 0:h * b * t["stride"]].rearrange("p (h b k) -> p h b k", h=h, b=b)[:, :, :, 0:w]
                    eng.wait_ge(s_mm, mm.add())
                    eng.tensor_reduce(rowmax[:, p, t["h0"]:t["h0"] + h, t["qb"]:t["qb"] + b], scores,
                                      AX_X, ALU.max).then_inc(s_red, red.one())

                def normalise(s, qc):
                    eng.wait_ge(s_tom, tom.add())
                    x = psX[:].rearrange("p (j h d) -> p j h d", j=TPC, h=HG)
                    eng.reciprocal(rz[:], x[:, :, :, dk]).then_inc(s_dve, chain.one())
                    eng.wait_ge(s_dve, chain.value())
                    eng.tensor_tensor(
                        ATT[:, bass.ds(s, 1), qc * TPC:(qc + 1) * TPC].rearrange("p g j h d -> p (g j) h d"),
                        x[:, :, :, 0:dk], rz[:][:, :, :, None].to_broadcast([P, TPC, HG, dk]), ALU.mult).then_inc(s_xfree, xfree.one())

                def cut_shift(s, trip, i):
                    eng.wait_ge(s_ct, ct.add())
                    eng.tensor_scalar(negf[:], psX[0:HG * TPB, 0:P], -1.0, None, ALU.mult).then_inc(s_xfree, xfree.one())
                    if is_group(s, 2):
                        eng.wait_ge(s_shift[(i - 2) % STACKS], (trip + (i - 2) // STACKS + 1) * SHIFT)
                    eng.wait_ge(s_xfree, xfree.value())
                    eng.tensor_copy(shift[:, 0, :], negf[:]).then_inc(s_dve, chain.one())
                    eng.wait_ge(s_dve, chain.value())
                    eng.tensor_tensor(rem[:], negf[:], shift[:, 0, :], ALU.subtract).then_inc(s_dve, chain.one())
                    eng.wait_ge(s_dve, chain.value())
                    eng.tensor_copy(shift[:, 1, :], rem[:]).then_inc(s_dve, chain.one())
                    eng.wait_ge(s_dve, chain.value())
                    eng.tensor_tensor(shift[:, 2, :], rem[:], shift[:, 1, :], ALU.subtract).then_inc(s_cs, cs.one())

                def emit(s, trip, i):
                    for x in range(NX):
                        if is_group(s, 0):
                            for m in range(starts[x], starts[x] + lots[x]):
                                reduce(m, i)
                        if x == 0 and is_group(s, 1):
                            cut_shift(s, trip, i)
                        if x == half0_slot and is_group(s, half0_back):
                            normalise(s - half0_back, 0)
                        if x == half1_slot and is_group(s, half1_back):
                            normalise(s - half1_back, 1)

                run_steps(eng, [mm, red, chain, ct, cs, tom, xfree], emit, NG + 2, 3, STACKS, NG - 1)



def gather_heads(eng, c, G, dk, out, half, p):
    src = c.ATT[:].rearrange("p (g j r) -> p g j r", g=BATCH * G, j=TPB)
    return eng.activation(out.rearrange("p j (g r) -> p g j r", g=G),
                          src[:, bass.ds(half * G, G), p * TPC:(p + 1) * TPC, :], ACT.Identity)


def output(nc, c, L, store=None):
    name, G, dk, nested = L["name"] + "o", L["heads"] // HG, L["dk"], L.get("double")
    with ExitStack() as ctx:
        sb = lambda n, s, d=F32: ctx.enter_context(nc.sbuf_tensor(f"{name}_{n}", s, d))
        ps = lambda n, s: ctx.enter_context(nc.psum_tensor(f"{name}_{n}", s, F32))
        sem = ctx.enter_context(semaphores(nc, name))
        heads, headsT, add = sb("heads", [P, 2, TPC, D]), sb("headsT", [P, 2, CHUNK]), sb("add", [P, 2, TPC, D])
        psT, psO = ps("psT", [P, 2, CHUNK]), ps("psO", [P, 2, CHUNK])
        s_h, s_T, s_hT, s_o, s_add, s_dve, s_out, s_tick = (
            sem(n) for n in ("h", "T", "hT", "o", "add", "dve", "out", "tick"))
        with nc.Block() as block:
            @block.scalar
            def _(eng):
                h, T, hT, o = (Tally(s) for s in (s_h, s_T, s_hT, s_o))

                def emit(s, half, p):
                    if not isinstance(s, int) or s < CHUNKS:
                        if T.past():
                            eng.wait_ge(s_T, T.value())
                        gather_heads(eng, c, G, dk, heads[:, p], half, p).then_inc(s_h, h.one())
                    if not isinstance(s, int) or s >= 1:
                        eng.wait_ge(s_T, T.add())
                        if o.past(1):
                            eng.wait_ge(s_o, o.value(1))
                        o.add()
                        if nested:
                            for k in range(2):
                                ins = eng.activation(headsT[:, 1 - p, k * 256:(k + 1) * 256], psT[:, 1 - p, k * 256:(k + 1) * 256],
                                                     ACT.Identity, scale=c.width[:, 2 * (1 - p) + k:2 * (1 - p) + k + 1])
                        else:
                            ins = eng.copy(headsT[:, 1 - p, :], psT[:, 1 - p, :])
                        ins.then_inc(s_hT, hT.one())

                run_steps(eng, [h, T, hT, o], emit, CHUNKS + 1, 2)

            @block.tensor
            def _(eng):
                h, T, hT, o, added = (Tally(s) for s in (s_h, s_T, s_hT, s_o, s_add))

                def emit(s, half, p):
                    eng.wait_ge(s_h, h.add())
                    if hT.past(1):
                        eng.wait_ge(s_hT, hT.value(1))
                    for j in range(TPC):
                        ins = eng.transpose(psT[:, p, j * P:(j + 1) * P], heads[:, p, j, :], c.ident[:])
                    ins.then_inc(s_T, T.one())
                    eng.wait_ge(s_hT, hT.add())
                    if added.past(1):
                        eng.wait_ge(s_add, added.value(1))
                    added.add()
                    for j in range(TPC):
                        ins = eng.matmul(psO[:, p, j * P:(j + 1) * P], headsT[:, p, j * P:(j + 1) * P], L["wo"],
                                         start=True, stop=True)
                    ins.then_inc(s_o, o.one())

                run_steps(eng, [h, T, hT, o, added], emit, CHUNKS, 1)

            @block.vector
            def _(eng):
                o, added, chain = Tally(s_o), Tally(s_add), Tally(s_dve)

                def emit(s, half, p):
                    eng.wait_ge(s_o, o.add())
                    x = c.X[:, bass.ds(s * TPC, TPC), :]
                    t, v = add[:, p], psO[:, p, :].rearrange("p (j d) -> p j d", j=TPC)
                    if "bo" in L:
                        eng.tensor_tensor(t, v, L["bo"][:, None, :].to_broadcast([P, TPC, D]), ALU.add).then_inc(s_add, added.one())
                        eng.wait_ge(s_add, added.value())
                        if nested:
                            cols = c.columns[:, p * TPC:(p + 1) * TPC, :]
                            eng.tensor_tensor(t, t, cols, ALU.mult).then_inc(s_dve, chain.one())
                            eng.wait_ge(s_dve, chain.value())
                            eng.tensor_tensor(t, t, c.Y[:, bass.ds(s * TPC, TPC), :], ALU.add).then_inc(s_dve, chain.one())
                            eng.wait_ge(s_dve, chain.value())
                        eng.tensor_tensor(x, x, t, ALU.add).then_inc(s_dve, chain.one())
                    else:
                        eng.tensor_tensor(x, x, v, ALU.add).then_inc(s_add, added.one())

                run_steps(eng, [o, added, chain], emit, CHUNKS, 1)


def experts_output(nc, c, L):
    name, G, dk = L["name"] + "o", L["heads"] // HG, L["dk"]
    NE, NF = 4, 4
    with ExitStack() as ctx:
        sb = lambda n, s, d=F32: ctx.enter_context(nc.sbuf_tensor(f"{name}_{n}", s, d))
        ps = lambda n, s: ctx.enter_context(nc.psum_tensor(f"{name}_{n}", s, F32))
        sem = ctx.enter_context(semaphores(nc, name))
        heads, headsT = sb("heads", [P, 2, TPC, D]), sb("headsT", [P, CHUNK])
        x1, x1T, hid = sb("x1", [P, 2, TPC, D]), sb("x1T", [P, 2, CHUNK]), sb("hid", [P, 2, NF, CHUNK])
        stats, mv, rs, tmp = sb("stats", [P, TPC, 6]), sb("mv", [P, TPC, 2]), sb("rs", [P, TPC]), sb("tmp", [P, TPC])
        src, acc, bias = sb("src", [P, TPC, D]), sb("acc", [P, TPC, D]), sb("bias", [P, TPC, D])
        chosen = sb("chosen", [P, TPC, NE])
        key, whole, over = sb("key", [P, TPC]), sb("whole", [P, TPC]), sb("over", [P, TPC])
        whole_i, index = sb("whole_i", [P, TPC], I32), sb("index", [P, TPC])
        psT, psO = ps("psT", [P, CHUNK]), ps("psO", [P, CHUNK])
        psH, psY = ps("psH", [P, NF, CHUNK]), ps("psY", [P, 2, TPC, D])
        s_h, s_T, s_hT, s_o, s_var, s_rstd, s_x1, s_x1t, s_x1T, s_key, s_chosen = (
            sem(n) for n in ("h", "T", "hT", "o", "var", "rstd", "x1", "x1t", "x1T", "key", "chosen"))
        s_up, s_relu, s_down, s_comb, s_dve, s_pool, tick, tickp = (
            sem(n) for n in ("up", "relu", "down", "comb", "dve", "pool", "tick", "tickp"))
        more = lambda s, n=1: not isinstance(s, int) or s + n < CHUNKS

        with nc.Block() as block:
            @block.scalar
            def _(eng):
                h, T, hT, up, relu, down, x1t, x1T_ = (
                    Tally(s) for s in (s_h, s_T, s_hT, s_up, s_relu, s_down, s_x1t, s_x1T))

                def heads_turned():
                    eng.wait_ge(s_T, T.add())
                    eng.copy(headsT[:], psT[:]).then_inc(s_hT, hT.one())

                def x1_turned(p):
                    eng.wait_ge(s_x1t, x1t.add())
                    eng.copy(x1T[:, p, :], psT[:]).then_inc(s_x1T, x1T_.one())

                def emit(s, half, p):
                    for e in range(NE):
                        if down.past(1):
                            eng.wait_ge(s_down, down.value(1))
                        down.add()
                        for f in range(NF):
                            eng.wait_ge(s_up, up.add())
                            eng.activation(hid[:, e % 2, f, :], psH[:, f, :], ACT.Relu,
                                           bias=c.b1[:, e * NF + f:e * NF + f + 1]).then_inc(s_relu, relu.one())
                        if e == 0 and more(s):
                            heads_turned()
                    if more(s, 2):
                        gather_heads(eng, c, G, dk, heads[:, p], half + 1, p).then_inc(s_h, h.one())
                    if more(s):
                        x1_turned(1 - p)

                gather_heads(eng, c, G, dk, heads[:, 0], 0, 0).then_inc(s_h, h.one())
                heads_turned()
                gather_heads(eng, c, G, dk, heads[:, 1], 0, 1).then_inc(s_h, h.one())
                x1_turned(0)
                run_steps(eng, [h, T, hT, up, relu, down, x1t, x1T_], emit, CHUNKS, 1, 2, CHUNKS - 3)

            @block.gpsimd
            def _(eng):
                var, chain, rstd = Tally(s_var), Tally(s_pool), Tally(s_rstd)

                def root():
                    eng.wait_ge(s_var, var.add())
                    hold(eng, tickp)
                    eng.tensor_scalar(tmp[:], mv[:, :, 1], EPS, None, ALU.add).then_inc(s_pool, chain.one())
                    eng.wait_ge(s_pool, chain.value())
                    eng.tensor_tensor(rs[:], tmp[:], c.minus_half[:, 0:TPC], ALU.pow).then_inc(s_rstd, rstd.one())

                def emit(s, half, p):
                    if more(s):
                        root()
                    root()

                root()
                run_steps(eng, [var, chain, rstd], emit, CHUNKS, 1)

            @block.tensor
            def _(eng):
                h, T, hT, o, x1_, x1t, x1T_, key_, chosen_ = (
                    Tally(s) for s in (s_h, s_T, s_hT, s_o, s_x1, s_x1t, s_x1T, s_key, s_chosen))
                up, relu, down, comb = (Tally(s) for s in (s_up, s_relu, s_down, s_comb))

                def hidden(e, p):
                    for f in range(NF):
                        if relu.past(NF - 1):
                            eng.wait_ge(s_relu, relu.value(NF - 1))
                        relu.add()
                        eng.matmul(psH[:, f, :], c.W1[:, e, f * P:(f + 1) * P], x1T[:, p, :],
                                   start=True, stop=True).then_inc(s_up, up.one())

                def out_of(e, later):
                    eng.wait_ge(s_relu, relu.value(later))
                    if comb.past(1):
                        eng.wait_ge(s_comb, comb.value(1))
                    comb.add()
                    for j in range(TPC):
                        for f in range(NF):
                            ins = eng.matmul(psY[:, e % 2, j, :], hid[:, e % 2, f, j * P:(j + 1) * P],
                                             c.W2[:, e, f, :], start=f == 0, stop=f == NF - 1)
                    ins.then_inc(s_down, down.one())

                def turn_heads(p):
                    eng.wait_ge(s_h, h.add())
                    for j in range(TPC):
                        ins = eng.transpose(psT[:, j * P:(j + 1) * P], heads[:, p, j, :], c.ident[:])
                    ins.then_inc(s_T, T.one())

                def heads_out():
                    eng.wait_ge(s_hT, hT.add())
                    if chosen_.past():
                        eng.wait_ge(s_chosen, chosen_.value())
                    chosen_.add()
                    for j in range(TPC):
                        ins = eng.matmul(psO[:, j * P:(j + 1) * P], headsT[:, j * P:(j + 1) * P], L["wo"],
                                         start=True, stop=True)
                    ins.then_inc(s_o, o.one())

                def turn_x1(p):
                    eng.wait_ge(s_x1, x1_.add())
                    for j in range(TPC):
                        ins = eng.transpose(psT[:, j * P:(j + 1) * P], x1[:, p, j, :], c.ident[:])
                    ins.then_inc(s_x1t, x1t.one())

                def keys(p):
                    eng.wait_ge(s_x1T, x1T_.add())
                    for j in range(TPC):
                        ins = eng.matmul(psO[:, j:j + 1], x1T[:, p, j * P:(j + 1) * P], c.router_w[:, 0:1],
                                         start=True, stop=True)
                    ins.then_inc(s_key, key_.one())

                def emit(s, half, p):
                    hidden(0, p)
                    if more(s):
                        turn_heads(1 - p)
                    hidden(1, p)
                    out_of(0, NF)
                    if more(s):
                        heads_out()
                    hidden(2, p)
                    out_of(1, NF)
                    hidden(3, p)
                    out_of(2, NF)
                    if more(s):
                        turn_x1(1 - p)
                    out_of(3, 0)
                    if more(s):
                        keys(1 - p)

                turn_heads(0)
                heads_out()
                turn_x1(0)
                keys(0)
                run_steps(eng, [h, T, hT, o, x1_, x1t, x1T_, key_, chosen_, up, relu, down, comb],
                          emit, CHUNKS, 1)

            @block.vector
            def _(eng):
                o, var, rstd, x1_, key_, chosen_, down, comb, chain = (
                    Tally(s) for s in (s_o, s_var, s_rstd, s_x1, s_key, s_chosen, s_down, s_comb, s_dve))
                tiles = lambda r: r[:, None, :].to_broadcast([P, TPC, D])

                def norm(x, out, gain, shift):
                    for j in range(TPC):
                        eng.bn_stats(stats[:, j, :], x[:, j, :]).then_inc(s_dve, chain.one())
                    eng.wait_ge(s_dve, chain.value())
                    hold(eng, tick)
                    for j in range(TPC):
                        ins = eng.bn_aggr(mv[:, j, :], stats[:, j, :])
                    ins.then_inc(s_var, var.one())
                    eng.wait_ge(s_rstd, rstd.add())
                    for j in range(TPC):
                        ins = eng.tensor_scalar(out[:, j, :], x[:, j, :], mv[:, j, 0:1], rs[:, j:j + 1],
                                                ALU.subtract, ALU.mult)
                    ins.then_inc(s_dve, chain.one())
                    eng.wait_ge(s_dve, chain.value())
                    eng.tensor_tensor(out, out, tiles(gain), ALU.mult).then_inc(s_dve, chain.one())
                    eng.wait_ge(s_dve, chain.value())
                    return eng.tensor_tensor(out, out, tiles(shift), ALU.add)

                def first_norm(s, p):
                    eng.wait_ge(s_o, o.add())
                    eng.tensor_tensor(src[:], psO[:].rearrange("p (j d) -> p j d", j=TPC), tiles(L["bo"]), ALU.add).then_inc(s_dve, chain.one())
                    eng.wait_ge(s_dve, chain.value())
                    eng.tensor_tensor(src[:], src[:], c.Y[:, bass.ds(s * TPC, TPC), :], ALU.add).then_inc(s_dve, chain.one())
                    eng.wait_ge(s_dve, chain.value())
                    norm(src[:], x1[:, p], c.ln1_g, c.ln1_b).then_inc(s_x1, x1_.one())

                def choose():
                    eng.wait_ge(s_key, key_.add())
                    eng.tensor_scalar(key[:], psO[:, 0:TPC], c.router_b[:, 0:1], None, ALU.add).then_inc(s_dve, chain.one())
                    eng.wait_ge(s_dve, chain.value())
                    eng.tensor_copy(whole_i[:], key[:]).then_inc(s_dve, chain.one())
                    eng.wait_ge(s_dve, chain.value())
                    eng.tensor_copy(whole[:], whole_i[:]).then_inc(s_dve, chain.one())
                    eng.wait_ge(s_dve, chain.value())
                    eng.tensor_tensor(over[:], whole[:], key[:], ALU.is_gt).then_inc(s_dve, chain.one())
                    eng.wait_ge(s_dve, chain.value())
                    eng.tensor_tensor(whole[:], whole[:], over[:], ALU.subtract).then_inc(s_dve, chain.one())
                    eng.wait_ge(s_dve, chain.value())
                    eng.tensor_copy(whole_i[:], whole[:]).then_inc(s_dve, chain.one())
                    eng.wait_ge(s_dve, chain.value())
                    eng.tensor_scalar(whole_i[:], whole_i[:], NE - 1, None, ALU.bitwise_and).then_inc(s_dve, chain.one())
                    eng.wait_ge(s_dve, chain.value())
                    eng.tensor_copy(index[:], whole_i[:]).then_inc(s_dve, chain.one())
                    eng.wait_ge(s_dve, chain.value())
                    eng.tensor_tensor(chosen[:], index[:][:, :, None].to_broadcast([P, TPC, NE]),
                                      c.iota[:, None, 0:NE].to_broadcast([P, TPC, NE]), ALU.is_equal).then_inc(s_chosen, chosen_.one())

                def chosen_bias():
                    eng.wait_ge(s_chosen, chosen_.value())
                    for j in range(TPC):
                        ins = eng.tensor_scalar(bias[:, j, :], c.b2[:, 0, :], chosen[:, j, 0:1], None, ALU.mult)
                    ins.then_inc(s_dve, chain.one())
                    for e in range(1, NE):
                        eng.wait_ge(s_dve, chain.value())
                        for j in range(TPC):
                            ins = eng.scalar_tensor_tensor(out=bias[:, j, :], in0=c.b2[:, e, :], scalar=chosen[:, j, e:e + 1],
                                                           in1=bias[:, j, :], op0=ALU.mult, op1=ALU.add)
                        ins.then_inc(s_dve, chain.one())
                    eng.wait_ge(s_dve, chain.value())

                def combine(e):
                    eng.wait_ge(s_down, down.add())
                    for j in range(TPC):
                        ins = eng.scalar_tensor_tensor(out=acc[:, j, :], in0=psY[:, e % 2, j, :],
                                                       scalar=chosen[:, j, e:e + 1],
                                                       in1=(acc if e else bias)[:, j, :], op0=ALU.mult, op1=ALU.add)
                    ins.then_inc(s_comb, comb.one())
                    eng.wait_ge(s_comb, comb.value())

                def emit(s, half, p):
                    combine(0)
                    if more(s):
                        first_norm(s + 1, 1 - p)
                    combine(1)
                    combine(2)
                    combine(3)
                    a = acc[:]
                    eng.tensor_tensor(a, a, x1[:, p], ALU.add).then_inc(s_dve, chain.one())
                    if more(s):
                        choose()
                    eng.wait_ge(s_dve, chain.value())
                    norm(a, a, c.ln2_g, c.ln2_b).then_inc(s_dve, chain.one())
                    eng.wait_ge(s_dve, chain.value())
                    x = c.X[:, bass.ds(s * TPC, TPC), :]
                    eng.tensor_tensor(x, x, a, ALU.add).then_inc(s_dve, chain.one())
                    if more(s):
                        chosen_bias()

                first_norm(0, 0)
                choose()
                chosen_bias()
                run_steps(eng, [o, var, rstd, x1_, key_, chosen_, down, comb, chain], emit, CHUNKS, 1)



RMS_EPS = 1.1920929e-07


def causal_columns(nc, c, a):
    NPAIR, KB, QC = 8, TPB, 2
    STEPS = NPAIR * BATCH
    with ExitStack() as ctx:
        sb = lambda n, s, d=F32: ctx.enter_context(nc.sbuf_tensor("aa_" + n, s, d))
        ps = lambda n, s: ctx.enter_context(nc.psum_tensor("aa_" + n, s, F32))
        sem = ctx.enter_context(semaphores(nc, "aa"))
        xT = c.Y[:].rearrange("p t d -> p (t d)")
        Wqkv = c.ATT[:, 0:3 * NPAIR * P].rearrange("p (h m e) -> p h m e", h=NPAIR, m=3)
        Wo = c.V[:, 0:NPAIR * D].rearrange("p (h e) -> p h e", h=NPAIR)
        bv = c.V[:, NPAIR * D:2 * NPAIR * D].rearrange("p (h e) -> p h e", h=NPAIR)
        bqk, nbq, bo = sb("bqk", [P, 2, NPAIR]), sb("nbq", [P, NPAIR]), sb("bo", [P, D])
        stats, mv = sb("stats", [P, 2, TPC, 6]), sb("mv", [P, 2, TPC, 2])
        tmp, rs = sb("tmp", [P, TPC]), sb("rs", [P, 2, 2, TPC])
        xn = sb("xn", [P, 2, TPC, D])
        s_w, s_const, ticka = sem("weights"), sem("const"), sem("ticka")

        with ExitStack() as c2:
            psT = c2.enter_context(nc.psum_tensor("aa_psT", [P, 2, CHUNK], F32))
            s_var, s_rstd, s_xn, s_T, s_xT, s_dve, s_pool, tick, tickp = (
                sem(n) for n in ("var", "rstd", "xn", "T", "xT", "dve", "pool", "tick", "tickp"))
            with nc.Block() as block:
                @block.sync
                def _(eng):
                    eng.dma_start(bo[:], a["aa_bo"]).then_inc(s_w, 16)
                    eng.dma_start(bqk[:], a["aa_bqk"]).then_inc(s_w, 16)
                    eng.dma_start(Wqkv, a["aa_Wqkv"]).then_inc(s_w, 16)
                    eng.dma_start(Wo, a["aa_Wo"]).then_inc(s_w, 16)
                    eng.dma_start(bv, a["aa_bv"]).then_inc(s_w, 16)

                @block.vector
                def _(eng):
                    chain, var, rstd, xn_, T = (Tally(s) for s in (s_dve, s_var, s_rstd, s_xn, s_T))
                    eng.wait_ge(s_w, 5 * 16)
                    eng.tensor_scalar(nbq[:], bqk[:, 0, :], -1.0, None, ALU.mult).then_inc(s_const, 1)

                    def moments(s, p):
                        for j in range(TPC):
                            eng.bn_stats(stats[:, p, j, :], c.X[:, s * TPC + j, :]).then_inc(s_dve, chain.one())
                        eng.wait_ge(s_dve, chain.value())
                        hold(eng, tick)
                        for j in range(TPC):
                            ins = eng.bn_aggr(mv[:, p, j, :], stats[:, p, j, :])
                        ins.then_inc(s_var, var.one())

                    def norm(s, p):
                        eng.wait_ge(s_rstd, rstd.add())
                        if T.past():
                            eng.wait_ge(s_T, T.value())
                        if not isinstance(s, int) or s >= 1:
                            T.add()
                        for j in range(TPC):
                            ins = eng.tensor_scalar(xn[:, p, j, :], c.X[:, s * TPC + j, :], mv[:, p, j, 0:1],
                                                    rs[:, p, 1, j:j + 1], ALU.subtract, ALU.mult)
                        ins.then_inc(s_xn, xn_.one())
                        eng.wait_ge(s_xn, xn_.value())
                        x = c.X[:, bass.ds(s * TPC, TPC), :]
                        eng.tensor_tensor(x, x, bo[:, None, :].to_broadcast([P, TPC, D]), ALU.add).then_inc(s_dve, chain.one())

                    def emit(s, half, p):
                        if not isinstance(s, int) or s < CHUNKS:
                            moments(s, p)
                        if not isinstance(s, int) or s >= 1:
                            norm(s - 1, 1 - p)

                    run_steps(eng, [chain, var, rstd, xn_, T], emit, CHUNKS + 1, 2)
                    if chain.past():
                        eng.wait_ge(s_dve, chain.value())

                @block.gpsimd
                def _(eng):
                    var, chain, rstd = Tally(s_var), Tally(s_pool), Tally(s_rstd)

                    def emit(s, half, p):
                        eng.wait_ge(s_var, var.add())
                        hold(eng, tickp)
                        eng.tensor_scalar(tmp[:], mv[:, p, :, 1], EPS, None, ALU.add).then_inc(s_pool, chain.one())
                        eng.wait_ge(s_pool, chain.value())
                        eng.tensor_tensor(rs[:, p, 0, :], tmp[:], c.minus_half[:, 0:TPC], ALU.pow).then_inc(s_pool, chain.one())
                        eng.wait_ge(s_pool, chain.value())
                        eng.tensor_tensor(tmp[:], mv[:, p, :, 1], rs[:, p, 0, :], ALU.mult).then_inc(s_pool, chain.one())
                        eng.wait_ge(s_pool, chain.value())
                        eng.tensor_tensor(tmp[:], tmp[:], rs[:, p, 0, :], ALU.mult).then_inc(s_pool, chain.one())
                        eng.wait_ge(s_pool, chain.value())
                        hold(eng, tickp)
                        eng.tensor_scalar(tmp[:], tmp[:], RMS_EPS, None, ALU.add).then_inc(s_pool, chain.one())
                        eng.wait_ge(s_pool, chain.value())
                        eng.tensor_tensor(rs[:, p, 1, :], tmp[:], c.minus_half[:, 0:TPC], ALU.pow).then_inc(s_pool, chain.one())
                        eng.wait_ge(s_pool, chain.value())
                        eng.tensor_tensor(rs[:, p, 1, :], rs[:, p, 1, :], rs[:, p, 0, :], ALU.mult).then_inc(s_rstd, rstd.one())

                    run_steps(eng, [var, chain, rstd], emit, CHUNKS, 1)

                @block.tensor
                def _(eng):
                    xn_, T, xT_ = (Tally(s) for s in (s_xn, s_T, s_xT))

                    def emit(s, half, p):
                        eng.wait_ge(s_xn, xn_.add())
                        if xT_.past(1):
                            eng.wait_ge(s_xT, xT_.value(1))
                        xT_.add()
                        for j in range(TPC):
                            ins = eng.transpose(psT[:, p, j * P:(j + 1) * P], xn[:, p, j, :], c.ident[:])
                        ins.then_inc(s_T, T.one())

                    run_steps(eng, [xn_, T, xT_], emit, CHUNKS, 1)

                @block.scalar
                def _(eng):
                    T, xT_ = Tally(s_T), Tally(s_xT)

                    def emit(s, half, p):
                        eng.wait_ge(s_T, T.add())
                        hold(eng, ticka)
                        eng.activation(xT[:, bass.ds(s * CHUNK, CHUNK)], psT[:, p, :], ACT.Identity).then_inc(s_xT, xT_.one())

                    run_steps(eng, [T, xT_], emit, CHUNKS, 1)

        q, k = sb("q", [P, 2, SEQ]), sb("k", [P, 2, 2, SEQ])
        v, vz = sb("v", [P, 2, KB, P]), sb("vz", [P, 2, P])
        E, zT = sb("E", [P, 2, 2, SEQ]), sb("zT", [P, 2, SEQ])
        w = sb("w", [P, 3, P])
        least, total, rz = sb("least", [P, 2 * KB]), sb("total", [P, 2 * KB]), sb("rz", [P, 2 * KB])
        psS, psZ, psW = ps("psS", [P, 2, SEQ]), ps("psZ", [P, SEQ]), ps("psW", [P, 2, CHUNK])
        s_set, s_wst, s_S, s_min, s_exp, s_rz, s_vz, s_ev, s_zT = (
            sem(n) for n in ("set", "wst", "S", "min", "exp", "rz", "vz", "ev", "zT"))
        s_qk, s_qkout, s_v, s_vout, s_o, s_oout, tickq = (
            sem(n) for n in ("qk", "qkout", "v", "vout", "o", "oout", "tickq"))
        SLOTS = [["o0"], ["o1", "q0"], ["q1"], ["k0"], ["k1"], ["v0"], ["v1"], []]
        chunks = lambda kb: [(max(kb * P, qc * CHUNK), (qc + 1) * CHUNK, qc) for qc in range(QC) if kb * P < (qc + 1) * CHUNK]
        more = lambda s: not isinstance(s, int) or s + 1 < STEPS
        later = lambda s: not isinstance(s, int) or s >= 1
        nxt = lambda pair, b: (pair + 1, 0) if b == BATCH - 1 else (pair, b + 1)
        prv = lambda pair, b: (pair - 1, BATCH - 1) if b == 0 else (pair, b - 1)

        with nc.Block() as block:
            @block.gpsimd
            def _(eng):
                eng.memset(k[:].rearrange("p u h n -> p (u h n)"), 0.0).then_inc(s_set, 1)
                eng.tensor_copy(w[:], Wqkv[:, 0]).then_inc(s_wst, 1)
                with eng.Fori(0, NPAIR - 1) as i:
                    eng.wait_ge(s_v, i * (2 * BATCH) + 2 * BATCH)
                    hold(eng, tickq)
                    eng.tensor_copy(w[:], Wqkv[:, bass.ds(i + 1, 1)].rearrange("p h m e -> p (h m) e")).then_inc(s_wst, 1)

            @block.tensor
            def _(eng):
                S, ex, vz_, ev, zT_ = (Tally(s) for s in (s_S, s_exp, s_vz, s_ev, s_zT))
                qk, qkout, v_, vout, o, oout = (Tally(s) for s in (s_qk, s_qkout, s_v, s_vout, s_o, s_oout))

                def fill(what, pair, b, p, outs_before=False):
                    kind, n = what[0], int(what[1])
                    bank = psW[:, n, :]
                    if kind == "q" and outs_before:
                        eng.wait_ge(s_oout, oout.add())
                    if kind in "kv":
                        eng.wait_ge(s_qkout, qkout.add())
                    if kind in "qk":
                        x = xT[:, b * SEQ + n * CHUNK:b * SEQ + (n + 1) * CHUNK]
                        eng.matmul(bank, w[:, "qk".index(kind), :], x, start=True, stop=True).then_inc(s_qk, qk.one())
                    elif kind == "v":
                        for j in range(TPC):
                            t = b * SEQ + n * CHUNK + j * P
                            ins = eng.matmul(bank[:, j * P:(j + 1) * P], xT[:, t:t + P], w[:, 2, :], start=True, stop=True)
                        ins.then_inc(s_v, v_.one())
                    else:
                        for j in range(TPC):
                            t = n * CHUNK + j * P
                            ins = eng.matmul(bank[:, j * P:(j + 1) * P], zT[:, p, t:t + P], Wo[:, pair, :], start=True, stop=True)
                        ins.then_inc(s_o, o.one())

                def out_product(what, pair, b, p):
                    if what == "o0":
                        eng.wait_ge(s_zT, zT_.add())
                    fill(what, pair, b, p)

                def score(kb, h, p, t):
                    if ex.past(1):
                        eng.wait_ge(s_exp, ex.value(1))
                    ex.add()
                    for a0, a1, qc in chunks(kb):
                        diag = a0 == kb * P
                        ins = eng.matmul(psS[:, t % 2, a0:a1], k[:, p, h, kb * P:(kb + 1) * P], q[:, p, a0:a1],
                                         start=True, stop=not diag)
                        if diag:
                            ins = eng.matmul(psS[:, t % 2, a0:a0 + P], c.ident_bf[:], c.mask_columns, start=False, stop=True)
                    ins.then_inc(s_S, S.one())

                def value(kb):
                    eng.wait_ge(s_vz, vz_.add(2))
                    if kb == 0:
                        if zT_.past():
                            eng.wait_ge(s_zT, zT_.value())
                    for a0, a1, qc in chunks(kb):
                        for h in range(2):
                            ins = eng.matmul(psZ[64 * h:64 * h + 64, a0:a1], vz[:, kb % 2, 64 * h:64 * h + 64],
                                             E[:, kb % 2, h, a0:a1], start=kb == 0, stop=kb == 4 * qc + 3)
                    ins.then_inc(s_ev, ev.one())

                def emit(s, pair, b):
                    p = b % 2
                    for kb in range(KB):
                        if kb == 0:
                            eng.wait_ge(s_vout, v_.value())
                        for h in range(2):
                            score(kb, h, p, h)
                        for what in SLOTS[kb]:
                            if what[0] == "o":
                                if later(s):
                                    out_product(what, *prv(pair, b), 1 - p)
                                continue
                            if more(s):
                                n_pair, n_b = nxt(pair, b)
                                if what == "q0" and n_b == 0:
                                    eng.wait_ge(s_wst, n_pair + 1)
                                fill(what, n_pair, n_b, 1 - p, later(s))
                        if kb:
                            value(kb - 1)
                    value(KB - 1)

                eng.wait_ge(s_wst, 1)
                for what in ("q0", "q1", "k0", "k1", "v0", "v1"):
                    fill(what, 0, 0, 0)
                run_steps(eng, [S, ex, vz_, ev, zT_, qk, qkout, v_, vout, o, oout], emit, STEPS, 1, unroll=BATCH)
                eng.wait_ge(s_oout, 2 * (STEPS - 1))
                for what in ("o0", "o1"):
                    out_product(what, *prv(NPAIR, 0), (STEPS - 1) % 2)

            @block.scalar
            def _(eng):
                mn, ex, ev, zT_, o, qk, qkout = (Tally(s) for s in (s_min, s_exp, s_ev, s_zT, s_o, s_qk, s_qkout))

                def take(what, pair, p):
                    kind, n = what[0], int(what[1])
                    eng.wait_ge(s_qk, qk.add())
                    hold(eng, ticka)
                    cols = slice(n * CHUNK, (n + 1) * CHUNK)
                    if kind == "q":
                        eng.activation(q[:, p, cols], psW[:, n, :], ACT.Identity, scale=-1.0,
                                              bias=nbq[:, bass.ds(pair, 1)]).then_inc(s_qkout, qkout.one())
                    else:
                        for h in range(2):
                            r = slice(64 * h, 64 * h + 64)
                            ins = eng.activation(k[r, p, h, cols], psW[r, n, :], ACT.Identity,
                                                 bias=bqk[r, 1, bass.ds(pair, 1)])
                        ins.then_inc(s_qkout, qkout.one())

                def emit(s, pair, b):
                    p = b % 2
                    for kb in range(KB):
                        if ev.past(1):
                            eng.wait_ge(s_ev, ev.value(1))
                        ev.add()
                        for h in range(2):
                            t = 2 * kb + h
                            eng.wait_ge(s_min, mn.add())
                            eng.activation(E[:, kb % 2, h, kb * P:SEQ], psS[:, h, kb * P:SEQ], ACT.Exp,
                                                  bias=least[:, t:t + 1], scale=-1.0, accum_out=total[:, t:t + 1]).then_inc(s_exp, ex.one())
                        for what in SLOTS[kb]:
                            if what[0] in "qk" and more(s):
                                n_pair, n_b = nxt(pair, b)
                                take(what, n_pair, 1 - p)
                    if ev.past():
                        eng.wait_ge(s_ev, ev.value())
                    if o.past(2):
                        eng.wait_ge(s_o, o.value(2))
                    if later(s):
                        o.add(2)
                    eng.copy(zT[:, p, :], psZ[:]).then_inc(s_zT, zT_.one())

                eng.wait_ge(s_set, 1)
                for what in ("q0", "q1", "k0", "k1"):
                    take(what, 0, 0)
                run_steps(eng, [mn, ex, ev, zT_, o, qk, qkout], emit, STEPS, 1, unroll=BATCH)

            @block.vector
            def _(eng):
                S, mn, ex, rz_, vz_, ev = (Tally(s) for s in (s_S, s_min, s_exp, s_rz, s_vz, s_ev))
                v_, vout, o, oout = (Tally(s) for s in (s_v, s_vout, s_o, s_oout))

                def minimum(kb, h):
                    eng.wait_ge(s_S, S.add())
                    t = 2 * kb + h
                    eng.tensor_reduce(least[:, t:t + 1], psS[:, h, kb * P:SEQ], AX_X, ALU.min).then_inc(s_min, mn.one())

                def scale_v(kb, h, p):
                    t = 2 * kb + h
                    eng.wait_ge(s_exp, ex.add())
                    eng.reciprocal(rz[:, t:t + 1], total[:, t:t + 1]).then_inc(s_rz, rz_.one())
                    eng.wait_ge(s_rz, rz_.value())
                    if h == 0:
                        if ev.past(1):
                            eng.wait_ge(s_ev, ev.value(1))
                        ev.add()
                    r = slice(64 * h, 64 * h + 64)
                    eng.tensor_scalar(vz[:, kb % 2, r], v[:, p, kb, r], rz[:, t:t + 1], None, ALU.mult).then_inc(s_vz, vz_.one())

                def take_v(n, pair, p):
                    eng.wait_ge(s_v, v_.add())
                    eng.tensor_tensor(v[:, p, n * TPC:(n + 1) * TPC, :], psW[:, n, :].rearrange("p (j e) -> p j e", j=TPC),
                                             bv[:, bass.ds(pair, 1), :].to_broadcast([P, TPC, P]), ALU.add).then_inc(s_vout, vout.one())

                def add_out(n, b):
                    eng.wait_ge(s_o, o.add())
                    x = c.X[:, b * TPB + n * TPC:b * TPB + (n + 1) * TPC, :]
                    eng.tensor_tensor(x, x, psW[:, n, :].rearrange("p (j d) -> p j d", j=TPC), ALU.add).then_inc(s_oout, oout.one())

                def emit(s, pair, b):
                    p = b % 2
                    for kb in range(KB):
                        minimum(kb, 0)
                        if kb:
                            scale_v(kb - 1, 1, p)
                        minimum(kb, 1)
                        scale_v(kb, 0, p)
                        for what in SLOTS[kb]:
                            if what[0] == "o" and later(s):
                                add_out(int(what[1]), prv(pair, b)[1])
                            if what[0] == "v" and more(s):
                                take_v(int(what[1]), nxt(pair, b)[0], 1 - p)
                    scale_v(KB - 1, 1, p)

                for n in range(2):
                    take_v(n, 0, 0)
                run_steps(eng, [S, mn, ex, rz_, vz_, ev, v_, vout, o, oout], emit, STEPS, 1, unroll=BATCH)
                for n in range(2):
                    add_out(n, BATCH - 1)



def iterated(nc, c, a):
    NT, H, HD, IT = 16, 16, 8, 3
    R = BATCH * NT
    COUNT = float(BATCH * H * SEQ * HD)
    THRESH, FACTOR = 0.01, 0.1
    with ExitStack() as ctx:
        sb = lambda n, s, d=F32: ctx.enter_context(nc.sbuf_tensor("la_" + n, s, d))
        ps = lambda n, s: ctx.enter_context(nc.psum_tensor("la_" + n, s, F32))
        sem = ctx.enter_context(semaphores(nc, "la"))
        xs, xn, va, vb_ = sb("xs", [R, D]), sb("xn", [R, D]), sb("va", [R, D]), sb("vb_", [R, D])
        stats, mv, rs, tmp = sb("stats", [R, 6]), sb("mv", [R, 2]), sb("rs", [R, 2]), sb("tmp", [R, H])
        turn_in, turnedT = sb("turn_in", [R, 3, D]), sb("turnedT", [P, 3, R])
        qcur, lin, cen, sq, inv = sb("qcur", [R, D]), sb("lin", [R, D]), sb("cen", [R, D]), sb("sq", [R, D]), sb("inv", [R, H])
        mean, kn, vi, qn = sb("mean", [R, H]), sb("kn", [R, D]), sb("vi", [R, D]), sb("qn", [R, D])
        knB, viB, prod = sb("knB", [R, NT, D]), sb("viB", [R, NT, D]), sb("prod", [R, NT, D])
        logit, top, expo, den = sb("logit", [R, NT, H]), sb("top", [R, H]), sb("expo", [R, NT, H]), sb("den", [R, H])
        outs = sb("outs", [R, IT, D])
        spread, ones, dif = sb("spread", [R, NT, R]), sb("ones", [R, R]), sb("dif", [R, 4])
        psA, psB = ps("psA", [P, CHUNK]), ps("psB", [R, NT, D])
        s_load, s_dve, s_act, s_pool, s_pe, s_back, tick, tickp = (
            sem(n) for n in ("load", "dve", "act", "pool", "pe", "back", "tick", "tickp"))
        s_turn, s_root, s_expo = sem("turn"), sem("root"), sem("expo")
        m = c.mat
        heads = lambda t: t.rearrange("p (h d) -> p h d", h=H)
        over_d = lambda t: t[:, :, None].to_broadcast([R, H, HD])

        with nc.Block() as block:
            @block.sync
            def _(eng):
                for b in range(BATCH):
                    eng.dma_start(xs[b * NT:(b + 1) * NT, :], c.X[0:NT, b * TPB, :]).then_inc(s_load, 16)
                eng.dma_start(spread[:], a["spread"]).then_inc(s_load, 16)
                eng.wait_ge(s_back, 1)
                for b in range(BATCH):
                    eng.dma_start(c.X[0:NT, b * TPB, :], xs[b * NT:(b + 1) * NT, :]).then_inc(s_load, 16)
                eng.wait_ge(s_load, 9 * 16)

            @block.gpsimd
            def _(eng):
                asked, chain = Tally(s_root), Tally(s_pool)

                def root(out, source, width):
                    eng.tensor_scalar(tmp[:, 0:width], source, EPS, None, ALU.add).then_inc(s_pool, chain.one())
                    eng.wait_ge(s_pool, chain.value())
                    return eng.tensor_tensor(out, tmp[:, 0:width], c.minus_half[0:R, 0:width], ALU.pow)

                eng.wait_ge(s_root, asked.add())
                root(rs[:, 0:1], mv[:, 1:2], 1).then_inc(s_pool, chain.one())
                eng.wait_ge(s_pool, chain.value())
                eng.tensor_tensor(mv[:, 1:2], mv[:, 1:2], rs[:, 0:1], ALU.mult).then_inc(s_pool, chain.one())
                eng.wait_ge(s_pool, chain.value())
                eng.tensor_tensor(mv[:, 1:2], mv[:, 1:2], rs[:, 0:1], ALU.mult).then_inc(s_pool, chain.one())
                eng.wait_ge(s_pool, chain.value())
                root(rs[:, 1:2], mv[:, 1:2], 1).then_inc(s_pool, chain.one())
                eng.wait_ge(s_pool, chain.value())
                eng.tensor_tensor(rs[:, 1:2], rs[:, 1:2], rs[:, 0:1], ALU.mult).then_inc(s_pool, chain.one())
                eng.wait_ge(s_pool, chain.value())
                for _ in range(1 + IT):
                    eng.wait_ge(s_root, asked.add())
                    root(inv[:], mean[:], H).then_inc(s_pool, chain.one())
                    eng.wait_ge(s_pool, chain.value())

            @block.scalar
            def _(eng):
                asked, done = Tally(s_expo), Tally(s_act)
                for _ in range(IT):
                    eng.wait_ge(s_expo, asked.add())
                    eng.activation(expo[:], logit[:], ACT.Exp, scale=HD ** -0.5).then_inc(s_act, done.one())

            @block.tensor
            def _(eng):
                asked, done = Tally(s_turn), Tally(s_pe)

                def turn(n):
                    eng.wait_ge(s_turn, asked.add())
                    for i in range(n):
                        ins = eng.transpose(psA[:, i * R:(i + 1) * R], turn_in[:, i, :], c.ident[0:R, 0:R])
                    ins.then_inc(s_pe, done.one())

                def product(weights):
                    eng.wait_ge(s_turn, asked.add())
                    for i, wt in enumerate(weights):
                        ins = eng.matmul(psA[0:R, i * D:(i + 1) * D], turnedT[:, i, :], wt, start=True, stop=True)
                    ins.then_inc(s_pe, done.one())

                def spread_rows(x):
                    eng.wait_ge(s_turn, asked.add())
                    for t in range(NT):
                        ins = eng.matmul(psB[:, t, :], spread[:, t, :], x[:], start=True, stop=True)
                    ins.then_inc(s_pe, done.one())

                turn(2)
                product([m["la_wq"]])
                eng.wait_ge(s_turn, asked.add())
                for i, n in enumerate(("la_wk", "la_wv")):
                    ins = eng.matmul(psA[0:R, i * D:(i + 1) * D], turnedT[:, 1, :], m[n], start=True, stop=True)
                ins.then_inc(s_pe, done.one())
                turn(3)
                product([m["la_lq"], m["la_lk"], m["la_lv"]])
                spread_rows(kn)
                spread_rows(vi)
                for it in range(IT):
                    if it:
                        turn(1)
                        product([m["la_lq"]])
                eng.wait_ge(s_turn, asked.add())
                eng.matmul(psA[0:R, 0:1], ones[:], dif[:, 0:1], start=True, stop=True).then_inc(s_pe, done.one())
                turn(1)
                product([m["la_wo"]])

            @block.vector
            def _(eng):
                chain, pe, pool, act = Tally(s_dve), Tally(s_pe), Tally(s_pool), Tally(s_act)
                ask_pe, ask_root, ask_exp = Tally(s_turn), Tally(s_root), Tally(s_expo)

                def nudge(tally):
                    eng.tensor_copy(dif[:, 3:4], dif[:, 2:3]).then_inc(tally.sem, tally.one())
                    if tally.past():
                        eng.wait_ge(tally.sem, tally.value())

                def product():
                    nudge(ask_pe)
                    eng.wait_ge(s_pe, pe.add())

                def turn(tiles):
                    for i, t in enumerate(tiles):
                        eng.tensor_copy(turn_in[:, i, :], t).then_inc(s_dve, chain.one())
                        eng.wait_ge(s_dve, chain.value())
                    product()
                    eng.tensor_copy(turnedT[:, 0:len(tiles), :], psA[:, 0:len(tiles) * R].rearrange("p (i r) -> p i r", r=R)).then_inc(s_dve, chain.one())
                    eng.wait_ge(s_dve, chain.value())

                def head_norm(out, x, gain):
                    eng.tensor_reduce(mean[:], heads(x), AX_X, ALU.add).then_inc(s_dve, chain.one())
                    eng.wait_ge(s_dve, chain.value())
                    eng.tensor_scalar(mean[:], mean[:], 1.0 / HD, None, ALU.mult).then_inc(s_dve, chain.one())
                    eng.wait_ge(s_dve, chain.value())
                    eng.tensor_tensor(heads(cen[:]), heads(x), over_d(mean[:]), ALU.subtract).then_inc(s_dve, chain.one())
                    eng.wait_ge(s_dve, chain.value())
                    eng.tensor_tensor(sq[:], cen[:], cen[:], ALU.mult).then_inc(s_dve, chain.one())
                    eng.wait_ge(s_dve, chain.value())
                    eng.tensor_reduce(mean[:], heads(sq[:]), AX_X, ALU.add).then_inc(s_dve, chain.one())
                    eng.wait_ge(s_dve, chain.value())
                    eng.tensor_scalar(mean[:], mean[:], 1.0 / HD, None, ALU.mult).then_inc(s_dve, chain.one())
                    eng.wait_ge(s_dve, chain.value())
                    nudge(ask_root)
                    eng.wait_ge(s_pool, pool.add(2))
                    eng.tensor_tensor(heads(cen[:]), heads(cen[:]), over_d(inv[:]), ALU.mult).then_inc(s_dve, chain.one())
                    eng.wait_ge(s_dve, chain.value())
                    eng.tensor_tensor(out, cen[:], gain, ALU.mult).then_inc(s_dve, chain.one())
                    eng.wait_ge(s_dve, chain.value())

                row = lambda n: c.row[n][0:R, :]
                eng.memset(dif[:], 0.0).then_inc(s_dve, chain.one())
                eng.wait_ge(s_dve, chain.value())
                eng.memset(ones[:], 1.0).then_inc(s_dve, chain.one())
                eng.wait_ge(s_dve, chain.value())
                eng.wait_ge(s_load, 5 * 16)
                eng.tensor_tensor(c.X[:], c.X[:], c.row["la_bo"][:, None, :].to_broadcast([P, TILES, D]), ALU.add).then_inc(s_dve, chain.one())
                eng.wait_ge(s_dve, chain.value())
                eng.bn_stats(stats[:], xs[:]).then_inc(s_dve, chain.one())
                eng.wait_ge(s_dve, chain.value())
                eng.bn_aggr(mv[:], stats[:]).then_inc(s_dve, chain.one())
                eng.wait_ge(s_dve, chain.value())
                nudge(ask_root)
                eng.wait_ge(s_pool, pool.add(7))
                eng.tensor_scalar(xn[:], xs[:], mv[:, 0:1], rs[:, 1:2], ALU.subtract, ALU.mult).then_inc(s_dve, chain.one())
                eng.wait_ge(s_dve, chain.value())
                eng.tensor_tensor(va[:], xn[:], row("la_lna"), ALU.mult).then_inc(s_dve, chain.one())
                eng.wait_ge(s_dve, chain.value())
                eng.tensor_tensor(vb_[:], xn[:], row("la_lnb"), ALU.mult).then_inc(s_dve, chain.one())
                eng.wait_ge(s_dve, chain.value())
                turn([va[:], vb_[:]])
                product()
                eng.tensor_tensor(qcur[:], psA[0:R, 0:D], row("la_bq"), ALU.add).then_inc(s_dve, chain.one())
                eng.wait_ge(s_dve, chain.value())
                product()
                eng.tensor_copy(va[:], psA[0:R, 0:D]).then_inc(s_dve, chain.one())
                eng.wait_ge(s_dve, chain.value())
                eng.tensor_tensor(vb_[:], psA[0:R, D:2 * D], row("la_bv"), ALU.add).then_inc(s_dve, chain.one())
                eng.wait_ge(s_dve, chain.value())
                turn([qcur[:], va[:], vb_[:]])
                product()
                eng.tensor_tensor(lin[:], psA[0:R, 0:D], row("la_lqb"), ALU.add).then_inc(s_dve, chain.one())
                eng.wait_ge(s_dve, chain.value())
                eng.tensor_tensor(kn[:], psA[0:R, D:2 * D], row("la_lkb"), ALU.add).then_inc(s_dve, chain.one())
                eng.wait_ge(s_dve, chain.value())
                eng.tensor_tensor(vi[:], psA[0:R, 2 * D:3 * D], row("la_lvb"), ALU.add).then_inc(s_dve, chain.one())
                eng.wait_ge(s_dve, chain.value())
                head_norm(kn[:], kn[:], row("la_lnd"))
                product()
                eng.tensor_copy(knB[:], psB[:]).then_inc(s_dve, chain.one())
                eng.wait_ge(s_dve, chain.value())
                product()
                eng.tensor_copy(viB[:], psB[:]).then_inc(s_dve, chain.one())
                eng.wait_ge(s_dve, chain.value())
                for it in range(IT):
                    if it:
                        eng.tensor_tensor(qcur[:], qcur[:], outs[:, it - 1, :], ALU.add).then_inc(s_dve, chain.one())
                        eng.wait_ge(s_dve, chain.value())
                        turn([qcur[:]])
                        product()
                        eng.tensor_tensor(lin[:], psA[0:R, 0:D], row("la_lqb"), ALU.add).then_inc(s_dve, chain.one())
                        eng.wait_ge(s_dve, chain.value())
                    head_norm(qn[:], lin[:], row("la_lnc"))
                    eng.tensor_tensor(prod[:], knB[:], qn[:, None, :].to_broadcast([R, NT, D]), ALU.mult).then_inc(s_dve, chain.one())
                    eng.wait_ge(s_dve, chain.value())
                    eng.tensor_reduce(logit[:].rearrange("p t h -> p (t h)"),
                                           prod[:].rearrange("p t (h d) -> p (t h) d", h=H), AX_X, ALU.add).then_inc(s_dve, chain.one())
                    eng.wait_ge(s_dve, chain.value())
                    eng.tensor_reduce(top[:], logit[:].rearrange("p t h -> p h t"), AX_X, ALU.max).then_inc(s_dve, chain.one())
                    eng.wait_ge(s_dve, chain.value())
                    eng.tensor_tensor(logit[:], logit[:], top[:, None, :].to_broadcast([R, NT, H]), ALU.subtract).then_inc(s_dve, chain.one())
                    eng.wait_ge(s_dve, chain.value())
                    nudge(ask_exp)
                    eng.wait_ge(s_act, act.add())
                    eng.tensor_reduce(den[:], expo[:].rearrange("p t h -> p h t"), AX_X, ALU.add).then_inc(s_dve, chain.one())
                    eng.wait_ge(s_dve, chain.value())
                    eng.reciprocal(den[:], den[:]).then_inc(s_dve, chain.one())
                    eng.wait_ge(s_dve, chain.value())
                    eng.tensor_tensor(expo[:], expo[:], den[:, None, :].to_broadcast([R, NT, H]), ALU.mult).then_inc(s_dve, chain.one())
                    eng.wait_ge(s_dve, chain.value())
                    eng.tensor_tensor(prod[:].rearrange("p t (h d) -> p (t h) d", h=H),
                                           viB[:].rearrange("p t (h d) -> p (t h) d", h=H),
                                           expo[:].rearrange("p t h -> p (t h)")[:, :, None].to_broadcast([R, NT * H, HD]), ALU.mult).then_inc(s_dve, chain.one())
                    eng.wait_ge(s_dve, chain.value())
                    eng.tensor_reduce(outs[:, it, :], prod[:].rearrange("p t e -> p e t"), AX_X, ALU.add).then_inc(s_dve, chain.one())
                    eng.wait_ge(s_dve, chain.value())
                eng.tensor_tensor(sq[:], outs[:, 1, :], outs[:, 0, :], ALU.subtract).then_inc(s_dve, chain.one())
                eng.wait_ge(s_dve, chain.value())
                eng.scalar_tensor_tensor(out=cen[:], in0=sq[:], scalar=-1.0, in1=sq[:], op0=ALU.mult, op1=ALU.max).then_inc(s_dve, chain.one())
                eng.wait_ge(s_dve, chain.value())
                eng.tensor_reduce(dif[:, 0:1], cen[:], AX_X, ALU.add).then_inc(s_dve, chain.one())
                eng.wait_ge(s_dve, chain.value())
                product()
                eng.tensor_scalar(dif[:, 0:1], psA[0:R, 0:1], 1.0 / COUNT, None, ALU.mult).then_inc(s_dve, chain.one())
                eng.wait_ge(s_dve, chain.value())
                eng.tensor_scalar(dif[:, 1:2], dif[:, 0:1], FACTOR, THRESH, ALU.mult, ALU.add).then_inc(s_dve, chain.one())
                eng.wait_ge(s_dve, chain.value())
                eng.tensor_tensor(dif[:, 0:1], dif[:, 0:1], dif[:, 1:2], ALU.is_lt).then_inc(s_dve, chain.one())
                eng.wait_ge(s_dve, chain.value())
                eng.tensor_scalar(dif[:, 1:2], dif[:, 0:1], -1.0, 1.0, ALU.mult, ALU.add).then_inc(s_dve, chain.one())
                eng.wait_ge(s_dve, chain.value())
                eng.tensor_scalar(sq[:], outs[:, 1, :], dif[:, 0:1], None, ALU.mult).then_inc(s_dve, chain.one())
                eng.wait_ge(s_dve, chain.value())
                eng.scalar_tensor_tensor(out=cen[:], in0=outs[:, 2, :], scalar=dif[:, 1:2], in1=sq[:], op0=ALU.mult, op1=ALU.add).then_inc(s_dve, chain.one())
                eng.wait_ge(s_dve, chain.value())
                turn([cen[:]])
                product()
                eng.tensor_tensor(xs[:], xs[:], row("la_bo"), ALU.add).then_inc(s_dve, chain.one())
                eng.wait_ge(s_dve, chain.value())
                eng.tensor_tensor(xs[:], xs[:], psA[0:R, 0:D], ALU.add).then_inc(s_back, 1)



MATRICES = ("f0_wq f0_wk f0_wv f0_wo ab_wq ab_wk ab_wv ab_wo f1_wq f1_wk f1_wv f1_wo "
            "rb_wq rb_wqs rb_wk rb_wks rb_wv rb_wo la_wq la_wk la_wv la_wo la_lq la_lk la_lv").split()
COLUMNS = "f0_bq f0_bk ab_bq ab_bk f1_bq f1_bk norm_w norm_b router_w router_b".split()
ROWS = ("f0_bv f0_bo ab_bv ab_bo f1_bv f1_bo rb_bv ln1_g ln1_b ln2_g ln2_b b2_0 b2_1 b2_2 b2_3 "
        "la_bq la_bv la_bo la_lna la_lnb la_lnc la_lnd la_lqb la_lkb la_lvb").split()
SIX = [(0, 0), (0, 1), (0, 2), (1, 0), (1, 1), (2, 0)]
NINE = [(i, j) for i in range(3) for j in range(3)]


def build(nc, a, out, stages=None):
    c = Core()
    with ExitStack() as ctx:
        sb = lambda n, s, d=F32: ctx.enter_context(nc.sbuf_tensor(n, s, d))
        c.X, c.Y = sb("X", [P, TILES, D]), sb("Y", [P, TILES, D])
        c.ATT, c.V = sb("ATT", [P, TILES * D]), sb("V", [P, TILES * D])
        mats, cols = sb("mats", [P, len(MATRICES), D]), sb("cols", [P, len(COLUMNS)])
        rows = sb("rows", [P, len(ROWS), D])
        c.b1, c.W1, c.W2 = sb("b1", [P, 16]), sb("W1", [P, 4, 512]), sb("W2", [P, 4, 4, D])
        c.ident, c.ident_bf = sb("ident", [P, P]), sb("ident_bf", [P, P], BF16)
        masks_f, masks = sb("masks_f", [P, 4, P]), sb("masks", [P, 4, P], BF16)
        c.mask_columns = masks[:, 3, :]
        c.rope = sb("rope", [P, 2, SEQ])
        c.width, c.minus_half, c.iota = sb("width", [P, 4]), sb("minus_half", [P, 16]), sb("iota", [P, 4])
        c.columns = sb("columns", [P, TPB, D])
        nw, nb = sb("nw", [P, 4]), sb("nb", [P, 4])
        c.scratch = nc.dram_tensor("qk_parts", [2 * 3 * D * BATCH * SEQ], BF16).ap()
        s_in, s_const, s_done = (ctx.enter_context(nc.semaphore(n)) for n in ("in", "const", "done"))
        mat = {n: mats[:, i, :] for i, n in enumerate(MATRICES)}
        col = {n: cols[:, i:i + 1] for i, n in enumerate(COLUMNS)}
        row = {n: rows[:, i, :] for i, n in enumerate(ROWS)}
        c.ln1_g, c.ln1_b, c.ln2_g, c.ln2_b = (row[n] for n in ("ln1_g", "ln1_b", "ln2_g", "ln2_b"))
        i = ROWS.index("b2_0")
        c.b2 = rows[:, i:i + 4, :]
        c.router_w, c.router_b = col["router_w"], col["router_b"]
        c.norm_w, c.norm_b = nw[:], nb[:]
        c.mat, c.col, c.row = mat, col, row

        loads = [(c.X[:], a["x"].rearrange("b (j p) d -> p (b j) d", p=P)), (mats[:], a["mats"]), (cols[:], a["cols"]),
                 (rows[:], a["rows"]), (c.b1[:], a["b1"]), (c.W1[:], a["W1"]), (c.W2[:], a["W2"]),
                 (c.ident[:], a["ident"]), (masks_f[:], a["masks"]), (c.rope[:], a["rope"]), (c.width[:], a["width"]),
                 (c.iota[:], a["iota"]), (c.columns[:], a["columns"])]
        with nc.Block() as block:
            @block.sync
            def _(eng):
                for dst, src in loads:
                    eng.dma_start(dst, src).then_inc(s_in, 16)

            @block.vector
            def _(eng):
                eng.memset(c.minus_half[:], -0.5).then_inc(s_const, 1)
                eng.wait_ge(s_in, 16 * len(loads))
                eng.tensor_copy(c.ident_bf[:], c.ident[:]).then_inc(s_const, 1)
                eng.tensor_copy(masks[:], masks_f[:]).then_inc(s_const, 1)
                eng.tensor_scalar(nw[:], c.width[:], col["norm_w"], None, ALU.mult).then_inc(s_const, 1)
                eng.tensor_scalar(nb[:], c.width[:], col["norm_b"], None, ALU.mult).then_inc(s_const, 1)
                eng.wait_ge(s_const, 5)

        f0 = dict(heads=16, dk=8, pairs=NINE, plan=plan_full(), scale=8 ** -0.5, keep=True,
                  wqk=[mat["f0_wq"], mat["f0_wk"]], bqk=[col["f0_bq"], col["f0_bk"]], wv=mat["f0_wv"],
                  bv=row["f0_bv"], wo=mat["f0_wo"], bo=row["f0_bo"])
        ab = dict(heads=8, dk=16, pairs=SIX, plan=plan_local(), scale=16 ** -0.5, lag=2,
                  mask_qk=masks[:, 2, :], mask_kq=masks[:, 2, :],
                  wqk=[mat["ab_wq"], mat["ab_wk"]], bqk=[col["ab_bq"], col["ab_bk"]], wv=mat["ab_wv"],
                  bv=row["ab_bv"], wo=mat["ab_wo"], bo=row["ab_bo"])
        f1 = dict(heads=8, dk=16, pairs=SIX, plan=plan_full(), scale=128 ** -0.5, keep=True, double=True,
                  wqk=[mat["f1_wq"], mat["f1_wk"]], bqk=[col["f1_bq"], col["f1_bk"]], wv=mat["f1_wv"],
                  bv=row["f1_bv"], wo=mat["f1_wo"], bo=row["f1_bo"])
        rb = dict(heads=16, dk=8, pairs=NINE, plan=plan_causal(), scale=8 ** -0.5, rope=True,
                  mask_qk=masks[:, 0, :], mask_kq=masks[:, 1, :],
                  wqk=[mat["rb_wq"], mat["rb_wqs"], mat["rb_wk"], mat["rb_wks"]], wv=mat["rb_wv"],
                  bv=row["rb_bv"], wo=mat["rb_wo"])

        def attention(L, name, finish):
            L = dict(L, name=name)
            with nc.sbuf_tensor(name + "_Q", [P, STACKS, HG, SEQ], BF16) as c.Q, \
                    nc.sbuf_tensor(name + "_K", [P, STACKS, HG, SEQ], BF16) as c.K:
                project(nc, c, L)
                attend(nc, c, L)
            finish(nc, c, L)

        order = [("aa", lambda: causal_columns(nc, c, a)),
                 ("f0a", lambda: attention(f0, "f0a", experts_output)),
                 ("ab", lambda: attention(ab, "ab", output)),
                 ("f0b", lambda: attention(f0, "f0b", experts_output)),
                 ("la", lambda: iterated(nc, c, a)),
                 ("f1a", lambda: attention(f1, "f1a", output)),
                 ("rb", lambda: attention(rb, "rb", output)),
                 ("f1b", lambda: attention(f1, "f1b", output))]
        for name, go in order:
            if stages is None or name in stages:
                go()

        with nc.Block() as block:
            @block.sync
            def _(eng):
                eng.dma_start(out.rearrange("b (j p) d -> p (b j) d", p=P), c.X[:]).then_inc(s_done, 16)
                eng.wait_ge(s_done, 16)


def lay_out(inputs):
    w = {k: np.asarray(v) for k, v in inputs.items()}
    f = np.float32

    def group_order(heads):
        dk = D // heads
        return np.arange(D).reshape(heads // HG, HG, dk).transpose(0, 2, 1).reshape(-1)

    g16, g8 = group_order(16), group_order(8)
    swap = np.arange(D) ^ 1

    def diagonal(m):
        o = np.zeros((D, D), f)
        for h in range(16):
            o[8 * h:8 * h + 8, 8 * h:8 * h + 8] = m
        return o

    A, B, F0, F1, R, LA = "L0_attn_a_", "L0_attn_b_", "L0_ffn_", "L1_ffn_", "L1_attn_b_", "L1_attn_a_"
    mats = dict(
        f0_wq=w[F0 + "Wq"][:, g16], f0_wk=w[F0 + "Wk"][:, g16], f0_wv=w[F0 + "Wv"], f0_wo=w[F0 + "Wo"],
        ab_wq=w[B + "Wq"][:, g8], ab_wk=w[B + "Wk"][:, g8], ab_wv=w[B + "Wv"], ab_wo=w[B + "Wo"],
        f1_wq=w[F1 + "q_w"].T[:, g8], f1_wk=w[F1 + "k_w"].T[:, g8], f1_wv=w[F1 + "v_w"].T, f1_wo=w[F1 + "o_w"].T,
        rb_wq=w[R + "wq"].T[:, g16], rb_wqs=w[R + "wq"].T[:, swap][:, g16],
        rb_wk=w[R + "wk"].T[:, g16], rb_wks=w[R + "wk"].T[:, swap][:, g16],
        rb_wv=w[R + "wv"].T, rb_wo=w[R + "wo"].T,
        la_wq=w[LA + "qw"].T, la_wk=w[LA + "kw"].T, la_wv=w[LA + "vw"].T, la_wo=w[LA + "ow"].T,
        la_lq=diagonal(w[LA + "lqw"].T), la_lk=diagonal(w[LA + "lkw"].T), la_lv=diagonal(w[LA + "lvw"].T))
    cols = dict(f0_bq=w[F0 + "bq"][g16], f0_bk=w[F0 + "bk"][g16], ab_bq=w[B + "bq"][g8], ab_bk=w[B + "bk"][g8],
                f1_bq=w[F1 + "q_b"][g8], f1_bk=w[F1 + "k_b"][g8], norm_w=w[F1 + "norm_w"], norm_b=w[F1 + "norm_b"],
                router_w=w[F0 + "router_w"][:, 0], router_b=np.broadcast_to(w[F0 + "router_b"], (D,)))
    tile8 = lambda v: np.tile(v, 16)
    rows = dict(f0_bv=w[F0 + "bv"], f0_bo=w[F0 + "bo"], ab_bv=w[B + "bv"], ab_bo=w[B + "bo"],
                f1_bv=w[F1 + "v_b"], f1_bo=w[F1 + "o_b"], rb_bv=np.zeros(D, f),
                ln1_g=w[F0 + "ln1_g"], ln1_b=w[F0 + "ln1_b"], ln2_g=w[F0 + "ln2_g"], ln2_b=w[F0 + "ln2_b"],
                **{f"b2_{e}": w[F0 + "b2"][e] for e in range(4)},
                la_bq=w[LA + "qb"], la_bv=w[LA + "vb"], la_bo=w[LA + "ob"], la_lna=w[LA + "lna_w"],
                la_lnb=w[LA + "lnb_w"], la_lnc=tile8(w[LA + "lnc_w"]), la_lnd=tile8(w[LA + "lnd_w"]),
                la_lqb=tile8(w[LA + "lqb"]), la_lkb=tile8(w[LA + "lkb"]), la_lvb=tile8(w[LA + "lvb"]))

    wqkv = w[A + "W_qkv"].reshape(8, 2, 64, 3, D)
    bqkv = w[A + "b_qkv"].reshape(8, 2, 64, 3)
    spread = np.zeros((64, 16, 64), f)
    for b in range(BATCH):
        for t in range(16):
            spread[16 * b + t, t, 16 * b:16 * b + 16] = 1
    n = np.arange(P)
    above = np.where(n[None, :] > n[:, None], f(MASKED), f(0))
    blocks = np.where(n[None, :] // 64 != n[:, None] // 64, f(MASKED), f(0))
    dk = 8
    pos = np.arange(SEQ, dtype=f)[:, None]
    angle = (pos / f(10000.0) ** (f(2.0) * np.arange(dk // 2, dtype=f)[None, :] / f(dk))).astype(f)
    sin, cos = np.sin(angle).astype(f), np.cos(angle).astype(f)
    d = g16 % dk
    sign = np.where(d % 2 == 0, f(-1), f(1))
    rope = np.stack([cos[:, d // 2].T, (sin[:, d // 2] * sign[None, :]).T], 1)
    width = (n[:, None] < (D >> np.arange(4))[None, :]).astype(f)
    per_tile = np.stack([width[:, j // 2] for j in range(TPB)], 0)
    return {
        "x": w[A + "x"],
        "mats": np.stack([mats[k] for k in MATRICES], 1),
        "cols": np.stack([cols[k] for k in COLUMNS], 1),
        "rows": np.broadcast_to(np.stack([rows[k] for k in ROWS], 0)[None], (P, len(ROWS), D)),
        "b1": w[F0 + "b1"].reshape(16, P).T,
        "W1": w[F0 + "W1"].transpose(1, 0, 2),
        "W2": w[F0 + "W2"].reshape(4, 4, P, D).transpose(2, 0, 1, 3),
        "ident": np.eye(P, dtype=f), "masks": np.stack([above, above.T, blocks, -above.T], 1), "rope": rope, "width": width,
        "iota": np.broadcast_to(np.arange(4, dtype=f), (P, 4)),
        "columns": np.broadcast_to(per_tile[None], (P, TPB, D)),
        "spread": spread, "aa_Wqkv": np.ascontiguousarray(wqkv.transpose(4, 0, 3, 1, 2)).reshape(P, 8, 3, P),
        "aa_bqk": bqkv[:, :, :, 0:2].transpose(1, 2, 3, 0).reshape(P, 2, 8),
        "aa_bv": np.broadcast_to(bqkv[:, :, :, 2].reshape(1, 8, P), (P, 8, P)),
        "aa_Wo": w[A + "W_o"].T.reshape(8, P, D).transpose(1, 0, 2), "aa_bo": np.broadcast_to(w[A + "b_o"], (P, D)),
    }


def kernel(**inputs):
    import concourse.bacc as bacc
    from concourse.bass_utils import run_bass_kernel_spmd

    nc = bacc.Bacc("TRN2", target_bir_lowering=False, num_devices=1)
    arrays = {k: np.ascontiguousarray(v) for k, v in lay_out(inputs).items()}
    aps = {k: nc.dram_tensor("in_" + k, v.shape, mybir.dt.from_np(v.dtype), kind="ExternalInput").ap()
           for k, v in arrays.items()}
    out = nc.dram_tensor("out", arrays["x"].shape, F32, kind="ExternalOutput").ap()
    build(nc, aps, out)
    r = run_bass_kernel_spmd(nc, [{"in_" + k: v for k, v in arrays.items()}], core_ids=[0])
    return r.results[0]["out"]
```
